# Optimizing a Trainium2 kernel written in Bass

```python
import numpy as np
import jax
import jax.numpy as jnp

def _softmax(x, axis=-1):
    return jax.nn.softmax(x, axis=axis)

def _gelu(x):
    return jax.nn.gelu(x, approximate=True)

def _silu(x):
    return jax.nn.silu(x)

def _sigmoid(x):
    return jax.nn.sigmoid(x)

def _layernorm(x, axis=-1, eps=1e-05):
    m = jnp.mean(x, axis=axis, keepdims=True)
    v = jnp.var(x, axis=axis, keepdims=True)
    return (x - m) / jnp.sqrt(v + eps)

def _scatter_add(tgt, idx, src, axis=0):
    return tgt.at[idx].add(src)

def _segment_sum(src, seg, n):
    return jax.ops.segment_sum(src, seg, n)
kernel_name = 'mk_gnn_ffn_d2_gnn_r32_9c7658'

def setup_inputs(seed: int=0):
    np.random.seed(seed)
    _w = jnp.asarray

    def _rec_inputs():
        import jax
        import jax.numpy as jnp
        _gk = jax.random.key(seed)
        x = -0.0003713 + 1 * jax.random.normal(jax.random.fold_in(_gk, 1), (3125, 256), jnp.float32)
        src = jax.random.randint(jax.random.fold_in(_gk, 2), (50000,), 0, 3125, jnp.int32)
        dst = jnp.minimum((3125 * jax.random.uniform(jax.random.fold_in(_gk, 3), (50000,)) ** 2.0).astype(jnp.int32), 99999)
        _o = jnp.argsort(dst, stable=True)
        src = src[_o]
        dst = dst[_o]
        return (x, src, dst)
    x, src, dst = _rec_inputs()

    def _L0_gnn_setup():
        import jax, jax.numpy as jnp
        import numpy as np
        NEG_SLOPE = 0.2
        N_NODES = 50000
        N_EDGES = 25000
        IN_DIM = 256
        HID_DIM = 256
        HEADS = 8
        HEAD_DIM = HID_DIM // HEADS

        def gat_layer(x, src, dst, W, al, ar, b):
            N = x.shape[0]
            feat = (x @ W).reshape(N, HEADS, HEAD_DIM)
            el = jnp.sum(feat * al[None], axis=-1)
            er = jnp.sum(feat * ar[None], axis=-1)
            e = el[src] + er[dst]
            e = jnp.where(e > 0, e, NEG_SLOPE * e)
            m = jax.ops.segment_max(e, dst, num_segments=N)
            a = jnp.exp(e - m[dst])
            denom = jax.ops.segment_sum(a, dst, num_segments=N)
            alpha = a / denom[dst]
            msg = feat[src] * alpha[:, :, None]
            out = jax.ops.segment_sum(msg, dst, num_segments=N)
            out = out + b.reshape(1, HEADS, HEAD_DIM)
            out = jax.nn.relu(out)
            return out.reshape(N, HID_DIM)
        key = jax.random.key(seed)
        ks = jax.random.split(key, 12)

        def glorot(k, shape):
            fan = sum(shape[-2:]) if len(shape) > 1 else shape[-1] + 1
            return jax.random.normal(k, shape, jnp.float32) * jnp.sqrt(2.0 / fan)
        return {'data': jax.random.normal(ks[0], (N_NODES, IN_DIM), jnp.float32), 'src': jax.random.randint(ks[1], (N_EDGES,), 0, N_NODES), 'dst': jax.random.randint(ks[2], (N_EDGES,), 0, N_NODES), 'W1': glorot(ks[3], (IN_DIM, HID_DIM)), 'al1': glorot(ks[4], (HEADS, HEAD_DIM)), 'ar1': glorot(ks[5], (HEADS, HEAD_DIM)), 'b1': jnp.zeros((HID_DIM,), jnp.float32), 'W2': glorot(ks[6], (HID_DIM, HID_DIM)), 'al2': glorot(ks[7], (HEADS, HEAD_DIM)), 'ar2': glorot(ks[8], (HEADS, HEAD_DIM)), 'b2': jnp.zeros((HID_DIM,), jnp.float32)}
    _L0_gnn_all = _L0_gnn_setup()
    _L0_gnn_in = {k: v for k, v in _L0_gnn_all.items() if k in ('W1', 'al1', 'ar1', 'b1', 'W2', 'al2', 'ar2', 'b2')}
    del _L0_gnn_all

    def _L0_ffn_setup():
        import jax, jax.numpy as jnp
        import numpy as np
        B, S, D, F, E, K = (8, 64, 256, 1024, 8, 2)
        key = jax.random.key(seed)
        ks = jax.random.split(key, 10)
        s = 0.02
        return {'x': jax.random.normal(ks[0], (B, S, D), dtype=jnp.float32), 'Wr': jax.random.normal(ks[1], (D, E), dtype=jnp.float32) * s, 'W1s': jax.random.normal(ks[2], (D, F), dtype=jnp.float32) * s, 'b1s': jnp.zeros((F,), dtype=jnp.float32), 'W2s': jax.random.normal(ks[3], (F, D), dtype=jnp.float32) * s, 'b2s': jnp.zeros((D,), dtype=jnp.float32), 'W1p': jax.random.normal(ks[4], (E, D, F), dtype=jnp.float32) * s, 'b1p': jnp.zeros((E, F), dtype=jnp.float32), 'W2p': jax.random.normal(ks[5], (E, F, D), dtype=jnp.float32) * s, 'b2p': jnp.zeros((E, D), dtype=jnp.float32)}
    _L0_ffn_all = _L0_ffn_setup()
    _L0_ffn_in = {k: v for k, v in _L0_ffn_all.items() if k in ('Wr', 'W1s', 'b1s', 'W2s', 'b2s', 'W1p', 'b1p', 'W2p', 'b2p')}
    del _L0_ffn_all

    def _L1_gnn_setup():
        import jax, jax.numpy as jnp
        import numpy as np
        N, E, D_IN, D_OUT = (50000, 50000, 256, 256)
        key = jax.random.key(seed)
        k1, k2, k3, k4, k5, k6 = jax.random.split(key, 6)
        x = jax.random.normal(k1, (N, D_IN), dtype=jnp.float32)
        edge_index = jax.random.randint(k2, (2, E), 0, N, dtype=jnp.int64)
        s = 1.0 / np.sqrt(D_IN)
        W1 = jax.random.uniform(k3, (D_OUT, D_IN), minval=-s, maxval=s, dtype=jnp.float32)
        b1 = jax.random.uniform(k4, (D_OUT,), minval=-s, maxval=s, dtype=jnp.float32)
        W2 = jax.random.uniform(k5, (D_OUT, D_IN), minval=-s, maxval=s, dtype=jnp.float32)
        b2 = jax.random.uniform(k6, (D_OUT,), minval=-s, maxval=s, dtype=jnp.float32)
        return {'x': x, 'W1': W1, 'b1': b1, 'W2': W2, 'b2': b2, 'edge_index': edge_index}
    _L1_gnn_all = _L1_gnn_setup()
    _L1_gnn_in = {k: v for k, v in _L1_gnn_all.items() if k in ('W1', 'b1', 'W2', 'b2')}
    del _L1_gnn_all

    def _L1_ffn_setup():
        import jax, jax.numpy as jnp
        import numpy as np
        B, S, H, F, E, K = (8, 128, 256, 512, 16, 2)
        EPS = 1e-05
        key = jax.random.key(seed)
        ks = jax.random.split(key, 9)
        sc = 0.02
        return {'x': jax.random.normal(ks[0], (B, S, H), dtype=jnp.float32), 'gate_w': jax.random.normal(ks[1], (H, E), dtype=jnp.float32) * sc, 'gate_b': jnp.zeros((E,), dtype=jnp.float32), 'w1': jax.random.normal(ks[2], (E, H, F), dtype=jnp.float32) * sc, 'b1': jnp.zeros((E, F), dtype=jnp.float32), 'w2': jax.random.normal(ks[3], (E, F, H), dtype=jnp.float32) * sc, 'b2': jnp.zeros((E, H), dtype=jnp.float32), 'gamma': jnp.ones((H,), dtype=jnp.float32), 'beta': jnp.zeros((H,), dtype=jnp.float32)}
    _L1_ffn_all = _L1_ffn_setup()
    _L1_ffn_in = {k: v for k, v in _L1_ffn_all.items() if k in ('gate_w', 'gate_b', 'w1', 'b1', 'w2', 'b2', 'gamma', 'beta')}
    del _L1_ffn_all
    return {'x': x, 'src': src, 'dst': dst, 'L0_gnn_W1': _L0_gnn_in['W1'], 'L0_gnn_al1': _L0_gnn_in['al1'], 'L0_gnn_ar1': _L0_gnn_in['ar1'], 'L0_gnn_b1': _L0_gnn_in['b1'], 'L0_gnn_W2': _L0_gnn_in['W2'], 'L0_gnn_al2': _L0_gnn_in['al2'], 'L0_gnn_ar2': _L0_gnn_in['ar2'], 'L0_gnn_b2': _L0_gnn_in['b2'], 'L0_ffn_Wr': _L0_ffn_in['Wr'], 'L0_ffn_W1s': _L0_ffn_in['W1s'], 'L0_ffn_b1s': _L0_ffn_in['b1s'], 'L0_ffn_W2s': _L0_ffn_in['W2s'], 'L0_ffn_b2s': _L0_ffn_in['b2s'], 'L0_ffn_W1p': _L0_ffn_in['W1p'], 'L0_ffn_b1p': _L0_ffn_in['b1p'], 'L0_ffn_W2p': _L0_ffn_in['W2p'], 'L0_ffn_b2p': _L0_ffn_in['b2p'], 'L1_gnn_W1': _L1_gnn_in['W1'], 'L1_gnn_b1': _L1_gnn_in['b1'], 'L1_gnn_W2': _L1_gnn_in['W2'], 'L1_gnn_b2': _L1_gnn_in['b2'], 'L1_ffn_gate_w': _L1_ffn_in['gate_w'], 'L1_ffn_gate_b': _L1_ffn_in['gate_b'], 'L1_ffn_w1': _L1_ffn_in['w1'], 'L1_ffn_b1': _L1_ffn_in['b1'], 'L1_ffn_w2': _L1_ffn_in['w2'], 'L1_ffn_b2': _L1_ffn_in['b2'], 'L1_ffn_gamma': _L1_ffn_in['gamma'], 'L1_ffn_beta': _L1_ffn_in['beta']}

def reference(x, src, dst, L0_gnn_W1, L0_gnn_al1, L0_gnn_ar1, L0_gnn_b1, L0_gnn_W2, L0_gnn_al2, L0_gnn_ar2, L0_gnn_b2, L0_ffn_Wr, L0_ffn_W1s, L0_ffn_b1s, L0_ffn_W2s, L0_ffn_b2s, L0_ffn_W1p, L0_ffn_b1p, L0_ffn_W2p, L0_ffn_b2p, L1_gnn_W1, L1_gnn_b1, L1_gnn_W2, L1_gnn_b2, L1_ffn_gate_w, L1_ffn_gate_b, L1_ffn_w1, L1_ffn_b1, L1_ffn_w2, L1_ffn_b2, L1_ffn_gamma, L1_ffn_beta):
    import jax
    import jax.numpy as jnp

    def _L0_gnn_ref(data, src, dst, W1, al1, ar1, b1, W2, al2, ar2, b2):
        import jax, jax.numpy as jnp
        import numpy as np
        NEG_SLOPE = 0.2
        N_NODES = 50000
        N_EDGES = 25000
        IN_DIM = 256
        HID_DIM = 256
        HEADS = 8
        HEAD_DIM = HID_DIM // HEADS

        def gat_layer(x, src, dst, W, al, ar, b):
            N = x.shape[0]
            feat = (x @ W).reshape(N, HEADS, HEAD_DIM)
            el = jnp.sum(feat * al[None], axis=-1)
            er = jnp.sum(feat * ar[None], axis=-1)
            e = el[src] + er[dst]
            e = jnp.where(e > 0, e, NEG_SLOPE * e)
            m = jax.ops.segment_max(e, dst, num_segments=N)
            a = jnp.exp(e - m[dst])
            denom = jax.ops.segment_sum(a, dst, num_segments=N)
            alpha = a / denom[dst]
            msg = feat[src] * alpha[:, :, None]
            out = jax.ops.segment_sum(msg, dst, num_segments=N)
            out = out + b.reshape(1, HEADS, HEAD_DIM)
            out = jax.nn.relu(out)
            return out.reshape(N, HID_DIM)
        h = gat_layer(data, src, dst, W1, al1, ar1, b1)
        h = gat_layer(h, src, dst, W2, al2, ar2, b2)
        return h

    def _L0_ffn_ref(x, Wr, W1s, b1s, W2s, b2s, W1p, b1p, W2p, b2p):
        import jax, jax.numpy as jnp
        import numpy as np
        B, S, D, F, E, K = (8, 64, 256, 1024, 8, 2)
        gelu = lambda t: jax.nn.gelu(t, approximate=False)
        shared = gelu(x @ W1s + b1s) @ W2s + b2s
        rw = jax.nn.softmax(x @ Wr, axis=-1)
        topw, topi = jax.lax.top_k(rw, K)
        topw = topw / jnp.sum(topw, axis=-1, keepdims=True)
        mask = jnp.sum(jax.nn.one_hot(topi, E, dtype=topw.dtype) * topw[..., None], axis=-2)
        h = gelu(jnp.einsum('bsd,edf->bsef', x, W1p) + b1p)
        priv = jnp.einsum('bsef,efd->bsed', h, W2p) + b2p
        routed = jnp.einsum('bsed,bse->bsd', priv, mask)
        return shared + routed

    def _L1_gnn_ref(x, W1, b1, W2, b2, edge_index):
        import jax, jax.numpy as jnp
        import numpy as np
        N, E, D_IN, D_OUT = (50000, 50000, 256, 256)
        dst = edge_index[0]
        nbr = edge_index[1]
        n = x.shape[0]
        agg = jax.ops.segment_sum(x[nbr], dst, num_segments=n)
        cnt = jax.ops.segment_sum(jnp.ones((nbr.shape[0],), x.dtype), dst, num_segments=n)
        mean = agg / jnp.maximum(cnt, 1.0)[:, None]
        return x @ W1.T + b1 + mean @ W2.T + b2

    def _L1_ffn_ref(x, gate_w, gate_b, w1, b1, w2, b2, gamma, beta):
        import jax, jax.numpy as jnp
        import numpy as np
        B, S, H, F, E, K = (8, 128, 256, 512, 16, 2)
        EPS = 1e-05
        gate_logits = x @ gate_w + gate_b
        topk_vals, topk_idx = jax.lax.top_k(gate_logits, K)
        topk_w = jax.nn.softmax(topk_vals, axis=-1)
        h = jax.nn.relu(jnp.einsum('bsh,ehf->bsef', x, w1) + b1)
        expert_out = jnp.einsum('bsef,efh->bseh', h, w2) + b2
        sel = jnp.take_along_axis(expert_out, topk_idx[:, :, :, None], axis=2)
        moe = jnp.sum(topk_w[..., None] * sel, axis=2)
        y = x + moe
        mu = jnp.mean(y, axis=-1, keepdims=True)
        var = jnp.var(y, axis=-1, keepdims=True)
        return (y - mu) / jnp.sqrt(var + EPS) * gamma + beta
    edge_index = jnp.stack([src, dst])
    x = x + _L0_gnn_ref(_layernorm(x, axis=-1), src, dst, L0_gnn_W1, L0_gnn_al1, L0_gnn_ar1, L0_gnn_b1, L0_gnn_W2, L0_gnn_al2, L0_gnn_ar2, L0_gnn_b2)
    x = x + _L0_ffn_ref(_layernorm(x, axis=-1)[None], L0_ffn_Wr, L0_ffn_W1s, L0_ffn_b1s, L0_ffn_W2s, L0_ffn_b2s, L0_ffn_W1p, L0_ffn_b1p, L0_ffn_W2p, L0_ffn_b2p)[0]
    x = x + _L1_gnn_ref(_layernorm(x, axis=-1), L1_gnn_W1, L1_gnn_b1, L1_gnn_W2, L1_gnn_b2, edge_index)
    x = x + _L1_ffn_ref(_layernorm(x, axis=-1)[None], L1_ffn_gate_w, L1_ffn_gate_b, L1_ffn_w1, L1_ffn_b1, L1_ffn_w2, L1_ffn_b2, L1_ffn_gamma, L1_ffn_beta)[0]
    return x

_drawn_inputs = setup_inputs


def setup_inputs(seed=0):
    import zlib

    import numpy as np

    out = dict(_drawn_inputs(seed))
    spreads = {'L0_gnn_b1': (0.0, 0.1),
     'L0_gnn_b2': (0.0, 0.1),
     'L0_ffn_b1s': (0.0, 0.1),
     'L0_ffn_b2s': (0.0, 0.1),
     'L0_ffn_b1p': (0.0, 0.301),
     'L0_ffn_b2p': (0.0, 0.1),
     'L1_ffn_gate_b': (0.0, 0.286),
     'L1_ffn_b1': (0.0, 0.772),
     'L1_ffn_b2': (0.0, 0.1),
     'L1_ffn_gamma': (1.0, 0.2),
     'L1_ffn_beta': (0.0, 0.1)}
    factors = {'L0_gnn_ar1': 3.12, 'L0_gnn_al2': 3.083, 'L0_gnn_ar2': 6.732}
    for name, (base, spread) in spreads.items():
        noise = np.random.default_rng([zlib.crc32(name.encode()), seed]).standard_normal(out[name].shape)
        drawn = base * np.exp(spread * noise) if base else spread * noise
        out[name] = jnp.asarray(drawn.astype(out[name].dtype))
    for name, factor in factors.items():
        out[name] = (out[name] * factor).astype(out[name].dtype)
    return out
```

```python
import concourse.bass as bass
from concourse import mybir

F32, BF16 = mybir.dt.float32, mybir.dt.bfloat16
I32, U32 = mybir.dt.int32, mybir.dt.uint32
ALU, ACT, AX = mybir.AluOpType, mybir.ActivationFunctionType, mybir.AxisListType

P = 128
BIG = 1.0e30
EPS = 1.0e-5
NEG_SLOPE = 0.2


def ceil_div(a, b):
    return -(-a // b)


class Engine:

    def __init__(self, nc, raw, name):
        self.raw, self.sem, self.count, self.waited = raw, nc.alloc_semaphore(name), 0, {}

    def done(self, instruction):
        self.count += 1
        instruction.then_inc(self.sem, 1)
        return (self.sem, self.count)

    def need(self, *marks):
        for mark in marks:
            if mark is None:
                continue
            if isinstance(mark, list):
                self.need(*mark)
                continue
            sem, value = mark
            if self.waited.get(sem.name, 0) < value:
                self.raw.wait_ge(sem, value)
                self.waited[sem.name] = value
        return self.raw


class Landing:

    def __init__(self, nc, name, n=1):
        self.sems, self.counts = [nc.alloc_semaphore(f"{name}{i}") for i in range(n)], [0] * n

    def sent(self, instruction, slot=0):
        self.counts[slot] += 16
        instruction.then_inc(self.sems[slot], 16)
        return (self.sems[slot], self.counts[slot])

    def all(self):
        return [(s, c) for s, c in zip(self.sems, self.counts) if c]


class Arena:

    def __init__(self, nc, nbytes):
        self.words = nbytes // 4
        self.whole = nc.alloc_sbuf_tensor("arena", [P, self.words], F32)
        self.used = 0

    def take(self, *dims, dtype=F32):
        n = 1
        for d in dims:
            n *= d
        size = 2 if dtype == BF16 else 4
        words = ceil_div(n * size, 4)
        words += words % 2
        assert self.used + words <= self.words, (self.used, words, self.words)
        view = self.whole[:, self.used:self.used + words]
        self.used += words
        if dtype != F32:
            view = view.bitcast(dtype)
        view = view[:, 0:n]
        if len(dims) == 2:
            return view.rearrange("p (a b) -> p a b", a=dims[0])
        if len(dims) == 3:
            return view.rearrange("p (a b c) -> p a b c", a=dims[0], b=dims[1])
        return view


def spread(ap, axis, n):
    v = ap.unsqueeze(axis)
    shape = list(v.shape)
    shape[axis] = n
    return v.to_broadcast(shape)


def build(nc, t, out):
    N, D = t["x"].shape
    E = t["src"].shape[0]
    H, HD = t["L0_gnn_al1"].shape
    NT, ET = ceil_div(N, P), ceil_div(E, P)
    NI = ET + NT - 1
    NIC = ceil_div(NI, P)
    LAST = N - (NT - 1) * P
    K = D // P
    ROW = D + H
    G = 4
    NG = ceil_div(NI, G)

    V = Engine(nc, nc.vector, "vector_done")
    S = Engine(nc, nc.scalar, "scalar_done")
    T = Engine(nc, nc.tensor, "tensor_done")
    L = Engine(nc, nc.gpsimd, "gpsimd_done")
    Q = Engine(nc, nc.sync, "sync_done")

    def dram(name, shape, dtype=F32):
        return nc.dram_tensor(name, shape, dtype, kind="Internal").ap()

    def sbuf(name, shape, dtype=F32):
        return nc.alloc_sbuf_tensor(name, shape, dtype)[tuple(slice(None) for _ in shape)]

    bank = [nc.alloc_psum_tensor(f"bank{i}", [P, 512], F32)[:, :] for i in range(8)]
    bank_free = [None] * 8

    x = sbuf("x_nodes", [P, NT, D])
    ident = sbuf("ident", [P, P])
    iota = sbuf("iota_free", [P, P])
    ones = sbuf("ones", [P, P])
    ones16 = sbuf("ones16", [P, P], BF16)
    tri16 = sbuf("tri16", [P, P], BF16)
    iota_item = sbuf("iota_item", [P, 4])
    valid_row = sbuf("valid_row", [P, 1])
    stats = sbuf("ln_stats", [P, NT, 6])
    mean_var = sbuf("ln_mean_var", [P, NT, 2])
    rstd = sbuf("ln_rstd", [P, NT])
    item_tile_row = sbuf("item_tile_row", [1, NI], I32)
    any_f_T = sbuf("any_fence_fwd", [H, P])
    any_b_T = sbuf("any_fence_bwd", [H, P])
    N_COL = E // P + 1
    edge_to_tile = sbuf("edge_to_tile", [P, N_COL])
    edge_to_row = sbuf("edge_to_row", [P, N_COL])
    edge_value = sbuf("edge_value", [P, N_COL])
    sorted_value = sbuf("sorted_value", [P, NI])
    arena = Arena(nc, 165 * 1024)
    item_local = arena.take(NIC * P)
    lane_src = arena.take(NI, dtype=U32)
    fence = arena.take(NI + 1)
    gat_base = arena.used

    constants = Landing(nc, "constants_landed")
    index_dma = Landing(nc, "index_landed")
    x_dma = Landing(nc, "x_landed")

    m_ident0 = L.done(L.raw.memset(ident, 0.0))
    m_ones = L.done(L.raw.memset(ones, 1.0))
    m_ident = L.done(L.need(m_ident0).affine_select(
        out=ident, in_=ident, compare_op=ALU.not_equal, fill=1.0, base=0, pattern=[[-1, P]],
        channel_multiplier=1))
    m_iota = L.done(L.raw.iota(iota, [[1, P]], base=0, channel_multiplier=0,
                               allow_small_or_imprecise_dtypes=True))
    m_iota = L.done(L.raw.iota(iota_item, [[P, 4]], base=0, channel_multiplier=1,
                               allow_small_or_imprecise_dtypes=True))
    m_ones16 = V.done(V.need(m_ones).tensor_copy(ones16, ones))
    m_tri = V.done(V.need(m_iota).tensor_scalar(tri16, iota, iota_item[:, 0:1], None, ALU.is_gt))
    m_valid = V.done(V.raw.tensor_scalar(valid_row, iota_item[:, 0:1], float(LAST), None, ALU.is_lt))
    m_const = [m_ident, m_iota, m_ones16, m_tri, m_valid]

    m_x0 = V.done(V.raw.memset(x[:, NT - 1, :], 0.0))
    half = (NT - 1) // 2
    for a, b in ((0, half), (half, NT - 1)):
        m_x = x_dma.sent(Q.raw.dma_start(
            x[:, a:b, :], t["x"][a * P:b * P, :].rearrange("(t p) d -> p t d", p=P)))
    m_x = x_dma.sent(Q.need(m_x0).dma_start(x[0:LAST, NT - 1, :], t["x"][(NT - 1) * P:N, :]))

    pad_node, pad_far, pad_key = (arena.take(P, dtype=d)[0:1, :] for d in (I32, I32, F32))
    src_rows = dram("src_rows", (ET * P,), I32)
    dst_rows = dram("dst_rows", (ET * P,), I32)
    src_stream = dram("src_stream", (NI * P,), U32)
    key_stream = dram("key_stream", (NI * P + 2,))
    item_tile = dram("item_tile", (NIC * P,), I32)

    m_pad = [V.done(V.raw.memset(pad_node, 0)), V.done(V.raw.memset(pad_far, 1 << 20)),
             V.done(V.raw.memset(pad_key, -5.0))]
    A = S
    n_pad = ET * P - E
    for rows, whole, pad in ((src_rows, t["src"], pad_node), (dst_rows, t["dst"], pad_far)):
        index_dma.sent(A.raw.dma_start(rows[0:E].rearrange("(a b) -> a b", a=16),
                                       whole.rearrange("(a b) -> a b", a=16)))
        m_rows = index_dma.sent(A.need(m_pad).dma_start(rows[E:ET * P].unsqueeze(0),
                                                        pad[:, 0:n_pad]))
    first_i = arena.take(ET, dtype=I32)[0:1, :]
    first_f = arena.take(ET)[0:1, :]
    tile_no = arena.take(ET)[0:1, :]
    with nc.allow_non_contiguous_dma(reason="the first dst of each edge tile"):
        m_rows = index_dma.sent(A.raw.dma_start(first_i, t["dst"][0:(ET - 1) * P + 1:P].unsqueeze(0)))
    m_tile_no = L.done(L.raw.iota(tile_no, [[1, ET]], base=0, channel_multiplier=0,
                                  allow_small_or_imprecise_dtypes=True))
    m = V.done(V.need(m_rows).tensor_scalar(first_i, first_i, 7, None, ALU.arith_shift_right))
    m = V.done(V.need(m).tensor_copy(first_f, first_i))
    m = V.done(V.need(m, m_tile_no).tensor_tensor(first_f, first_f, tile_no, ALU.add))
    m_bc = T.done(T.need(m, m_ones).matmul(bank[0][:, 0:ET], ones[0:1, :], first_f, start=True, stop=True))
    before = arena.take(NIC, ET)
    edge_tile = arena.take(NIC)
    node_tile = arena.take(NIC)
    minus_base = arena.take(NIC)
    edge_tile_u = arena.take(NIC, dtype=U32)
    node_tile_i = arena.take(NIC, dtype=I32)
    for c in range(NIC):
        m = V.done(V.need(m_bc, m_iota).tensor_scalar(before[:, c, :], bank[0][:, 0:ET],
                                                      iota_item[:, c:c + 1], None, ALU.is_le))
    bank_free[0] = m
    m = V.done(V.need(m).tensor_reduce(edge_tile, before, AX.X, ALU.add))
    m = V.done(V.need(m).tensor_scalar(edge_tile, edge_tile, -1.0, None, ALU.add))
    m_eu = V.done(V.need(m).tensor_copy(edge_tile_u, edge_tile))
    m = V.done(V.raw.tensor_tensor(node_tile, iota_item[:, 0:NIC], edge_tile, ALU.subtract))
    m_nb = V.done(V.need(m).tensor_scalar(minus_base, node_tile, -float(P), None, ALU.mult))
    m_ni = V.done(V.raw.tensor_copy(node_tile_i, node_tile))
    with nc.allow_non_contiguous_dma(reason="one word per item"):
        m_it = index_dma.sent(Q.need(m_ni).dma_start(item_tile.rearrange("(c p) -> p c", p=P), node_tile_i))
        m_item_row = index_dma.sent(Q.need(m_it, m_rows).dma_start(item_tile_row, item_tile[0:NI].unsqueeze(0)))

    src_i = arena.take(NIC, P, dtype=U32)
    dst_i = arena.take(NIC, P, dtype=I32)
    gather_dma = Landing(nc, "item_rows_landed")
    for c in range(NIC):
        for rows, into in ((src_rows, src_i), (dst_rows, dst_i)):
            m_rows_in = gather_dma.sent(L.need(m_eu, m_rows, m_item_row).indirect_dma_start(
                out=into[:, c, :].bitcast(I32), out_offset=None, in_=rows.rearrange("(a b) -> a b", b=P),
                in_offset=bass.IndirectOffsetOnAxis(ap=edge_tile_u[:, c:c + 1], axis=0)))
    dst_f = arena.take(NIC, P)
    local = arena.take(NIC, P)
    inside = arena.take(NIC, P)
    m_df = V.done(V.need(m_rows_in).tensor_copy(dst_f, dst_i))
    for c in range(NIC):
        m = V.done(V.need(m_df, m_nb).tensor_scalar(local[:, c, :], dst_f[:, c, :],
                                                    minus_base[:, c:c + 1], None, ALU.add))
    m_local = m
    m = V.done(V.need(m).tensor_scalar(inside, local, 0.0, None, ALU.is_ge))
    m = V.done(V.need(m).scalar_tensor_tensor(inside, local, float(P), inside, ALU.is_lt, ALU.mult))
    m = V.done(V.need(m).scalar_tensor_tensor(dst_f, dst_f, 1.0, inside, ALU.add, ALU.mult))
    m_key = V.done(V.need(m).tensor_scalar(dst_f, dst_f, -1.0, None, ALU.add))
    stream_dma = Landing(nc, "stream_written")
    for c in range(NIC):
        n = min(P, NI - c * P)
        m_st = stream_dma.sent(Q.need(m_rows_in).dma_start(
            src_stream[c * P * P:(c * P + n) * P].rearrange("(a b) -> a b", b=P), src_i[0:n, c, :]))
        m_st = stream_dma.sent(Q.need(m_key).dma_start(
            key_stream[1 + c * P * P:1 + (c * P + n) * P].rearrange("(a b) -> a b", b=P), dst_f[0:n, c, :]))
    m_st = stream_dma.sent(Q.need(m_pad).dma_start(key_stream[0:1].unsqueeze(0), pad_key[:, 0:1]))
    m_st = stream_dma.sent(Q.raw.dma_start(key_stream[NI * P + 1:NI * P + 2].unsqueeze(0), pad_key[:, 1:2]))
    keys = arena.take(NI + 2)
    lane_dma = Landing(nc, "lanes_landed")
    lane_dma.sent(Q.need(m_st).dma_start(lane_src, src_stream.rearrange("(p c) -> p c", p=P)))
    with nc.allow_non_contiguous_dma(reason="the neighbours of each lane's ends"):
        for at in (0, 1, 2):
            view = key_stream[at:at + NI * P].rearrange("(p c) -> p c", p=P)
            lo, hi = ((0, 1), (0, NI), (NI - 1, NI))[at]
            m_lane = lane_dma.sent(Q.raw.dma_start(keys[:, at + lo:at + hi], view[:, lo:hi]))
    m = V.done(V.need(m_lane).tensor_tensor(fence, keys[:, 1:NI + 2], keys[:, 0:NI + 1], ALU.not_equal))
    m_fence = V.done(V.need(m).tensor_scalar(fence, fence, -BIG, None, ALU.mult))
    any_f, any_b = arena.take(1), arena.take(1)
    V.done(V.need(m_fence).tensor_reduce(any_f, fence[:, 0:NI], AX.X, ALU.min))
    m = V.done(V.raw.tensor_reduce(any_b, fence[:, 1:NI + 1], AX.X, ALU.min))
    rep = arena.take(2, H)
    V.done(V.need(m).tensor_copy(rep[:, 0, :], any_f.to_broadcast([P, H])))
    m = V.done(V.raw.tensor_copy(rep[:, 1, :], any_b.to_broadcast([P, H])))
    T.need(m, m_ident).transpose(bank[1][0:H, 0:P], rep[:, 0, :], ident)
    m = T.done(T.raw.transpose(bank[1][0:H, P:2 * P], rep[:, 1, :], ident))
    V.done(V.need(m).tensor_copy(any_f_T, bank[1][0:H, 0:P]))
    m_any = V.done(V.raw.tensor_copy(any_b_T, bank[1][0:H, P:2 * P]))
    bank_free[1] = m_any
    for c in range(NIC):
        mt = T.done(T.need(m_local, m_ident).transpose(bank[2][:, c * P:(c + 1) * P], local[:, c, :], ident))
    m_item_local = V.done(V.need(mt).tensor_copy(item_local, bank[2][:, 0:NIC * P]))
    bank_free[2] = m_item_local
    m_items = [m_item_local, m_fence, m_any, m_lane, m_item_row]

    E0, F0 = t["L0_ffn_b1p"].shape
    E1, F1 = t["L1_ffn_b1"].shape
    max_tiles = [(2 * N + e * (P - 1)) // P for e in (E0, E1)]

    def ln_stats(m_in):
        for j in range(NT):
            m = V.done(V.need(m_in if not isinstance(m_in, dict) else m_in[j]).bn_stats(stats[:, j, :], x[:, j, :]))
        V.need(m)
        for j in range(NT):
            m = V.done(V.raw.bn_aggr(mean_var[:, j, :], stats[:, j, :]))
        m = V.done(V.need(m).tensor_scalar(rstd, mean_var[:, :, 1], EPS, None, ALU.add))
        m = S.done(S.need(m).activation(rstd, rstd, ACT.Sqrt))
        return V.done(V.need(m).reciprocal(rstd, rstd))

    def ln_rows(into, j, m_stats, m_free=None):
        return V.done(V.need(m_stats, m_free).tensor_scalar(
            into, x[:, j, :], mean_var[:, j, 0:1], rstd[:, j:j + 1], ALU.subtract, ALU.mult))

    class Buckets:

        def __init__(self, member, groups, n, prefix, work, small, banks):
            self.member, self.groups, self.n, self.prefix, self.banks = member, groups, n, prefix, banks
            self.chunk = 512 // n
            self.chunks = [(a, min(groups, a + self.chunk)) for a in range(0, groups, self.chunk)]
            self.work, self.small, self.free = work, small, {}

        def totals(self, q, m_member):
            a, b = self.chunks[q]
            bk = self.banks[q % 2]
            m = T.done(T.need(m_member, bank_free[bk]).matmul(
                bank[bk][:, 0:(b - a) * self.n], ones16,
                self.member[:, a:b, :].rearrange("p g b -> p (g b)"), start=True, stop=True))
            by_bucket = self.prefix[:, 1:1 + self.groups * self.n].rearrange("p (b g) -> p b g", b=self.n)
            self.m = V.done(V.need(m).tensor_copy(
                by_bucket[:, :, a:b], bank[bk][:, 0:(b - a) * self.n].rearrange("p (g b) -> p b g", b=self.n)))
            bank_free[bk] = self.m

        def scan(self):
            g, n, s, pre = self.groups, self.n, self.small, self.prefix
            m0 = V.done(V.raw.memset(pre[:, 0:1], 0.0))
            run = pre[:, 1:1 + g * n]
            m = V.done(V.need(self.m, m0).tensor_tensor_scan(run, run, run, 0.0, ALU.add, ALU.max))
            first = pre[:, 0:g * n].rearrange("p (b g) -> p b g", b=n)[:, :, 0]
            last = run.rearrange("p (b g) -> p b g", b=n)[:, :, g - 1]
            padded, self.end, shift, whole = s[:, 0, :], s[:, 1, :], s[:, 2, :], s[:, 3, :].bitcast(I32)
            m = V.done(V.need(m).tensor_tensor(padded, last, first, ALU.subtract))
            m = V.done(V.need(m).tensor_scalar(padded, padded, float(P - 1), None, ALU.add))
            m = V.done(V.need(m).tensor_copy(whole, padded))
            m = V.done(V.need(m).tensor_scalar(whole, whole, 7, 7, ALU.arith_shift_right, ALU.logical_shift_left))
            m = V.done(V.need(m).tensor_copy(padded, whole))
            m = V.done(V.need(m).tensor_tensor_scan(self.end, padded, padded, 0.0, ALU.add, ALU.max))
            m = V.done(V.need(m).tensor_tensor(shift, self.end, padded, ALU.subtract))
            m = V.done(V.need(m).tensor_tensor(shift, shift, first, ALU.subtract))
            base = pre[:, 0:g * n].rearrange("p (b g) -> p b g", b=n)
            self.m = V.done(V.need(m).tensor_tensor(base, base, spread(shift, 2, g), ALU.add))

        def positions(self, q, to):
            a, b = self.chunks[q]
            bk = self.banks[q % 2]
            m = T.done(T.need(bank_free[bk]).matmul(
                bank[bk][:, 0:(b - a) * self.n], tri16,
                self.member[:, a:b, :].rearrange("p g b -> p (g b)"), start=True, stop=True))
            base = self.prefix[:, 0:self.groups * self.n].rearrange("p (b g) -> p g b", b=self.n)[:, a:b, :]
            w = self.work[:, q % 2, 0:(b - a) * self.n].rearrange("p (g b) -> p g b", b=self.n)
            m = V.done(V.need(m, self.m, self.free.get(q % 2)).tensor_tensor(
                w, bank[bk][:, 0:(b - a) * self.n].rearrange("p (g b) -> p g b", b=self.n), base, ALU.add))
            bank_free[bk] = m
            m = V.done(V.need(m).tensor_tensor(w, w, self.member[:, a:b, :], ALU.mult))
            self.m_pos = self.free[q % 2] = V.done(V.need(m).tensor_reduce(to[:, a:b], w, AX.X, ALU.add))

        def tile_row(self, n_tiles, compare, tiles_f, tiles_i, dram_row, row, landing):
            cols = ceil_div(n_tiles, P)
            m = V.done(V.need(m_iota).tensor_scalar(tiles_f, iota_item[:, 0:cols], float(P), None, ALU.mult))
            m = V.done(V.need(m, self.m).tensor_tensor(
                compare, spread(self.end, 1, cols), spread(tiles_f, 2, self.n), ALU.is_le))
            m = V.done(V.need(m).tensor_reduce(tiles_f, compare, AX.X, ALU.add))
            m = V.done(V.need(m).tensor_scalar(tiles_f, tiles_f, float(self.n - 1), None, ALU.min))
            m = V.done(V.need(m).tensor_copy(tiles_i, tiles_f))
            with nc.allow_non_contiguous_dma(reason="one word per tile"):
                m = landing.sent(Q.need(m).dma_start(dram_row.rearrange("(c p) -> p c", p=P), tiles_i))
            return landing.sent(Q.need(m).dma_start(row, dram_row[0:n_tiles].unsqueeze(0)))


    arena.used = gat_base
    spill = dram("spilled_features", (NI * P, D))
    er_slots = dram("er_slots", (NI * P, H))
    w_slots = dram("w_slots", (NI * P, H))
    tables = [dram(f"table{n}", (N, ROW)) for n in range(2)]
    hidden = arena.take(NT, D)
    acc = arena.take(NT, ROW)
    fwd = arena.take(H, NI)
    top = arena.take(H, NI)
    after_idle = arena.used
    el = arena.take(H, NI)
    er_lane = arena.take(NI, H)
    per_item = arena.take(NI, H)
    ring = arena.take(4 * G, ROW)
    ring_b = ring.rearrange("p a b -> p (a b)")[:, 0:4 * G * D].rearrange("p (a b) -> p a b", b=D)
    messages_at = arena.used
    messages = arena.take(2 * G, ROW)
    after_messages, arena.used = arena.used, messages_at
    a_rows = arena.take(2, D)
    a_prod = arena.take(K, D)
    rows_in = arena.take(2, D)
    rows_T = arena.take(2, K * P)
    assert arena.used <= after_messages
    arena.used = after_messages
    one_hot = arena.take(2 * G, P)
    one_hot_T = arena.take(2 * G, P)
    w_ext = arena.take(K, D + 2 * H)
    bias = arena.take(D)
    er_nodes = arena.take(NT, H)
    feats = arena.take(3, ROW)
    r_den = arena.take(NT, H)
    carry = arena.take(H)
    carry_T = arena.take(P + 1)
    carry_back = arena.take(H)

    table_dma = Landing(nc, "table_rows_written", 3)
    weight_dma = Landing(nc, "gat_weights_landed")
    gathered = Landing(nc, "rows_gathered", 4)
    spilled = Landing(nc, "rows_spilled", 4)
    slot_dma = Landing(nc, "slots_moved")
    back_dma = Landing(nc, "features_back", 4)
    er_dma = Landing(nc, "er_slots_written")

    tile_regs_v = [nc.vector.alloc_register(f"node_tile_v{i}") for i in range(G)]
    tile_regs_t = [nc.tensor.alloc_register(f"node_tile_t{i}") for i in range(G)]
    free = {}

    def gat(layer, W, al, ar, b, rows_of, before_slots, background):
        Q.need(before_slots)
        weight_dma.sent(Q.raw.dma_start(w_ext[:, :, 0:D], W.rearrange("(k p) n -> p k n", p=P)))
        for n, a in ((0, al), (1, ar)):
            weight_dma.sent(Q.raw.dma_start(a_rows[:, n, :], a.rearrange("h d -> (h d)").partition_broadcast(P)))
        m_w = weight_dma.sent(Q.raw.dma_start(bias, b.partition_broadcast(P)))
        for n in range(2):
            m = V.done(V.need(m_w, before_slots).tensor_tensor(a_prod, w_ext[:, :, 0:D],
                                                               spread(a_rows[:, n, :], 1, K), ALU.mult))
            m_wext = V.done(V.need(m).tensor_reduce(
                w_ext[:, :, D + n * H:D + (n + 1) * H],
                a_prod.rearrange("p k (h d) -> p k h d", h=H), AX.X, ALU.add))
            V.need(m_wext)
        m_table = []
        for j in range(NT):
            rows, m_rows = rows_of(j)
            tb, fb = bank[j % 2], bank[2 + j % 2]
            for k in range(K):
                m = T.done(T.need(m_rows, bank_free[j % 2]).transpose(tb[:, k * P:(k + 1) * P],
                                                                      rows[:, k * P:(k + 1) * P], ident))
            m_tr = m
            m = S.done(S.need(m_tr, free.get(("rows_T", j % 2))).activation(rows_T[:, j % 2, :], tb[:, 0:K * P], ACT.Copy))
            bank_free[j % 2] = m
            for k in range(K):
                m2 = T.done(T.need(m, m_wext, bank_free[2 + j % 2]).matmul(
                    fb[:, 0:D + 2 * H], rows_T[:, j % 2, k * P:(k + 1) * P], w_ext[:, k, :],
                    start=(k == 0), stop=(k == K - 1)))
            free[("rows_T", j % 2)] = m2
            V.need(m2, free.get(("feats", j % 3)))
            m3 = V.done(V.raw.tensor_copy(feats[:, j % 3, :], fb[:, 0:ROW]))
            m4 = V.done(V.raw.tensor_copy(er_nodes[:, j, :], fb[:, ROW:ROW + H]))
            bank_free[2 + j % 2] = m4
            n = P if j < NT - 1 else LAST
            free[("feats", j % 3)] = table_dma.sent(Q.need(m3).dma_start(
                tables[layer][j * P:j * P + n, :], feats[0:n, j % 3, :]), j % 3)
            free[("rows", j % 2)] = m_tr
        m_er_nodes = m4
        m_table = table_dma.all()

        L.need(m_table)
        for g in range(NG):
            n = min(G, NI - g * G)
            s0 = (g % 4) * G
            for k in range(n):
                c = g * G + k
                m_g = gathered.sent(L.need(m_items, free.get(("ring", g % 4))).indirect_dma_start(
                    out=ring[:, s0 + k, :], out_offset=None, in_=tables[layer],
                    in_offset=bass.IndirectOffsetOnAxis(ap=lane_src[:, c:c + 1], axis=0)), g % 4)
            m_el = S.done(S.need(m_g).activation(el[:, :, g * G:g * G + n],
                                                 ring[:, s0:s0 + n, D:ROW].rearrange("p c h -> p h c"), ACT.Copy))
            m_sp = spilled.sent(Q.need(m_g).dma_start(
                spill.rearrange("(p c) d -> p c d", p=P)[:, g * G:g * G + n, :], ring[:, s0:s0 + n, 0:D]), g % 4)
            free[("ring", g % 4)] = [m_el, m_sp]
            half, tb = (g % 2) * G, bank[4 + g % 2]
            m_oh = V.done(V.need(m_items, free.get(("one_hot", g % 2))).tensor_tensor(
                one_hot[:, half:half + n, :], spread(iota, 1, n),
                spread(item_local[:, g * G:g * G + n], 2, P), ALU.is_equal))
            for k in range(n):
                m = T.done(T.need(m_oh, bank_free[4 + g % 2]).transpose(
                    tb[:, k * P:(k + 1) * P], one_hot[:, half + k, :], ident))
            free[("one_hot", g % 2)] = m
            m = S.done(S.need(m, free.get(("one_hot_T", g % 2))).activation(
                one_hot_T[:, half:half + n, :], tb[:, 0:n * P].rearrange("p (a b) -> p a b", b=P), ACT.Copy))
            bank_free[4 + g % 2] = m
            eb = bank[6 + g % 2]
            T.need(m, m_er_nodes, bank_free[6 + g % 2], m_item_row)
            T.raw.reg_load(tile_regs_t[0:n], item_tile_row[:, g * G:g * G + n])
            for k in range(n):
                r = T.raw.snap(tile_regs_t[k], min_val=0, max_val=NT - 1)
                m = T.done(T.raw.matmul(eb[:, k * H:(k + 1) * H], one_hot_T[:, half + k, :],
                                        er_nodes.rearrange("p a b -> p (a b)")[:, bass.ds(r * H, H)],
                                        start=True, stop=True))
            free[("one_hot_T", g % 2)] = m
            m_ei = V.done(V.need(m).tensor_copy(per_item[:, g * G:g * G + n, :],
                                                eb[:, 0:n * H].rearrange("p (a b) -> p a b", b=H)))
            bank_free[6 + g % 2] = m_ei
            if g % 16 == 15 or g == NG - 1:
                a, b_ = (g // 16) * 16 * G, min(NI, g * G + G)
                m_es = er_dma.sent(Q.need(m_ei).dma_start(
                    er_slots[a * P:b_ * P, :].rearrange("(i p) h -> p i h", p=P), per_item[:, a:b_, :]))
            background(g)
        m_el_all, m_spilled = m_el, spilled.all()
        m_er = slot_dma.sent(Q.need(m_es).dma_start(er_lane, er_slots.rearrange("(p c) h -> p c h", p=P)))

        def scan(to, data, mask, start, backwards):
            for h in range(H):
                o, d, f = to[:, h, :], data[:, h, :], mask
                if backwards:
                    o, d, f = o[:, ::-1], d[:, ::-1], f[:, ::-1]
                m = V.done(V.raw.tensor_tensor_scan(o, f, d, start if start.__class__ is float else start[:, h:h + 1],
                                                    ALU.add, ALU.max))
            return m

        def carry_in(ends, any_T, backwards, m):
            m = V.done(V.need(m).tensor_copy(carry, ends))
            m = T.done(T.need(m, bank_free[0]).transpose(bank[0][0:H, 0:P], carry, ident))
            m2 = V.done(V.raw.memset(carry_T[0:H, :], -BIG))
            o, f, d = (carry_T[0:H, 0:P], any_T, bank[0][0:H, 0:P]) if backwards else (
                carry_T[0:H, 1:P + 1], any_T, bank[0][0:H, 0:P])
            if backwards:
                o, f, d = o[:, ::-1], f[:, ::-1], d[:, ::-1]
            m = V.done(V.need(m, m2).tensor_tensor_scan(o, f, d, -BIG, ALU.add, ALU.max))
            at = 1 if backwards else 0
            m = T.done(T.need(m).transpose(bank[0][:, P:P + H], carry_T[0:H, at:at + P], ident[0:H, 0:H]))
            m = V.done(V.need(m).tensor_copy(carry_back, bank[0][:, P:P + H]))
            bank_free[0] = m
            return m

        V.need(m_el_all)
        m = scan(fwd, el, fence[:, 0:NI], -BIG, False)
        m = carry_in(fwd[:, :, NI - 1], any_f_T, False, m)
        V.need(m)
        m = scan(fwd, el, fence[:, 0:NI], carry_back, False)
        V.need(m)
        m = scan(top, fwd, fence[:, 1:NI + 1], -BIG, True)
        m = carry_in(top[:, :, 0], any_b_T, True, m)
        V.need(m)
        m = scan(top, fwd, fence[:, 1:NI + 1], carry_back, True)
        er_hc = er_lane.rearrange("p c h -> p h c")
        V.done(V.need(m, m_er).tensor_tensor(el, el, er_hc, ALU.add))
        m = V.done(V.raw.tensor_tensor(top, top, er_hc, ALU.add))
        V.done(V.need(m).scalar_tensor_tensor(el, el, NEG_SLOPE, el, ALU.mult, ALU.max))
        m = V.done(V.raw.scalar_tensor_tensor(top, top, NEG_SLOPE, top, ALU.mult, ALU.max))
        m = V.done(V.need(m).tensor_tensor(el, el, top, ALU.subtract))
        m = S.done(S.need(m).activation(er_lane.rearrange("p c h -> p h c"), el, ACT.Exp))
        m = slot_dma.sent(Q.need(m).dma_start(w_slots.rearrange("(p c) h -> p c h", p=P), er_lane))
        m_w_items = []
        CH = 64
        Q.need(m, m_er)
        for i, a in enumerate(range(0, NI, CH)):
            b_ = min(NI, a + CH)
            m_w_items.append(w_dma[i].sent(Q.raw.dma_start(
                per_item[:, a:b_, :], w_slots[a * P:b_ * P, :].rearrange("(i p) h -> p i h", p=P))))

        m_acc = V.done(V.raw.memset(acc, 0.0))
        acc_flat = acc.rearrange("p a b -> p (a b)")
        Q.need(m_spilled, m_el_all)
        for g in range(NG):
            n = min(G, NI - g * G)
            s0, half = (g % 4) * G, (g % 2) * G
            m_f = back_dma.sent(Q.need(free.get(("ring", g % 4))).dma_start(
                ring_b[:, s0:s0 + n, :], spill[g * G * P:(g * G + n) * P, :].rearrange("(i p) d -> p i d", p=P)), g % 4)
            m_oh = V.done(V.need(free.get(("one_hot", g % 2))).tensor_tensor(
                one_hot[:, half:half + n, :], spread(iota, 1, n),
                spread(item_local[:, g * G:g * G + n], 2, P), ALU.is_equal))
            w_g = per_item[:, g * G:g * G + n, :]
            m_wi = m_w_items[(g * G) // CH]
            msg = messages[:, half:half + n, :]
            m1 = V.done(V.need(m_f, m_wi, free.get(("messages", g % 2))).tensor_tensor(
                msg[:, :, 0:D].rearrange("p i (h d) -> p i h d", h=H),
                ring_b[:, s0:s0 + n, :].rearrange("p i (h d) -> p i h d", h=H),
                spread(w_g, 3, HD), ALU.mult))
            free[("ring", g % 4)] = m1
            m2 = S.done(S.need(m_wi, free.get(("messages", g % 2))).activation(msg[:, :, D:ROW], w_g, ACT.Copy))
            for k in range(n):
                ob = (g * G + k) % 8
                m = T.done(T.need(m1, m2, m_oh, bank_free[ob]).matmul(
                    bank[ob][:, 0:ROW], one_hot[:, half + k, :], messages[:, half + k, :], start=True, stop=True))
                bank_free[ob] = m
            free[("one_hot", g % 2)] = free[("messages", g % 2)] = m
            m_sums = m
            V.raw.reg_load(tile_regs_v[0:n], item_tile_row[:, g * G:g * G + n])
            for k in range(n):
                ob = (g * G + k) % 8
                r = V.raw.snap(tile_regs_v[k], min_val=0, max_val=NT - 1)
                V.need(bank_free[ob], m_acc)
                at = bass.ds(r * ROW, ROW)
                m_acc = V.done(V.raw.tensor_tensor(acc_flat[:, at], acc_flat[:, at], bank[ob][:, 0:ROW], ALU.add))
                bank_free[ob] = m_acc
        m = V.done(V.need(m_acc).tensor_scalar(r_den, acc[:, :, D:ROW], 1e-30, None, ALU.max))
        m = V.done(V.need(m).reciprocal(r_den, r_den))
        V.need(m)
        marks = {}
        for j in range(NT):
            m = V.done(V.raw.tensor_tensor(hidden[:, j, :].rearrange("p (h d) -> p h d", h=H),
                                           acc[:, j, 0:D].rearrange("p (h d) -> p h d", h=H),
                                           spread(r_den[:, j, :], 2, HD), ALU.mult))
            m = V.done(V.need(m).tensor_tensor(hidden[:, j, :], hidden[:, j, :], bias, ALU.add))
            marks[j] = S.done(S.need(m).activation(hidden[:, j, :], hidden[:, j, :], ACT.Relu))
        return marks

    w_dma = [Landing(nc, f"w_items_landed{i}_") for i in range(ceil_div(NI, 64))]

    m_ln = ln_stats([m_x, m_x0])

    def ln_tile(j):
        return rows_in[:, j % 2, :], ln_rows(rows_in[:, j % 2, :], j, m_ln, free.get(("rows", j % 2)))


    keep = arena.used
    arena.used = gat_base
    sort_member = arena.take(N_COL, NT, dtype=BF16)
    sort_prefix = arena.take(N_COL * NT + 1)
    sort_work = arena.take(2, 512)
    sort_small = arena.take(4, NT)
    sort_src = arena.take(N_COL, dtype=I32)
    sort_dst = arena.take(N_COL, dtype=I32)
    sort_local = arena.take(N_COL, dtype=I32)
    sort_tile = arena.take(N_COL)
    sort_pos = arena.take(N_COL)
    sort_void = arena.take(N_COL)
    sort_cmp = arena.take(NIC, NT)
    sort_tiles_f = arena.take(NIC)
    sort_tiles_i = arena.take(NIC, dtype=I32)
    assert arena.used <= after_idle
    arena.used = keep
    sorted_tile_row = sbuf("sorted_tile_row", [1, NI], I32)
    sorted_tile = dram("sorted_tile", (NIC * P,), I32)
    sort_dma = Landing(nc, "sort_landed")
    buckets = Buckets(sort_member, N_COL, NT, sort_prefix, sort_work, sort_small, (0, 1))
    sort = {}

    def split(pos, pos_i, tile, row, m):
        m = V.done(V.need(m).tensor_copy(pos_i, pos))
        m = V.done(V.need(m).tensor_scalar(pos_i, pos_i, 7, None, ALU.arith_shift_right))
        m = V.done(V.need(m).tensor_copy(tile, pos_i))
        return V.done(V.need(m).scalar_tensor_tensor(row, tile, -float(P), pos, ALU.mult, ALU.add))

    def sort_begin():
        full = (N_COL - 1) * P
        m = [V.done(V.raw.memset(sort_src[:, N_COL - 1:N_COL], 1 << 20)),
             V.done(V.raw.memset(sort_dst[:, N_COL - 1:N_COL], 0))]
        Q.need(m, table_dma.all())
        for whole, to in ((t["src"], sort_src), (t["dst"], sort_dst)):
            sort_dma.sent(Q.raw.dma_start(to[:, 0:N_COL - 1], whole[0:full].rearrange("(p c) -> p c", p=P)))
            m_in = sort_dma.sent(Q.raw.dma_start(to[0:E - full, N_COL - 1:N_COL], whole[full:E].unsqueeze(1)))
        m = V.done(V.need(m_in).tensor_scalar(sort_dst, sort_dst, 7, None, ALU.logical_shift_left))
        m2 = V.done(V.raw.tensor_scalar(sort_local, sort_src, P - 1, None, ALU.bitwise_and))
        m = V.done(V.need(m, m2).tensor_tensor(sort_local, sort_local, sort_dst, ALU.bitwise_or))
        m = V.done(V.need(m).tensor_copy(edge_value, sort_local))
        sort["value"] = V.done(V.need(m).tensor_scalar(edge_value, edge_value, 1.0, None, ALU.add))
        m = V.done(V.need(m).tensor_scalar(sort_src, sort_src, 7, None, ALU.arith_shift_right))
        m = V.done(V.need(m).tensor_copy(sort_tile, sort_src))
        sort["m"] = V.done(V.need(m).tensor_scalar(sort_void, sort_tile, float(NT), None, ALU.is_ge))

    def sort_members(a, b):
        sort["m"] = V.done(V.need(sort["m"]).tensor_tensor(
            sort_member[:, a:b, :], spread(iota[:, 0:NT], 1, b - a), spread(sort_tile[:, a:b], 2, NT), ALU.is_equal))

    def sort_end():
        m = V.done(V.need(buckets.m_pos).tensor_tensor(sort_pos, sort_pos, sort_void, ALU.subtract))
        sort["m"] = split(sort_pos, sort_src, edge_to_tile, edge_to_row, m)
        sort["row"] = buckets.tile_row(NI, sort_cmp, sort_tiles_f, sort_tiles_i, sorted_tile, sorted_tile_row, sort_dma)

    sort_todo = [sort_begin]
    for a, b in buckets.chunks:
        sort_todo.append(lambda a=a, b=b: sort_members(a, b))
    for q in range(len(buckets.chunks)):
        sort_todo.append(lambda q=q: buckets.totals(q, sort["m"]))
    sort_todo.append(buckets.scan)
    for q in range(len(buckets.chunks)):
        sort_todo.append(lambda q=q: buckets.positions(q, sort_pos))
    sort_todo.append(sort_end)
    assert len(sort_todo) + 4 <= NG

    def sort_step(g):
        if g >= 4 and sort_todo:
            sort_todo.pop(0)()

    arena.used = gat_base + NT * D + 64
    to_row = arena.take(8, P)
    to_tile = arena.take(8, NI)
    iota_tiles = arena.take(NI)
    assert arena.used <= after_idle
    arena.used = keep
    INV = 3

    def invert_step(g):
        if g == 0:
            sort["iota"] = L.done(L.need(h1[0]).iota(iota_tiles, [[1, NI]], base=0, channel_multiplier=0,
                                                     allow_small_or_imprecise_dtypes=True))
            return
        per = ceil_div(N_COL, NG - 4)
        for c in range((g - 1) * per, min(N_COL, g * per)):
            s = c % 8
            m1 = V.done(V.need(sort["m"], sort["iota"], sort.get(("inv", s))).tensor_scalar(
                to_row[:, s, :], iota, edge_to_row[:, c:c + 1], None, ALU.is_equal))
            m = V.done(V.raw.tensor_scalar(to_tile[:, s, :], iota_tiles, edge_to_tile[:, c:c + 1],
                                           edge_value[:, c:c + 1], ALU.is_equal, ALU.mult))
            sort[("inv", s)] = m = T.done(T.need(m, bank_free[INV]).matmul(
                bank[INV][:, 0:NI], to_row[:, s, :], to_tile[:, s, :], start=(c == 0), stop=(c == N_COL - 1)))
            if c == N_COL - 1:
                sort["sorted"] = bank_free[INV] = V.done(V.need(m).tensor_copy(sorted_value, bank[INV][:, 0:NI]))

    h1 = gat(0, t["L0_gnn_W1"], t["L0_gnn_al1"], t["L0_gnn_ar1"], t["L0_gnn_b1"], ln_tile,
             [m_fence, m_any, m_item_local, m_lane, stream_dma.all(), ], sort_step)
    h2 = gat(1, t["L0_gnn_W2"], t["L0_gnn_al2"], t["L0_gnn_ar2"], t["L0_gnn_b2"],
             lambda j: (hidden[:, j, :], h1[j]), list(h1.values()), invert_step)
    m_x = {}
    for j in range(NT):
        m_x[j] = V.done(V.need(h2[j]).tensor_tensor(x[:, j, :], x[:, j, :], hidden[:, j, :], ALU.add))

    arena.used = 0
    probs_dma = Landing(nc, "router_landed")
    wide_dma = Landing(nc, "expert_weights_landed")
    shared_dma = Landing(nc, "shared_weights_landed")
    wide2_dma = Landing(nc, "expert_weights2_landed")
    token_dma = Landing(nc, "token_rows_written", 4)
    tile_in_dma = Landing(nc, "expert_tile_in", 4)
    tile_out_dma = Landing(nc, "expert_tile_out", 2)
    pick_dma = Landing(nc, "expert_rows_picked", 4)
    misc_dma = Landing(nc, "tile_rows_moved")

    def experts(layer, m_x, n_exp, F, w1_dram, b1_dram, w2_dram, b2_dram, router, router_bias,
                shared, base, w1_ready, act, m_space, finish):
        FC = F // P
        ntiles, expert_out = max_tiles[layer], expert_rows[layer]
        free = {}
        arena.used = base[0]
        w1 = arena.take(n_exp, K, F) if w1_ready is None else w1_ready[0]
        w2_at = arena.used
        w2 = arena.take(n_exp, FC, D)
        w2_end = arena.used
        now_at = arena.used
        w1_now = arena.take(2, K, F)
        if shared:
            arena.used = now_at
            w1s, w2s = arena.take(K, F), arena.take(FC, D)
            b1s = arena.take(FC)
        b1 = arena.take(n_exp, FC)
        b2 = arena.take(D)
        wr = arena.take(K, n_exp)
        mask = arena.take(NT, n_exp + 1)
        mask_T = arena.take(2, P)
        pair_w = arena.take(2, NT)
        pair_at = arena.take(2 * NT, dtype=U32)
        tile_row = arena.take(max(max_tiles), dtype=I32)[0:1, :]
        slot_token = arena.take(max(max_tiles), dtype=U32)
        work_at = arena.used
        rows = arena.take(4, D)
        rows_T = arena.take(2, K, 2 * P)
        hid_s = arena.take(FC, 2 * P) if shared else None
        arena.used = w2_at
        logits = arena.take(NT, n_exp)
        hit = arena.take(2, NT, n_exp)
        probs = arena.take(NT, n_exp)
        tmp = arena.take(NT, n_exp)
        one = arena.take(4, NT)
        member = arena.take(2 * NT, n_exp, dtype=BF16)
        prefix = arena.take(2 * NT * n_exp + 1)
        work = arena.take(2, 512)
        small = arena.take(4, n_exp)
        compare = arena.take(1, n_exp)
        tiles_f, tiles_i = arena.take(1), arena.take(1, dtype=I32)
        pos = arena.take(2 * NT)
        bias_r = arena.take(n_exp)
        pos_i = arena.take(2 * NT, dtype=I32)
        at_tile, at_row = arena.take(2 * NT), arena.take(2 * NT)
        token = arena.take(2, NT)
        to_row = arena.take(2 * NT, P)
        to_tile = arena.take(2 * NT, ntiles)
        assert arena.used <= w2_end

        Q.need(m_space)
        m_wr = probs_dma.sent(Q.raw.dma_start(wr, router.rearrange("(k p) e -> p k e", p=P)))
        probs_dma.sent(Q.raw.dma_start(b2[0:n_exp, :], b2_dram))
        if shared:
            probs_dma.sent(Q.raw.dma_start(b2[n_exp:n_exp + 1, :], shared[3].unsqueeze(0)))
        if router_bias is not None:
            probs_dma.sent(Q.raw.dma_start(bias_r, router_bias.partition_broadcast(P)))
        with nc.allow_non_contiguous_dma(reason="the first biases, one column per 128 units"):
            if shared:
                probs_dma.sent(Q.raw.dma_start(b1s, shared[1].rearrange("(c p) -> p c", p=P)))
            for e in range(n_exp):
                m_wr = probs_dma.sent(Q.raw.dma_start(b1[:, e, :], b1_dram[e].rearrange("(c p) -> p c", p=P)))
        if shared:
            shared_dma.sent(Q.raw.dma_start(w1s, shared[0].rearrange("(k p) f -> p k f", p=P)))
            m_ws = shared_dma.sent(Q.raw.dma_start(w2s, shared[2].rearrange("(c p) d -> p c d", p=P)))
        if w1_ready is None:
            for e in range(n_exp):
                m_w1 = wide_dma.sent(Q.raw.dma_start(w1[:, e, :, :], w1_dram[e].rearrange("(k p) f -> p k f", p=P)))
        else:
            m_w1 = w1_ready[1]

        m_ln = ln_stats(m_x)
        lb = 2
        for j in range(NT):
            m = ln_rows(rows[:, j % 4, :], j, [m_ln, m_space], free.get(("rows", j % 4)))
            for k in range(K):
                m2 = T.done(T.need(m, bank_free[j % 2]).transpose(bank[j % 2][:, k * P:(k + 1) * P],
                                                                  rows[:, j % 4, k * P:(k + 1) * P], ident))
            n = P if j < NT - 1 else LAST
            free[("rows", j % 4)] = [m2, token_dma.sent(Q.need(m).dma_start(
                token_rows[layer][j * P:j * P + n, :], rows[0:n, j % 4, :]), j % 4)]
            m2 = S.done(S.need(m2, free.get(("rows_T", j % 2))).activation(
                rows_T[:, j % 2, :, 0:P], bank[j % 2][:, 0:K * P].rearrange("p (k n) -> p k n", k=K), ACT.Copy))
            bank_free[j % 2] = m2
            for k in range(K):
                m = T.done(T.need(m2, m_wr, bank_free[lb]).matmul(
                    bank[lb][:, j * n_exp:(j + 1) * n_exp], rows_T[:, j % 2, k, 0:P], wr[:, k, :],
                    start=(k == 0), stop=(k == K - 1)))
            free[("rows_T", j % 2)] = m
        m = V.done(V.need(m, m_space).tensor_copy(logits, bank[lb][:, 0:NT * n_exp].rearrange("p (j e) -> p j e", e=n_exp)))
        bank_free[lb] = m
        if router_bias is not None:
            m = V.done(V.need(m, m_wr).tensor_tensor(logits, logits, spread(bias_r, 1, NT), ALU.add))
        top1, top2, den, s4 = (one[:, i, :] for i in range(4))

        def over(v):
            return spread(v, 2, n_exp)

        if shared:
            m = V.done(V.need(m).tensor_reduce(top1, logits, AX.X, ALU.max))
            m = V.done(V.need(m).tensor_tensor(probs, logits, over(top1), ALU.subtract))
            m = S.done(S.need(m).activation(probs, probs, ACT.Exp))
            m = V.done(V.need(m).tensor_reduce(den, probs, AX.X, ALU.add))
            m = V.done(V.need(m).reciprocal(den, den))
            m = V.done(V.need(m).tensor_tensor(probs, probs, over(den), ALU.mult))
            score = probs
        else:
            score = logits
        m_score = m
        experts_iota = iota[:, 0:n_exp]
        for k, best in ((0, top1), (1, top2)):
            src_ = score if k == 0 else tmp
            m = V.done(V.need(m).tensor_reduce(best, src_, AX.X, ALU.max))
            h_ = hit[:, k, :, :]
            m = V.done(V.need(m).tensor_tensor(h_, src_, over(best), ALU.is_lt))
            m = V.done(V.need(m).scalar_tensor_tensor(h_, h_, float(P), spread(experts_iota, 1, NT), ALU.mult, ALU.add))
            m = V.done(V.need(m).tensor_reduce(s4, h_, AX.X, ALU.min))
            m = V.done(V.need(m).tensor_tensor(h_, spread(experts_iota, 1, NT), over(s4), ALU.is_equal))
            if k == 0:
                m = V.done(V.need(m).scalar_tensor_tensor(tmp, h_, -BIG, score, ALU.mult, ALU.add))
        m_hit = m
        if shared:
            m = V.done(V.need(m).tensor_tensor(den, top1, top2, ALU.add))
            m = V.done(V.need(m).reciprocal(den, den))
            V.done(V.need(m).tensor_tensor(pair_w[:, 0, :], top1, den, ALU.mult))
            m = V.done(V.raw.tensor_tensor(pair_w[:, 1, :], top2, den, ALU.mult))
        else:
            m = V.done(V.need(m).tensor_tensor(top2, top2, top1, ALU.subtract))
            m = S.done(S.need(m).activation(top2, top2, ACT.Exp))
            m = V.done(V.need(m).tensor_scalar(den, top2, 1.0, None, ALU.add))
            m = V.done(V.need(m).reciprocal(pair_w[:, 0, :], den))
            m = V.done(V.need(m).tensor_tensor(pair_w[:, 1, :], top2, pair_w[:, 0, :], ALU.mult))
        for k in range(2):
            m = V.done(V.need(m, m_valid).tensor_scalar(hit[:, k, NT - 1, :], hit[:, k, NT - 1, :],
                                                        valid_row, None, ALU.mult))
        V.need(m)
        m = V.done(V.raw.tensor_copy(member, hit.rearrange("p k j e -> p (k j) e")))
        m_mask = V.done(V.raw.memset(mask, 1.0))
        V.done(V.need(m).tensor_tensor(hit[:, 0, :, :], hit[:, 0, :, :], over(pair_w[:, 0, :]), ALU.mult))
        m2 = V.done(V.raw.tensor_tensor(hit[:, 1, :, :], hit[:, 1, :, :], over(pair_w[:, 1, :]), ALU.mult))
        m_mask = V.done(V.need(m2, m_mask).tensor_tensor(mask[:, :, 0:n_exp], hit[:, 0, :, :], hit[:, 1, :, :], ALU.add))
        bk = Buckets(member, 2 * NT, n_exp, prefix, work, small, (2, 3))
        for q in range(len(bk.chunks)):
            bk.totals(q, m)
        bk.scan()
        for q in range(len(bk.chunks)):
            bk.positions(q, pos)
        m = bk.m_pos
        m_pos = V.done(V.need(m).tensor_copy(pair_at, pos))
        m2 = V.done(V.need(m_valid, m).tensor_scalar(s4[:, 0:1], valid_row, -1.0, None, ALU.add))
        m = m_pos
        for k in range(2):
            at = k * NT + NT - 1
            m = V.done(V.need(m, m2).tensor_tensor(pos[:, at:at + 1], pos[:, at:at + 1], s4[:, 0:1], ALU.add))
        m = split(pos, pos_i, at_tile, at_row, m)
        V.done(V.need(m).tensor_tensor(to_row, spread(iota, 1, 2 * NT), spread(at_row, 2, P), ALU.is_equal))
        m1 = V.done(V.raw.tensor_tensor(to_tile, spread(iota[:, 0:ntiles], 1, 2 * NT), spread(at_tile, 2, ntiles),
                                        ALU.is_equal))
        for k in range(2):
            m2 = V.done(V.raw.tensor_scalar(token[:, k, :], iota[:, 0:NT], float(P), iota_item[:, 0:1], ALU.mult, ALU.add))
        m = V.done(V.need(m1, m2).tensor_tensor(to_tile, to_tile, spread(token.rearrange("p k j -> p (k j)"), 2, ntiles), ALU.mult))
        for q in range(2 * NT):
            mt = T.need(m, bank_free[4]).matmul(bank[4][:, 0:ntiles], to_row[:, q, :], to_tile[:, q, :],
                                                start=(q == 0), stop=(q == 2 * NT - 1))
        mt = T.done(mt)
        m_slots = bank_free[4] = V.done(V.need(mt).tensor_copy(slot_token[:, 0:ntiles], bank[4][:, 0:ntiles]))
        m_row = bk.tile_row(ntiles, compare, tiles_f, tiles_i, misc_row[layer], tile_row[:, 0:ntiles], misc_dma)
        for e in range(n_exp):
            m_w2 = wide2_dma.sent(Q.need(m_row, m_slots, m_mask).dma_start(
                w2[:, e, :, :], w2_dram[e].rearrange("(c p) d -> p c d", p=P)))

        m_tokens = token_dma.all()
        for a in range(0, NT if shared else 0, 2):
            js = list(range(a, min(NT, a + 2)))
            half = (a // 2) % 2
            for i, j in enumerate(js):
                s = half * 2 + i
                m = ln_rows(rows[:, s, :], j, m_ln, free.get(("rows", s)))
                for k in range(K):
                    m2 = T.done(T.need(m, bank_free[i]).transpose(bank[i][:, k * P:(k + 1) * P],
                                                                  rows[:, s, k * P:(k + 1) * P], ident))
                free[("rows", s)] = m2
                m2 = S.done(S.need(m2, free.get(("rows_T", half))).activation(
                    rows_T[:, half, :, i * P:(i + 1) * P],
                    bank[i][:, 0:K * P].rearrange("p (k n) -> p k n", k=K), ACT.Copy))
                bank_free[i] = m2
            n = len(js) * P
            for f in range(FC):
                hb = 2 + f % 4
                for k in range(K):
                    m = T.done(T.need(m2, m_ws, bank_free[hb]).matmul(
                        bank[hb][:, 0:n], w1s[:, k, f * P:(f + 1) * P], rows_T[:, half, k, 0:n],
                        start=(k == 0), stop=(k == K - 1)))
                m3 = S.done(S.need(m, free.get("hid_s")).activation(hid_s[:, f, 0:n], bank[hb][:, 0:n], act,
                                                                    bias=b1s[:, f:f + 1]))
                bank_free[hb] = m3
            free[("rows_T", half)] = m
            for i, j in enumerate(js):
                m = T.done(T.need(m_mask, bank_free[i]).transpose(bank[i][0:n_exp + 1, 0:P], mask[:, j, :], ident))
                m = S.done(S.need(m, free.get(("mask_T", i))).activation(mask_T[0:n_exp + 1, i, :], bank[i][0:n_exp + 1, 0:P], ACT.Copy))
                bank_free[i] = m
                yb = 6 + i
                T.need(m, m_wr, bank_free[yb]).matmul(bank[yb][:, 0:D], mask_T[0:n_exp + 1, i, :], b2[0:n_exp + 1, :],
                                                      start=True, stop=False)
                for f in range(FC):
                    m = T.done(T.need(m3).matmul(bank[yb][:, 0:D], hid_s[:, f, i * P:(i + 1) * P], w2s[:, f, :],
                                                 start=False, stop=(f == FC - 1)))
                free[("mask_T", i)] = m
                m_x[j] = V.done(V.need(m).tensor_tensor(x[:, j, :], x[:, j, :], bank[yb][:, 0:D], ALU.add))
                bank_free[yb] = m_x[j]
            free["hid_s"] = m
        m_shared = [m, m_tokens, bank_free[0], bank_free[1], m_x[NT - 1] if shared else None]

        arena.used = work_at
        tin = arena.take(4, D)
        tin_T = arena.take(2, K, P)
        hid = arena.take(2, FC, P)
        tout = arena.take(2, D)
        bcol = arena.take(2, FC)
        assert arena.used <= arena.words
        pre = ("first_w", layer)
        w1_flat = w1.rearrange("p e k f -> p (e k f)")
        w2_flat = w2.rearrange("p e c d -> p (e c d)")
        b1_flat = b1.rearrange("p e c -> p (e c)")
        m_hid, m_b = {}, {}

        def second(q):
            s = q % 2
            T.need(m_hid[q], m_w2, bank_free[6 + s])
            T.raw.reg_load(exp_t2, tile_row[:, q:q + 1])
            r = T.raw.snap(exp_t2, min_val=0, max_val=n_exp - 1)
            for f in range(FC):
                m = T.raw.matmul(bank[6 + s][:, 0:D], hid[:, s, f, :], w2_flat[:, bass.ds(r * (FC * D) + f * D, D)],
                                 start=(f == 0), stop=(f == FC - 1))
            m = T.done(m)
            free[("hid", s)] = m
            m = V.done(V.need(m, free.get(("tout", s))).tensor_copy(tout[:, s, :], bank[6 + s][:, 0:D]))
            bank_free[6 + s] = m
            free[("tout", s)] = tile_out_dma.sent(Q.need(m).dma_start(expert_out[q * P:(q + 1) * P, :], tout[:, s, :]), s)

        def load(q):
            m_in[q] = tile_in_dma.sent(L.need(m_tokens, m_shared, m_slots, free.get(("tin", q % 4))).indirect_dma_start(
                out=tin[:, q % 4, :], out_offset=None, in_=token_rows[layer],
                in_offset=bass.IndirectOffsetOnAxis(ap=slot_token[:, q:q + 1], axis=0)), q % 4)

        m_in = {}
        for q in range(3):
            load(q)
        S.need(m_shared)
        V.need(m_shared)
        for q in range(ntiles):
            s = q % 2
            if q + 3 < ntiles:
                load(q + 3)
            for k in range(K):
                m = T.done(T.need(m_in[q], bank_free[s]).transpose(bank[s][:, k * P:(k + 1) * P],
                                                                   tin[:, q % 4, k * P:(k + 1) * P], ident))
            free[("tin", q % 4)] = m
            m = V.done(V.need(m, free.get(("tin_T", s))).tensor_copy(
                tin_T[:, s, :, :], bank[s][:, 0:K * P].rearrange("p (k n) -> p k n", k=K)))
            bank_free[s] = m
            S.need(m_row, m_wr, free.get(("bcol", s)))
            S.raw.reg_load(exp_s, tile_row[:, q:q + 1])
            r = S.raw.snap(exp_s, min_val=0, max_val=n_exp - 1)
            m_b = S.done(S.raw.activation(bcol[:, s, :], b1_flat[:, bass.ds(r * FC, FC)], ACT.Copy))
            V.need(m_w1, m_row, free.get(("w1_now", s)))
            V.raw.reg_load(exp_v, tile_row[:, q:q + 1])
            r = V.raw.snap(exp_v, min_val=0, max_val=n_exp - 1)
            m_now = V.done(V.raw.tensor_copy(w1_now[:, s, :, :].rearrange("p k f -> p (k f)"),
                                             w1_flat[:, bass.ds(r * (K * F), K * F)]))
            T.need(m, m_now)
            per = 4
            for f0 in range(0, FC, per):
                hb = 2 + s * 2 + f0 // per
                T.need(bank_free[hb])
                for f in range(f0, min(FC, f0 + per)):
                    for k in range(K):
                        m = T.raw.matmul(bank[hb][:, (f - f0) * P:(f - f0 + 1) * P],
                                         w1_now[:, s, k, f * P:(f + 1) * P], tin_T[:, s, k, :],
                                         start=(k == 0), stop=(k == K - 1))
                m = T.done(m)
                for f in range(f0, min(FC, f0 + per)):
                    m2 = S.done(S.need(m, m_b, free.get(("hid", s))).activation(
                        hid[:, s, f, :], bank[hb][:, (f - f0) * P:(f - f0 + 1) * P], act, bias=bcol[:, s, f:f + 1]))
                bank_free[hb] = m2
            free[("tin_T", s)] = free[("w1_now", s)] = m
            m_hid[q] = m2
            free[("bcol", s)] = m2
            if q:
                second(q - 1)
        second(ntiles - 1)
        m_tiles = tile_out_dma.all()

        arena.used = base[0]
        picked = arena.take(4, 2, D)
        finish_space = arena.used
        L.need(m_tiles)
        for j in range(NT):
            s = j % 4
            for k in range(2):
                at = k * NT + j
                m = pick_dma.sent(L.need(free.get(("picked", s)), free[("hid", 0)], free[("hid", 1)]).indirect_dma_start(
                    out=picked[:, s, k, :], out_offset=None, in_=expert_out,
                    in_offset=bass.IndirectOffsetOnAxis(ap=pair_at[:, at:at + 1], axis=0)), s)
            free[("picked", s)] = finish(j, m, picked[:, s, :, :], pair_w, mask, mask_T, b2, m_ln, finish_space, m_x)
        return free

    exp_v, exp_t2, exp_s = (e.raw.alloc_register(n) for e, n in ((V, "expert_first"), (T, "expert_second"), (S, "expert_bias")))
    token_rows = [dram(f"token_rows{n}", (N, D)) for n in range(2)]
    expert_rows = [dram(f"expert_rows{n}", (max_tiles[n] * P, D)) for n in range(2)]
    misc_row = [dram(f"expert_of_tile{n}", (P,), I32) for n in range(2)]

    def finish_shared(j, m, rows, pair_w, mask, mask_T, b2, m_ln, space, m_x):
        for k in range(2):
            m = V.done(V.need(m, m_x[j]).scalar_tensor_tensor(
                x[:, j, :], rows[:, k, :], pair_w[:, k, j:j + 1], x[:, j, :], ALU.mult, ALU.add))
        m_x[j] = m
        return m

    m_space0 = [list(h2.values()), list(m_x.values())]
    experts(0, m_x, E0, F0, t["L0_ffn_W1p"], t["L0_ffn_b1p"], t["L0_ffn_W2p"], t["L0_ffn_b2p"], t["L0_ffn_Wr"], None,
            (t["L0_ffn_W1s"], t["L0_ffn_b1s"], t["L0_ffn_W2s"], t["L0_ffn_b2s"]), [0], None, ACT.Gelu,
            m_space0, finish_shared)

    arena.used = 0
    w1_next = arena.take(E1, K, F1)
    next_base = 0
    space = list(m_x.values())
    sums = arena.take(NT, D + 2)
    g_ring = arena.take(16, D + 2)
    g_hot = arena.take(2 * G, P)
    s_dst_i = arena.take(NI, dtype=I32)
    s_dst_f = arena.take(NI)
    s_dst = arena.take(NI, dtype=U32)
    s_loc = arena.take(NI)
    wa = arena.take(2, K, D)
    wT = arena.take(2, K, D)
    b12 = arena.take(2, D)
    n_rows = arena.take(4, D)
    n_T = arena.take(2, K * P)
    means = arena.take(2, D)
    r_cnt = arena.take(NT)
    norm_table = dram("norm_table", (N, D))
    l1_dma = Landing(nc, "second_graph_landed")
    norm_dma = Landing(nc, "norm_rows_written", 4)
    g_dma = Landing(nc, "neighbours_gathered", 4)
    next_dma = Landing(nc, "next_weights_landed")
    Q.need(space)
    for n, name in ((0, "L1_gnn_W1"), (1, "L1_gnn_W2")):
        l1_dma.sent(Q.raw.dma_start(wa[:, n, :, :], t[name].rearrange("(o p) i -> p o i", p=P)))
    for n, name in ((0, "L1_gnn_b1"), (1, "L1_gnn_b2")):
        m_in = l1_dma.sent(Q.raw.dma_start(b12[:, n, :], t[name].partition_broadcast(P)))
    V.need(space)
    m_ln = ln_stats(m_x)
    m = V.done(V.need(m_in).tensor_tensor(b12[:, 0, :], b12[:, 0, :], b12[:, 1, :], ALU.add))
    m_b12 = m
    for n in range(2):
        for o in range(K):
            for i in range(K):
                mt = T.done(T.need(m_in, bank_free[4 + n]).transpose(
                    bank[4 + n][:, (i * K + o) * P:(i * K + o + 1) * P], wa[:, n, o, i * P:(i + 1) * P], ident))
        m_wT = V.done(V.need(mt).tensor_copy(wT[:, n, :, :].rearrange("p i o -> p (i o)"), bank[4 + n][:, 0:K * D]))
        bank_free[4 + n] = m_wT
    m = V.done(V.need(sort["sorted"]).tensor_scalar(s_loc, sorted_value, -1.0, None, ALU.add))
    m = V.done(V.need(m).tensor_copy(s_dst_i, s_loc))
    m = V.done(V.need(m).tensor_scalar(s_dst_i, s_dst_i, 7, None, ALU.arith_shift_right))
    m = V.done(V.need(m).tensor_copy(s_dst_f, s_dst_i))
    m = V.done(V.need(m).tensor_scalar(s_dst_f, s_dst_f, 0.0, None, ALU.max))
    m = V.done(V.need(m).scalar_tensor_tensor(s_loc, s_dst_f, -float(P), s_loc, ALU.mult, ALU.add))
    m_sd = V.done(V.raw.tensor_copy(s_dst, s_dst_f))
    m_own = V.done(V.raw.memset(sums, 0.0))
    m_one = V.done(V.raw.memset(g_ring[:, :, D:D + 2], 1.0))
    lfree = {}
    m_rows_of = {}
    for j in range(NT):
        s = j % 4
        m_rows_of[j] = ln_rows(n_rows[:, s, :], j, m_ln, lfree.get(("n_rows", s)))
        n = P if j < NT - 1 else LAST
        m_t = norm_dma.sent(Q.need(m_rows_of[j]).dma_start(norm_table[j * P:j * P + n, :], n_rows[0:n, s, :]), s)
        b_ = j % 2
        for k in range(K):
            m = T.done(T.need(m_rows_of[j], bank_free[b_]).transpose(bank[b_][:, k * P:(k + 1) * P],
                                                                     n_rows[:, s, k * P:(k + 1) * P], ident))
        lfree[("n_rows", s)] = [m, m_t]
        m = S.done(S.need(m, lfree.get(("n_T", b_))).activation(n_T[:, b_, :], bank[b_][:, 0:K * P], ACT.Copy))
        bank_free[b_] = m
        for k in range(K):
            m = T.done(T.need(m, m_wT, bank_free[2 + b_]).matmul(
                bank[2 + b_][:, 0:D], n_T[:, b_, k * P:(k + 1) * P], wT[:, 0, k, :], start=(k == 0), stop=(k == K - 1)))
        lfree[("n_T", b_)] = m
        m = V.done(V.need(m).tensor_tensor(x[:, j, :], x[:, j, :], bank[2 + b_][:, 0:D], ALU.add))
        bank_free[2 + b_] = m
        m_x[j] = V.done(V.need(m, m_b12).tensor_tensor(x[:, j, :], x[:, j, :], b12[:, 0, :], ALU.add))
    for e in range(E1):
        m_w1n = next_dma.sent(Q.raw.dma_start(w1_next[:, e, :, :], t["L1_ffn_w1"][e].rearrange("(k p) f -> p k f", p=P)))
    L.need(norm_dma.all())
    sums_flat = sums.rearrange("p a b -> p (a b)")
    m_acc = m_own
    for g in range(NG):
        n = min(G, NI - g * G)
        s0, half = (g % 4) * G, (g % 2) * G
        for k in range(n):
            c = g * G + k
            m_g = g_dma.sent(L.need(m_sd, lfree.get(("ring", g % 4)), m_one).indirect_dma_start(
                out=g_ring[:, s0 + k, 0:D], out_offset=None, in_=norm_table,
                in_offset=bass.IndirectOffsetOnAxis(ap=s_dst[:, c:c + 1], axis=0)), g % 4)
        m_oh = V.done(V.need(lfree.get(("hot", g % 2))).tensor_tensor(
            g_hot[:, half:half + n, :], spread(iota, 1, n),
            spread(s_loc[:, g * G:g * G + n], 2, P), ALU.is_equal))
        for k in range(n):
            ob = (g * G + k) % 8
            m = T.done(T.need(m_g, m_oh, m_one, bank_free[ob]).matmul(
                bank[ob][:, 0:D + 2], g_hot[:, half + k, :], g_ring[:, s0 + k, :], start=True, stop=True))
            bank_free[ob] = m
        lfree[("hot", g % 2)] = lfree[("ring", g % 4)] = m
        V.need(sort["row"])
        V.raw.reg_load(tile_regs_v[0:n], sorted_tile_row[:, g * G:g * G + n])
        for k in range(n):
            ob = (g * G + k) % 8
            r = V.raw.snap(tile_regs_v[k], min_val=0, max_val=NT - 1)
            V.need(bank_free[ob], m_acc)
            at = bass.ds(r * (D + 2), D + 2)
            m_acc = V.done(V.raw.tensor_tensor(sums_flat[:, at], sums_flat[:, at], bank[ob][:, 0:D + 2], ALU.add))
            bank_free[ob] = m_acc
    m = V.done(V.need(m_acc).tensor_scalar(r_cnt, sums[:, :, D], 1.0, None, ALU.max))
    m_rc = V.done(V.need(m).reciprocal(r_cnt, r_cnt))
    for j in range(NT):
        b_ = j % 2
        m = V.done(V.need(m_rc, lfree.get(("means", b_))).tensor_scalar(
            means[:, b_, :], sums[:, j, 0:D], r_cnt[:, j:j + 1], None, ALU.mult))
        for k in range(K):
            m2 = T.done(T.need(m, bank_free[b_]).transpose(bank[b_][:, k * P:(k + 1) * P],
                                                           means[:, b_, k * P:(k + 1) * P], ident))
        lfree[("means", b_)] = m2
        m = S.done(S.need(m2, lfree.get(("n_T", b_))).activation(n_T[:, b_, :], bank[b_][:, 0:K * P], ACT.Copy))
        bank_free[b_] = m
        for k in range(K):
            m = T.done(T.need(m, bank_free[2 + b_]).matmul(
                bank[2 + b_][:, 0:D], n_T[:, b_, k * P:(k + 1) * P], wT[:, 1, k, :], start=(k == 0), stop=(k == K - 1)))
        lfree[("n_T", b_)] = m
        m_x[j] = V.done(V.need(m, m_x[j]).tensor_tensor(x[:, j, :], x[:, j, :], bank[2 + b_][:, 0:D], ALU.add))
        bank_free[2 + b_] = m_x[j]

    out_dma = Landing(nc, "out_written")
    efree = {}

    def finish_last(j, m, rows, pair_w, mask, mask_T, b2, m_ln, space, m_x):
        if "y" not in efree:
            arena.used = space
            efree["y"] = arena.take(2, D)
            efree["st"] = arena.take(2, 10)
            efree["gb"] = arena.take(2, D)
            for n, name in ((0, "L1_ffn_gamma"), (1, "L1_ffn_beta")):
                efree["m_gb"] = l1_dma.sent(Q.need(m).dma_start(efree["gb"][:, n, :], t[name].partition_broadcast(P)))
        y, st = efree["y"][:, j % 2, :], efree["st"][:, j % 2, :]
        gamma_beta, m_gb = efree["gb"], efree["m_gb"]
        b_ = j % 2
        mt = T.done(T.need(bank_free[b_]).transpose(bank[b_][0:E1, 0:P], mask[:, j, 0:E1], ident))
        mt = S.done(S.need(mt, efree.get(("mask_T", b_))).activation(mask_T[0:E1, b_, :], bank[b_][0:E1, 0:P], ACT.Copy))
        bank_free[b_] = mt
        mt = T.done(T.need(mt, bank_free[2 + b_]).matmul(bank[2 + b_][:, 0:D], mask_T[0:E1, b_, :], b2[0:E1, :],
                                                         start=True, stop=True))
        efree[("mask_T", b_)] = mt
        my = ln_rows(y, j, [m_ln, m], efree.get(("y", b_)))
        my = V.done(V.need(my, mt).tensor_tensor(y, y, bank[2 + b_][:, 0:D], ALU.add))
        bank_free[2 + b_] = my
        for k in range(2):
            my = V.done(V.need(my, m).scalar_tensor_tensor(y, rows[:, k, :], pair_w[:, k, j:j + 1], y, ALU.mult, ALU.add))
        m_free = my
        my = V.done(V.need(my).bn_stats(st[:, 0:6], y))
        my = V.done(V.need(my).bn_aggr(st[:, 6:8], st[:, 0:6]))
        my = V.done(V.need(my).tensor_scalar(st[:, 8:9], st[:, 7:8], EPS, None, ALU.add))
        my = S.done(S.need(my).activation(st[:, 8:9], st[:, 8:9], ACT.Sqrt))
        my = V.done(V.need(my).reciprocal(st[:, 8:9], st[:, 8:9]))
        my = V.done(V.need(my).tensor_scalar(y, y, st[:, 6:7], st[:, 8:9], ALU.subtract, ALU.mult))
        my = V.done(V.need(my, m_gb).tensor_tensor(y, y, gamma_beta[:, 0, :], ALU.mult))
        my = V.done(V.need(my).tensor_tensor(y, y, gamma_beta[:, 1, :], ALU.add))
        efree[("y", b_)] = m_x[j] = V.done(V.need(my, m_x[j]).tensor_tensor(x[:, j, :], x[:, j, :], y, ALU.add))
        n = P if j < NT - 1 else LAST
        out_dma.sent(Q.need(m_x[j]).dma_start(out[j * P:j * P + n, :], x[0:n, j, :]))
        return m_free

    arena.used = 0
    w1_ready = (arena.take(E1, K, F1), m_w1n)
    experts(1, m_x, E1, F1, None, t["L1_ffn_b1"], t["L1_ffn_w2"], t["L1_ffn_b2"], t["L1_ffn_gate_w"],
            t["L1_ffn_gate_b"], None, [arena.used], w1_ready, ACT.Relu,
            list(m_x.values()), finish_last)
    Q.need(out_dma.all())
    return

    out_dma = Landing(nc, "out_written")
    for j in range(NT):
        n = P if j < NT - 1 else LAST
        out_dma.sent(Q.need(m_x[j]).dma_start(out[j * P:j * P + n, :], x[0:n, j, :]))
    Q.need(out_dma.all())


_INS = ['x', 'src', 'dst', 'L0_gnn_W1', 'L0_gnn_al1', 'L0_gnn_ar1', 'L0_gnn_b1', 'L0_gnn_W2', 'L0_gnn_al2',
        'L0_gnn_ar2', 'L0_gnn_b2', 'L0_ffn_Wr', 'L0_ffn_W1s', 'L0_ffn_b1s', 'L0_ffn_W2s', 'L0_ffn_b2s',
        'L0_ffn_W1p', 'L0_ffn_b1p', 'L0_ffn_W2p', 'L0_ffn_b2p', 'L1_gnn_W1', 'L1_gnn_b1', 'L1_gnn_W2',
        'L1_gnn_b2', 'L1_ffn_gate_w', 'L1_ffn_gate_b', 'L1_ffn_w1', 'L1_ffn_b1', 'L1_ffn_w2', 'L1_ffn_b2',
        'L1_ffn_gamma', 'L1_ffn_beta']


def kernel(**inputs):
    import numpy as _np
    import concourse.bacc as _bacc
    from concourse.bass_utils import run_bass_kernel_spmd as _run

    nc = _bacc.Bacc("TRN2", target_bir_lowering=False, num_devices=1)
    arrays, tensors = {}, {}
    for name in _INS:
        a = _np.ascontiguousarray(inputs[name])
        arrays[f"in_{name}"] = a
        tensors[name] = nc.dram_tensor(f"in_{name}", a.shape, mybir.dt.from_np(a.dtype), kind="ExternalInput").ap()
    out = nc.dram_tensor("out_0", tuple(inputs["x"].shape), F32, kind="ExternalOutput").ap()
    build(nc, tensors, out)
    r = _run(nc, [arrays], core_ids=[0])
    return r.results[0]["out_0"]
```

```python
import concourse.bass as bass
from concourse import mybir

F32, BF16 = mybir.dt.float32, mybir.dt.bfloat16
I32, U32 = mybir.dt.int32, mybir.dt.uint32
ALU, ACT, AX = mybir.AluOpType, mybir.ActivationFunctionType, mybir.AxisListType

P = 128
BIG = 1.0e30
EPS = 1.0e-5
NEG_SLOPE = 0.2




def ceil_div(a, b):
    return -(-a // b)


class Engine:

    def __init__(self, nc, raw, name):
        self.raw, self.sem, self.count, self.waited = raw, nc.alloc_semaphore(name), 0, {}

    def done(self, instruction):
        self.count += 1
        instruction.then_inc(self.sem, 1)
        return (self.sem, self.count)

    def need(self, *marks):
        for mark in marks:
            if mark is None:
                continue
            if isinstance(mark, list):
                self.need(*mark)
                continue
            sem, value = mark
            if self.waited.get(sem.name, 0) < value:
                self.raw.wait_ge(sem, value)
                self.waited[sem.name] = value
        return self.raw


class Landing:

    def __init__(self, nc, name, n=1):
        self.sems, self.counts = [nc.alloc_semaphore(f"{name}{i}") for i in range(n)], [0] * n

    def sent(self, instruction, slot=0):
        self.counts[slot] += 16
        instruction.then_inc(self.sems[slot], 16)
        return (self.sems[slot], self.counts[slot])

    def all(self):
        return [(s, c) for s, c in zip(self.sems, self.counts) if c]


class Arena:

    def __init__(self, nc, nbytes):
        self.words = nbytes // 4
        self.whole = nc.alloc_sbuf_tensor("arena", [P, self.words], F32)
        self.used = 0

    def take(self, *dims, dtype=F32):
        n = 1
        for d in dims:
            n *= d
        size = 2 if dtype == BF16 else 4
        words = ceil_div(n * size, 4)
        words += words % 2
        assert self.used + words <= self.words, (self.used, words, self.words)
        view = self.whole[:, self.used:self.used + words]
        self.used += words
        if dtype != F32:
            view = view.bitcast(dtype)
        view = view[:, 0:n]
        if len(dims) == 2:
            return view.rearrange("p (a b) -> p a b", a=dims[0])
        if len(dims) == 3:
            return view.rearrange("p (a b c) -> p a b c", a=dims[0], b=dims[1])
        return view


def spread(ap, axis, n):
    v = ap.unsqueeze(axis)
    shape = list(v.shape)
    shape[axis] = n
    return v.to_broadcast(shape)


def build(nc, t, out):
    N, D = t["x"].shape
    E = t["src"].shape[0]
    H, HD = t["L0_gnn_al1"].shape
    NT, ET = ceil_div(N, P), ceil_div(E, P)
    NI = ET + NT - 1
    NIC = ceil_div(NI, P)
    LAST = N - (NT - 1) * P
    K = D // P
    ROW = D + H
    G = 4
    NG = ceil_div(NI, G)

    V = Engine(nc, nc.vector, "vector_done")
    S = Engine(nc, nc.scalar, "scalar_done")
    T = Engine(nc, nc.tensor, "tensor_done")
    L = Engine(nc, nc.gpsimd, "gpsimd_done")
    Q = Engine(nc, nc.sync, "sync_done")

    def dram(name, shape, dtype=F32):
        return nc.dram_tensor(name, shape, dtype, kind="Internal").ap()

    def sbuf(name, shape, dtype=F32):
        return nc.alloc_sbuf_tensor(name, shape, dtype)[tuple(slice(None) for _ in shape)]

    bank = [nc.alloc_psum_tensor(f"bank{i}", [P, 512], F32)[:, :] for i in range(8)]
    bank_free = [None] * 8

    x = sbuf("x_nodes", [P, NT, D])
    ident = sbuf("ident", [P, P])
    iota = sbuf("iota_free", [P, P])
    ones = sbuf("ones", [P, P])
    ones16 = sbuf("ones16", [P, P], BF16)
    tri16 = sbuf("tri16", [P, P], BF16)
    iota_item = sbuf("iota_item", [P, 4])
    valid_row = sbuf("valid_row", [P, 1])
    stats = sbuf("ln_stats", [P, NT, 6])
    mean_var = sbuf("ln_mean_var", [P, NT, 2])
    rstd = sbuf("ln_rstd", [P, NT])
    item_tile_row = sbuf("item_tile_row", [1, NI], I32)
    any_f_T = sbuf("any_fence_fwd", [H, P])
    any_b_T = sbuf("any_fence_bwd", [H, P])
    N_COL = E // P + 1
    edge_to_tile = sbuf("edge_to_tile", [P, N_COL])
    edge_to_row = sbuf("edge_to_row", [P, N_COL])
    edge_value = sbuf("edge_value", [P, N_COL])
    sorted_value = sbuf("sorted_value", [P, NI])
    arena = Arena(nc, 165 * 1024)
    item_local = arena.take(NIC * P)
    lane_src = arena.take(NI, dtype=U32)
    fence = arena.take(NI + 1)
    gat_base = arena.used

    constants = Landing(nc, "constants_landed")
    index_dma = Landing(nc, "index_landed")
    x_dma = Landing(nc, "x_landed")

    m_ident0 = L.done(L.raw.memset(ident, 0.0))
    m_ones = L.done(L.raw.memset(ones, 1.0))
    m_ident = L.done(L.need(m_ident0).affine_select(
        out=ident, in_=ident, compare_op=ALU.not_equal, fill=1.0, base=0, pattern=[[-1, P]],
        channel_multiplier=1))
    m_iota = L.done(L.raw.iota(iota, [[1, P]], base=0, channel_multiplier=0,
                               allow_small_or_imprecise_dtypes=True))
    m_iota = L.done(L.raw.iota(iota_item, [[P, 4]], base=0, channel_multiplier=1,
                               allow_small_or_imprecise_dtypes=True))
    m_ones16 = V.done(V.need(m_ones).tensor_copy(ones16, ones))
    m_tri = V.done(V.need(m_iota).tensor_scalar(tri16, iota, iota_item[:, 0:1], None, ALU.is_gt))
    m_valid = V.done(V.raw.tensor_scalar(valid_row, iota_item[:, 0:1], float(LAST), None, ALU.is_lt))
    m_const = [m_ident, m_iota, m_ones16, m_tri, m_valid]

    m_x0 = V.done(V.raw.memset(x[:, NT - 1, :], 0.0))
    half = (NT - 1) // 2
    for a, b in ((0, half), (half, NT - 1)):
        m_x = x_dma.sent(Q.raw.dma_start(
            x[:, a:b, :], t["x"][a * P:b * P, :].rearrange("(t p) d -> p t d", p=P)))
    m_x = x_dma.sent(Q.need(m_x0).dma_start(x[0:LAST, NT - 1, :], t["x"][(NT - 1) * P:N, :]))

    pad_node, pad_far, pad_key = (arena.take(P, dtype=d)[0:1, :] for d in (I32, I32, F32))
    src_rows = dram("src_rows", (ET * P,), I32)
    dst_rows = dram("dst_rows", (ET * P,), I32)
    src_stream = dram("src_stream", (NI * P,), U32)
    key_stream = dram("key_stream", (NI * P + 2,))
    item_tile = dram("item_tile", (NIC * P,), I32)

    m_pad = [V.done(V.raw.memset(pad_node, 0)), V.done(V.raw.memset(pad_far, 1 << 20)),
             V.done(V.raw.memset(pad_key, -5.0))]
    A = S
    n_pad = ET * P - E
    for rows, whole, pad in ((src_rows, t["src"], pad_node), (dst_rows, t["dst"], pad_far)):
        index_dma.sent(A.raw.dma_start(rows[0:E].rearrange("(a b) -> a b", a=16),
                                       whole.rearrange("(a b) -> a b", a=16)))
        m_rows = index_dma.sent(A.need(m_pad).dma_start(rows[E:ET * P].unsqueeze(0),
                                                        pad[:, 0:n_pad]))
    first_i = arena.take(ET, dtype=I32)[0:1, :]
    first_f = arena.take(ET)[0:1, :]
    tile_no = arena.take(ET)[0:1, :]
    with nc.allow_non_contiguous_dma(reason="the first dst of each edge tile"):
        m_rows = index_dma.sent(A.raw.dma_start(first_i, t["dst"][0:(ET - 1) * P + 1:P].unsqueeze(0)))
    m_tile_no = L.done(L.raw.iota(tile_no, [[1, ET]], base=0, channel_multiplier=0,
                                  allow_small_or_imprecise_dtypes=True))
    m = V.done(V.need(m_rows).tensor_scalar(first_i, first_i, 7, None, ALU.arith_shift_right))
    m = V.done(V.need(m).tensor_copy(first_f, first_i))
    m = V.done(V.need(m, m_tile_no).tensor_tensor(first_f, first_f, tile_no, ALU.add))
    m_bc = T.done(T.need(m, m_ones).matmul(bank[0][:, 0:ET], ones[0:1, :], first_f, start=True, stop=True))
    before = arena.take(NIC, ET)
    edge_tile = arena.take(NIC)
    node_tile = arena.take(NIC)
    minus_base = arena.take(NIC)
    edge_tile_u = arena.take(NIC, dtype=U32)
    node_tile_i = arena.take(NIC, dtype=I32)
    for c in range(NIC):
        m = V.done(V.need(m_bc, m_iota).tensor_scalar(before[:, c, :], bank[0][:, 0:ET],
                                                      iota_item[:, c:c + 1], None, ALU.is_le))
    bank_free[0] = m
    m = V.done(V.need(m).tensor_reduce(edge_tile, before, AX.X, ALU.add))
    m = V.done(V.need(m).tensor_scalar(edge_tile, edge_tile, -1.0, None, ALU.add))
    m_eu = V.done(V.need(m).tensor_copy(edge_tile_u, edge_tile))
    m = V.done(V.raw.tensor_tensor(node_tile, iota_item[:, 0:NIC], edge_tile, ALU.subtract))
    m_nb = V.done(V.need(m).tensor_scalar(minus_base, node_tile, -float(P), None, ALU.mult))
    m_ni = V.done(V.raw.tensor_copy(node_tile_i, node_tile))
    with nc.allow_non_contiguous_dma(reason="one word per item"):
        m_it = index_dma.sent(Q.need(m_ni).dma_start(item_tile.rearrange("(c p) -> p c", p=P), node_tile_i))
        m_item_row = index_dma.sent(Q.need(m_it, m_rows).dma_start(item_tile_row, item_tile[0:NI].unsqueeze(0)))

    src_i = arena.take(NIC, P, dtype=U32)
    dst_i = arena.take(NIC, P, dtype=I32)
    gather_dma = Landing(nc, "item_rows_landed")
    for c in range(NIC):
        for rows, into in ((src_rows, src_i), (dst_rows, dst_i)):
            m_rows_in = gather_dma.sent(L.need(m_eu, m_rows, m_item_row).indirect_dma_start(
                out=into[:, c, :].bitcast(I32), out_offset=None, in_=rows.rearrange("(a b) -> a b", b=P),
                in_offset=bass.IndirectOffsetOnAxis(ap=edge_tile_u[:, c:c + 1], axis=0)))
    dst_f = arena.take(NIC, P)
    local = arena.take(NIC, P)
    inside = arena.take(NIC, P)
    m_df = V.done(V.need(m_rows_in).tensor_copy(dst_f, dst_i))
    for c in range(NIC):
        m = V.done(V.need(m_df, m_nb).tensor_scalar(local[:, c, :], dst_f[:, c, :],
                                                    minus_base[:, c:c + 1], None, ALU.add))
    m_local = m
    m = V.done(V.need(m).tensor_scalar(inside, local, 0.0, None, ALU.is_ge))
    m = V.done(V.need(m).scalar_tensor_tensor(inside, local, float(P), inside, ALU.is_lt, ALU.mult))
    m = V.done(V.need(m).scalar_tensor_tensor(dst_f, dst_f, 1.0, inside, ALU.add, ALU.mult))
    m_key = V.done(V.need(m).tensor_scalar(dst_f, dst_f, -1.0, None, ALU.add))
    stream_dma = Landing(nc, "stream_written")
    for c in range(NIC):
        n = min(P, NI - c * P)
        m_st = stream_dma.sent(Q.need(m_rows_in).dma_start(
            src_stream[c * P * P:(c * P + n) * P].rearrange("(a b) -> a b", b=P), src_i[0:n, c, :]))
        m_st = stream_dma.sent(Q.need(m_key).dma_start(
            key_stream[1 + c * P * P:1 + (c * P + n) * P].rearrange("(a b) -> a b", b=P), dst_f[0:n, c, :]))
    m_st = stream_dma.sent(Q.need(m_pad).dma_start(key_stream[0:1].unsqueeze(0), pad_key[:, 0:1]))
    m_st = stream_dma.sent(Q.raw.dma_start(key_stream[NI * P + 1:NI * P + 2].unsqueeze(0), pad_key[:, 1:2]))
    keys = arena.take(NI + 2)
    lane_dma = Landing(nc, "lanes_landed")
    lane_dma.sent(Q.need(m_st).dma_start(lane_src, src_stream.rearrange("(p c) -> p c", p=P)))
    with nc.allow_non_contiguous_dma(reason="the neighbours of each lane's ends"):
        for at in (0, 1, 2):
            view = key_stream[at:at + NI * P].rearrange("(p c) -> p c", p=P)
            lo, hi = ((0, 1), (0, NI), (NI - 1, NI))[at]
            m_lane = lane_dma.sent(Q.raw.dma_start(keys[:, at + lo:at + hi], view[:, lo:hi]))
    m = V.done(V.need(m_lane).tensor_tensor(fence, keys[:, 1:NI + 2], keys[:, 0:NI + 1], ALU.not_equal))
    m_fence = V.done(V.need(m).tensor_scalar(fence, fence, -BIG, None, ALU.mult))
    any_f, any_b = arena.take(1), arena.take(1)
    V.done(V.need(m_fence).tensor_reduce(any_f, fence[:, 0:NI], AX.X, ALU.min))
    m = V.done(V.raw.tensor_reduce(any_b, fence[:, 1:NI + 1], AX.X, ALU.min))
    rep = arena.take(2, H)
    V.done(V.need(m).tensor_copy(rep[:, 0, :], any_f.to_broadcast([P, H])))
    m = V.done(V.raw.tensor_copy(rep[:, 1, :], any_b.to_broadcast([P, H])))
    T.need(m, m_ident).transpose(bank[1][0:H, 0:P], rep[:, 0, :], ident)
    m = T.done(T.raw.transpose(bank[1][0:H, P:2 * P], rep[:, 1, :], ident))
    V.done(V.need(m).tensor_copy(any_f_T, bank[1][0:H, 0:P]))
    m_any = V.done(V.raw.tensor_copy(any_b_T, bank[1][0:H, P:2 * P]))
    bank_free[1] = m_any
    for c in range(NIC):
        mt = T.done(T.need(m_local, m_ident).transpose(bank[2][:, c * P:(c + 1) * P], local[:, c, :], ident))
    m_item_local = V.done(V.need(mt).tensor_copy(item_local, bank[2][:, 0:NIC * P]))
    bank_free[2] = m_item_local
    m_items = [m_item_local, m_fence, m_any, m_lane, m_item_row]

    E0, F0 = t["L0_ffn_b1p"].shape
    E1, F1 = t["L1_ffn_b1"].shape
    max_tiles = [(2 * N + e * (P - 1)) // P for e in (E0, E1)]

    def ln_stats(m_in):
        for j in range(NT):
            m = V.done(V.need(m_in if not isinstance(m_in, dict) else m_in[j]).bn_stats(stats[:, j, :], x[:, j, :]))
        V.need(m)
        for j in range(NT):
            m = V.done(V.raw.bn_aggr(mean_var[:, j, :], stats[:, j, :]))
        m = V.done(V.need(m).tensor_scalar(rstd, mean_var[:, :, 1], EPS, None, ALU.add))
        m = S.done(S.need(m).activation(rstd, rstd, ACT.Sqrt))
        return V.done(V.need(m).reciprocal(rstd, rstd))

    def ln_rows(into, j, m_stats, m_free=None):
        return V.done(V.need(m_stats, m_free).tensor_scalar(
            into, x[:, j, :], mean_var[:, j, 0:1], rstd[:, j:j + 1], ALU.subtract, ALU.mult))

    class Buckets:

        def __init__(self, member, groups, n, prefix, work, small, banks):
            self.member, self.groups, self.n, self.prefix, self.banks = member, groups, n, prefix, banks
            self.chunk = 512 // n
            self.chunks = [(a, min(groups, a + self.chunk)) for a in range(0, groups, self.chunk)]
            self.work, self.small, self.free = work, small, {}

        def totals(self, q, m_member):
            a, b = self.chunks[q]
            bk = self.banks[q % 2]
            m = T.done(T.need(m_member, bank_free[bk]).matmul(
                bank[bk][:, 0:(b - a) * self.n], ones16,
                self.member[:, a:b, :].rearrange("p g b -> p (g b)"), start=True, stop=True))
            by_bucket = self.prefix[:, 1:1 + self.groups * self.n].rearrange("p (b g) -> p b g", b=self.n)
            self.m = V.done(V.need(m).tensor_copy(
                by_bucket[:, :, a:b], bank[bk][:, 0:(b - a) * self.n].rearrange("p (g b) -> p b g", b=self.n)))
            bank_free[bk] = self.m

        def scan(self):
            g, n, s, pre = self.groups, self.n, self.small, self.prefix
            m0 = V.done(V.raw.memset(pre[:, 0:1], 0.0))
            run = pre[:, 1:1 + g * n]
            m = V.done(V.need(self.m, m0).tensor_tensor_scan(run, run, run, 0.0, ALU.add, ALU.max))
            first = pre[:, 0:g * n].rearrange("p (b g) -> p b g", b=n)[:, :, 0]
            last = run.rearrange("p (b g) -> p b g", b=n)[:, :, g - 1]
            padded, self.end, shift, whole = s[:, 0, :], s[:, 1, :], s[:, 2, :], s[:, 3, :].bitcast(I32)
            m = V.done(V.need(m).tensor_tensor(padded, last, first, ALU.subtract))
            m = V.done(V.need(m).tensor_scalar(padded, padded, float(P - 1), None, ALU.add))
            m = V.done(V.need(m).tensor_copy(whole, padded))
            m = V.done(V.need(m).tensor_scalar(whole, whole, 7, 7, ALU.arith_shift_right, ALU.logical_shift_left))
            m = V.done(V.need(m).tensor_copy(padded, whole))
            m = V.done(V.need(m).tensor_tensor_scan(self.end, padded, padded, 0.0, ALU.add, ALU.max))
            m = V.done(V.need(m).tensor_tensor(shift, self.end, padded, ALU.subtract))
            m = V.done(V.need(m).tensor_tensor(shift, shift, first, ALU.subtract))
            base = pre[:, 0:g * n].rearrange("p (b g) -> p b g", b=n)
            self.m = V.done(V.need(m).tensor_tensor(base, base, spread(shift, 2, g), ALU.add))

        def positions(self, q, to):
            a, b = self.chunks[q]
            bk = self.banks[q % 2]
            m = T.done(T.need(bank_free[bk]).matmul(
                bank[bk][:, 0:(b - a) * self.n], tri16,
                self.member[:, a:b, :].rearrange("p g b -> p (g b)"), start=True, stop=True))
            base = self.prefix[:, 0:self.groups * self.n].rearrange("p (b g) -> p g b", b=self.n)[:, a:b, :]
            w = self.work[:, q % 2, 0:(b - a) * self.n].rearrange("p (g b) -> p g b", b=self.n)
            m = V.done(V.need(m, self.m, self.free.get(q % 2)).tensor_tensor(
                w, bank[bk][:, 0:(b - a) * self.n].rearrange("p (g b) -> p g b", b=self.n), base, ALU.add))
            bank_free[bk] = m
            m = V.done(V.need(m).tensor_tensor(w, w, self.member[:, a:b, :], ALU.mult))
            self.m_pos = self.free[q % 2] = V.done(V.need(m).tensor_reduce(to[:, a:b], w, AX.X, ALU.add))

        def tile_row(self, n_tiles, compare, tiles_f, tiles_i, dram_row, row, landing):
            cols = ceil_div(n_tiles, P)
            m = V.done(V.need(m_iota).tensor_scalar(tiles_f, iota_item[:, 0:cols], float(P), None, ALU.mult))
            m = V.done(V.need(m, self.m).tensor_tensor(
                compare, spread(self.end, 1, cols), spread(tiles_f, 2, self.n), ALU.is_le))
            m = V.done(V.need(m).tensor_reduce(tiles_f, compare, AX.X, ALU.add))
            m = V.done(V.need(m).tensor_scalar(tiles_f, tiles_f, float(self.n - 1), None, ALU.min))
            m = V.done(V.need(m).tensor_copy(tiles_i, tiles_f))
            with nc.allow_non_contiguous_dma(reason="one word per tile"):
                m = landing.sent(Q.need(m).dma_start(dram_row.rearrange("(c p) -> p c", p=P), tiles_i))
            return landing.sent(Q.need(m).dma_start(row, dram_row[0:n_tiles].unsqueeze(0)))


    arena.used = gat_base
    spill = dram("spilled_features", (NI * P, D))
    er_slots = dram("er_slots", (NI * P, H))
    w_slots = dram("w_slots", (NI * P, H))
    tables = [dram(f"table{n}", (N, ROW)) for n in range(2)]
    hidden = arena.take(NT, D)
    acc = arena.take(NT, ROW)
    fwd = arena.take(H, NI)
    top = arena.take(H, NI)
    after_idle = arena.used
    el = arena.take(H, NI)
    er_lane = arena.take(NI, H)
    per_item = arena.take(NI, H)
    ring = arena.take(4 * G, ROW)
    ring_b = ring.rearrange("p a b -> p (a b)")[:, 0:4 * G * D].rearrange("p (a b) -> p a b", b=D)
    messages_at = arena.used
    messages = arena.take(2 * G, ROW)
    after_messages, arena.used = arena.used, messages_at
    a_rows = arena.take(2, D)
    a_prod = arena.take(K, D)
    rows_in = arena.take(2, D)
    rows_T = arena.take(2, K * P)
    assert arena.used <= after_messages
    arena.used = after_messages
    one_hot = arena.take(2 * G, P)
    one_hot_T = arena.take(2 * G, P)
    w_ext = arena.take(K, D + 2 * H)
    bias = arena.take(D)
    er_nodes = arena.take(NT, H)
    feats = arena.take(3, ROW)
    r_den = arena.take(NT, H)
    carry = arena.take(H)
    carry_T = arena.take(P + 1)
    carry_back = arena.take(H)

    table_dma = Landing(nc, "table_rows_written", 3)
    weight_dma = Landing(nc, "gat_weights_landed")
    gathered = Landing(nc, "rows_gathered", 4)
    spilled = Landing(nc, "rows_spilled", 4)
    slot_dma = Landing(nc, "slots_moved")
    back_dma = Landing(nc, "features_back", 4)
    er_dma = Landing(nc, "er_slots_written")

    tile_regs_v = [nc.vector.alloc_register(f"node_tile_v{i}") for i in range(G)]
    tile_regs_t = [nc.tensor.alloc_register(f"node_tile_t{i}") for i in range(G)]
    free = {}

    def gat(layer, W, al, ar, b, rows_of, before_slots, background):
        Q.need(before_slots)
        weight_dma.sent(Q.raw.dma_start(w_ext[:, :, 0:D], W.rearrange("(k p) n -> p k n", p=P)))
        for n, a in ((0, al), (1, ar)):
            weight_dma.sent(Q.raw.dma_start(a_rows[:, n, :], a.rearrange("h d -> (h d)").partition_broadcast(P)))
        m_w = weight_dma.sent(Q.raw.dma_start(bias, b.partition_broadcast(P)))
        for n in range(2):
            m = V.done(V.need(m_w, before_slots).tensor_tensor(a_prod, w_ext[:, :, 0:D],
                                                               spread(a_rows[:, n, :], 1, K), ALU.mult))
            m_wext = V.done(V.need(m).tensor_reduce(
                w_ext[:, :, D + n * H:D + (n + 1) * H],
                a_prod.rearrange("p k (h d) -> p k h d", h=H), AX.X, ALU.add))
            V.need(m_wext)
        def feat_transpose(j):
            rows, m_rows = rows_of(j)
            tb = bank[j % 2]
            for k in range(K):
                m = T.done(T.need(m_rows, bank_free[j % 2]).transpose(tb[:, k * P:(k + 1) * P],
                                                                      rows[:, k * P:(k + 1) * P], ident))
            free[("rows", j % 2)] = m
            m = S.done(S.need(m, free.get(("rows_T", j % 2))).activation(rows_T[:, j % 2, :], tb[:, 0:K * P], ACT.Copy))
            bank_free[j % 2] = m_rows_T[j] = m

        def feat_product(j):
            fb = bank[2 + j % 2]
            for k in range(K):
                m2 = T.done(T.need(m_rows_T[j], m_wext, bank_free[2 + j % 2]).matmul(
                    fb[:, 0:D + 2 * H], rows_T[:, j % 2, k * P:(k + 1) * P], w_ext[:, k, :],
                    start=(k == 0), stop=(k == K - 1)))
            free[("rows_T", j % 2)] = m2
            V.need(m2, free.get(("feats", j % 3)))
            m3 = V.done(V.raw.tensor_copy(feats[:, j % 3, :], fb[:, 0:ROW]))
            m4 = V.done(V.raw.tensor_copy(er_nodes[:, j, :], fb[:, ROW:ROW + H]))
            bank_free[2 + j % 2] = m4
            n = P if j < NT - 1 else LAST
            free[("feats", j % 3)] = table_dma.sent(Q.need(m3).dma_start(
                tables[layer][j * P:j * P + n, :], feats[0:n, j % 3, :]), j % 3)
            return m4

        m_rows_T = {}
        for j in range(NT + 1):
            if j < NT:
                feat_transpose(j)
            if j:
                m4 = feat_product(j - 1)
        m_er_nodes = m4
        m_table = table_dma.all()

        L.need(m_table)

        def gather_group(g):
            n = min(G, NI - g * G)
            s0 = (g % 4) * G
            for k in range(n):
                c = g * G + k
                m_g = gathered.sent(L.need(m_items, free.get(("ring", g % 4))).indirect_dma_start(
                    out=ring[:, s0 + k, :], out_offset=None, in_=tables[layer],
                    in_offset=bass.IndirectOffsetOnAxis(ap=lane_src[:, c:c + 1], axis=0)), g % 4)
            return m_g

        def keep_group(g, m_g):
            n, s0 = min(G, NI - g * G), (g % 4) * G
            m_el = S.done(S.need(m_g).activation(el[:, :, g * G:g * G + n],
                                                 ring[:, s0:s0 + n, D:ROW].rearrange("p c h -> p h c"), ACT.Copy))
            m_sp = spilled.sent(Q.need(m_g).dma_start(
                spill.rearrange("(p c) d -> p c d", p=P)[:, g * G:g * G + n, :], ring[:, s0:s0 + n, 0:D]), g % 4)
            free[("ring", g % 4)] = [m_el, m_sp]
            return m_el

        def er_one_hot(g):
            n, half, tb = min(G, NI - g * G), (g % 2) * G, bank[4 + g % 2]
            m_oh = V.done(V.need(m_items, free.get(("one_hot", g % 2))).tensor_tensor(
                one_hot[:, half:half + n, :], spread(iota, 1, n),
                spread(item_local[:, g * G:g * G + n], 2, P), ALU.is_equal))
            for k in range(n):
                m = T.done(T.need(m_oh, bank_free[4 + g % 2]).transpose(
                    tb[:, k * P:(k + 1) * P], one_hot[:, half + k, :], ident))
            free[("one_hot", g % 2)] = marks[("transposed", g)] = m

        def er_turn(g):
            n, half, tb = min(G, NI - g * G), (g % 2) * G, bank[4 + g % 2]
            m = S.done(S.need(marks[("transposed", g)], free.get(("one_hot_T", g % 2))).activation(
                one_hot_T[:, half:half + n, :], tb[:, 0:n * P].rearrange("p (a b) -> p a b", b=P), ACT.Copy))
            bank_free[4 + g % 2] = marks[("turned", g)] = m

        def er_product(g):
            n, half, eb = min(G, NI - g * G), (g % 2) * G, bank[6 + g % 2]
            T.need(m_er_nodes, m_item_row)
            T.raw.reg_load(tile_regs_t[0:n], item_tile_row[:, g * G:g * G + n])
            T.need(marks[("turned", g)], bank_free[6 + g % 2])
            for k in range(n):
                r = T.raw.snap(tile_regs_t[k], min_val=0, max_val=NT - 1)
                m = T.raw.matmul(eb[:, k * H:(k + 1) * H], one_hot_T[:, half + k, :],
                                 er_nodes.rearrange("p a b -> p (a b)")[:, bass.ds(r * H, H)],
                                 start=True, stop=True)
            free[("one_hot_T", g % 2)] = marks[("er", g)] = T.done(m)

        def er_keep(g):
            n, eb = min(G, NI - g * G), bank[6 + g % 2]
            m_ei = V.done(V.need(marks[("er", g)]).tensor_copy(per_item[:, g * G:g * G + n, :],
                                                             eb[:, 0:n * H].rearrange("p (a b) -> p a b", b=H)))
            bank_free[6 + g % 2] = m_ei
            if g % 16 == 15 or g == NG - 1:
                a, b_ = (g // 16) * 16 * G, min(NI, g * G + G)
                marks["er_written"] = er_dma.sent(Q.need(m_ei).dma_start(
                    er_slots[a * P:b_ * P, :].rearrange("(i p) h -> p i h", p=P), per_item[:, a:b_, :]))

        marks, m_gathered = {}, {}
        for g in range(NG + 3):
            if g < NG:
                m_gathered[g] = gather_group(g)
                er_one_hot(g)
            if 1 <= g < NG + 1:
                er_turn(g - 1)
            if 2 <= g < NG + 2:
                er_product(g - 2)
                m_el = keep_group(g - 2, m_gathered[g - 2])
            if g >= 3:
                er_keep(g - 3)
            if g < NG:
                background(g)
        m_es = marks["er_written"]
        m_el_all, m_spilled = m_el, spilled.all()
        m_er = slot_dma.sent(Q.need(m_es).dma_start(er_lane, er_slots.rearrange("(p c) h -> p c h", p=P)))

        def scan(to, data, mask, start, backwards):
            for h in range(H):
                o, d, f = to[:, h, :], data[:, h, :], mask
                if backwards:
                    o, d, f = o[:, ::-1], d[:, ::-1], f[:, ::-1]
                m = V.done(V.raw.tensor_tensor_scan(o, f, d, start if start.__class__ is float else start[:, h:h + 1],
                                                    ALU.add, ALU.max))
            return m

        def carry_in(ends, any_T, backwards, m):
            m = V.done(V.need(m).tensor_copy(carry, ends))
            m = T.done(T.need(m, bank_free[0]).transpose(bank[0][0:H, 0:P], carry, ident))
            m2 = V.done(V.raw.memset(carry_T[0:H, :], -BIG))
            o, f, d = (carry_T[0:H, 0:P], any_T, bank[0][0:H, 0:P]) if backwards else (
                carry_T[0:H, 1:P + 1], any_T, bank[0][0:H, 0:P])
            if backwards:
                o, f, d = o[:, ::-1], f[:, ::-1], d[:, ::-1]
            m = V.done(V.need(m, m2).tensor_tensor_scan(o, f, d, -BIG, ALU.add, ALU.max))
            at = 1 if backwards else 0
            m = T.done(T.need(m).transpose(bank[0][:, P:P + H], carry_T[0:H, at:at + P], ident[0:H, 0:H]))
            m = V.done(V.need(m).tensor_copy(carry_back, bank[0][:, P:P + H]))
            bank_free[0] = m
            return m

        V.need(m_el_all)
        m = scan(fwd, el, fence[:, 0:NI], -BIG, False)
        m = carry_in(fwd[:, :, NI - 1], any_f_T, False, m)
        V.need(m)
        m = scan(fwd, el, fence[:, 0:NI], carry_back, False)
        V.need(m)
        m = scan(top, fwd, fence[:, 1:NI + 1], -BIG, True)
        m = carry_in(top[:, :, 0], any_b_T, True, m)
        V.need(m)
        m = scan(top, fwd, fence[:, 1:NI + 1], carry_back, True)
        er_hc = er_lane.rearrange("p c h -> p h c")
        V.done(V.need(m, m_er).tensor_tensor(el, el, er_hc, ALU.add))
        m = V.done(V.raw.tensor_tensor(top, top, er_hc, ALU.add))
        V.done(V.need(m).scalar_tensor_tensor(el, el, NEG_SLOPE, el, ALU.mult, ALU.max))
        m = V.done(V.raw.scalar_tensor_tensor(top, top, NEG_SLOPE, top, ALU.mult, ALU.max))
        m = V.done(V.need(m).tensor_tensor(el, el, top, ALU.subtract))
        m = S.done(S.need(m).activation(er_lane.rearrange("p c h -> p h c"), el, ACT.Exp))
        m = slot_dma.sent(Q.need(m).dma_start(w_slots.rearrange("(p c) h -> p c h", p=P), er_lane))
        m_w_items, m_w_slots, CH = {}, [m, m_er], 64

        def load_weights(i):
            a, b_ = i * CH, min(NI, (i + 1) * CH)
            m_w_items[i] = w_dma[i].sent(Q.need(m_w_slots).dma_start(
                per_item[:, a:b_, :], w_slots[a * P:b_ * P, :].rearrange("(i p) h -> p i h", p=P)))

        m_acc = V.done(V.raw.memset(acc, 0.0))
        acc_flat = acc.rearrange("p a b -> p (a b)")
        Q.need(m_spilled, m_el_all)

        def load_features(g):
            n, s0 = min(G, NI - g * G), (g % 4) * G
            marks[("features", g)] = back_dma.sent(Q.need(free.get(("ring", g % 4))).dma_start(
                ring_b[:, s0:s0 + n, :], spill[g * G * P:(g * G + n) * P, :].rearrange("(i p) d -> p i d", p=P)), g % 4)

        def make_messages(g):
            n, s0, half = min(G, NI - g * G), (g % 4) * G, (g % 2) * G
            w_g = per_item[:, g * G:g * G + n, :]
            m_wi = m_w_items[(g * G) // CH]
            msg = messages[:, half:half + n, :]
            m1 = L.done(L.need(marks[("features", g)], m_wi, free.get(("messages", g % 2))).tensor_tensor(
                msg[:, :, 0:D].rearrange("p i (h d) -> p i h d", h=H),
                ring_b[:, s0:s0 + n, :].rearrange("p i (h d) -> p i h d", h=H),
                spread(w_g, 3, HD), ALU.mult))
            free[("ring", g % 4)] = m1
            m2 = S.done(S.need(m_wi, free.get(("messages", g % 2))).activation(msg[:, :, D:ROW], w_g, ACT.Copy))
            m_oh = V.done(V.need(free.get(("one_hot", g % 2))).tensor_tensor(
                one_hot[:, half:half + n, :], spread(iota, 1, n),
                spread(item_local[:, g * G:g * G + n], 2, P), ALU.is_equal))
            for k in range(n):
                ob = (g * G + k) % 8
                m = T.done(T.need(m1, m2, m_oh, bank_free[ob]).matmul(
                    bank[ob][:, 0:ROW], one_hot[:, half + k, :], messages[:, half + k, :], start=True, stop=True))
                marks[("sum", g, k)] = m
            free[("one_hot", g % 2)] = free[("messages", g % 2)] = m

        def add_sums(g, m_acc):
            n = min(G, NI - g * G)
            V.raw.reg_load(tile_regs_v[0:n], item_tile_row[:, g * G:g * G + n])
            for k in range(n):
                ob = (g * G + k) % 8
                r = V.raw.snap(tile_regs_v[k], min_val=0, max_val=NT - 1)
                V.need(marks[("sum", g, k)], m_acc)
                at = bass.ds(r * ROW, ROW)
                m_acc = V.done(V.raw.tensor_tensor(acc_flat[:, at], acc_flat[:, at], bank[ob][:, 0:ROW], ALU.add))
                bank_free[ob] = m_acc
            return m_acc

        for g in range(3):
            load_features(g)
        load_weights(0)
        for g in range(NG + 1):
            if g % (CH // G) == 2 and g // (CH // G) + 1 < len(w_dma):
                load_weights(g // (CH // G) + 1)
            if g + 3 < NG:
                load_features(g + 3)
            if g < NG:
                make_messages(g)
            if g:
                m_acc = add_sums(g - 1, m_acc)
        m = V.done(V.need(m_acc).tensor_scalar(r_den, acc[:, :, D:ROW], 1e-30, None, ALU.max))
        m = V.done(V.need(m).reciprocal(r_den, r_den))
        V.need(m)
        marks = {}
        for j in range(NT):
            m = V.done(V.raw.tensor_tensor(hidden[:, j, :].rearrange("p (h d) -> p h d", h=H),
                                           acc[:, j, 0:D].rearrange("p (h d) -> p h d", h=H),
                                           spread(r_den[:, j, :], 2, HD), ALU.mult))
            m = V.done(V.need(m).tensor_tensor(hidden[:, j, :], hidden[:, j, :], bias, ALU.add))
            marks[j] = S.done(S.need(m).activation(hidden[:, j, :], hidden[:, j, :], ACT.Relu))
        return marks

    w_dma = [Landing(nc, f"w_items_landed{i}_") for i in range(ceil_div(NI, 64))]

    m_ln = ln_stats([m_x, m_x0])

    def ln_tile(j):
        return rows_in[:, j % 2, :], ln_rows(rows_in[:, j % 2, :], j, m_ln, free.get(("rows", j % 2)))


    keep = arena.used
    arena.used = gat_base
    sort_member = arena.take(N_COL, NT, dtype=BF16)
    sort_prefix = arena.take(N_COL * NT + 1)
    sort_work = arena.take(2, 512)
    sort_small = arena.take(4, NT)
    sort_src = arena.take(N_COL, dtype=I32)
    sort_dst = arena.take(N_COL, dtype=I32)
    sort_local = arena.take(N_COL, dtype=I32)
    sort_tile = arena.take(N_COL)
    sort_pos = arena.take(N_COL)
    sort_void = arena.take(N_COL)
    sort_cmp = arena.take(NIC, NT)
    sort_tiles_f = arena.take(NIC)
    sort_tiles_i = arena.take(NIC, dtype=I32)
    assert arena.used <= after_idle
    arena.used = keep
    sorted_tile_row = sbuf("sorted_tile_row", [1, NI], I32)
    sorted_tile = dram("sorted_tile", (NIC * P,), I32)
    sort_dma = Landing(nc, "sort_landed")
    buckets = Buckets(sort_member, N_COL, NT, sort_prefix, sort_work, sort_small, (0, 1))
    sort = {}

    def split(pos, pos_i, tile, row, m):
        m = V.done(V.need(m).tensor_copy(pos_i, pos))
        m = V.done(V.need(m).tensor_scalar(pos_i, pos_i, 7, None, ALU.arith_shift_right))
        m = V.done(V.need(m).tensor_copy(tile, pos_i))
        return V.done(V.need(m).scalar_tensor_tensor(row, tile, -float(P), pos, ALU.mult, ALU.add))

    def sort_begin():
        full = (N_COL - 1) * P
        m = [V.done(V.raw.memset(sort_src[:, N_COL - 1:N_COL], 1 << 20)),
             V.done(V.raw.memset(sort_dst[:, N_COL - 1:N_COL], 0))]
        Q.need(m, table_dma.all())
        for whole, to in ((t["src"], sort_src), (t["dst"], sort_dst)):
            sort_dma.sent(Q.raw.dma_start(to[:, 0:N_COL - 1], whole[0:full].rearrange("(p c) -> p c", p=P)))
            m_in = sort_dma.sent(Q.raw.dma_start(to[0:E - full, N_COL - 1:N_COL], whole[full:E].unsqueeze(1)))
        m = V.done(V.need(m_in).tensor_scalar(sort_dst, sort_dst, 7, None, ALU.logical_shift_left))
        m2 = V.done(V.raw.tensor_scalar(sort_local, sort_src, P - 1, None, ALU.bitwise_and))
        m = V.done(V.need(m, m2).tensor_tensor(sort_local, sort_local, sort_dst, ALU.bitwise_or))
        m = V.done(V.need(m).tensor_copy(edge_value, sort_local))
        sort["value"] = V.done(V.need(m).tensor_scalar(edge_value, edge_value, 1.0, None, ALU.add))
        m = V.done(V.need(m).tensor_scalar(sort_src, sort_src, 7, None, ALU.arith_shift_right))
        m = V.done(V.need(m).tensor_copy(sort_tile, sort_src))
        sort["m"] = V.done(V.need(m).tensor_scalar(sort_void, sort_tile, float(NT), None, ALU.is_ge))

    def sort_members(a, b):
        sort["m"] = V.done(V.need(sort["m"]).tensor_tensor(
            sort_member[:, a:b, :], spread(iota[:, 0:NT], 1, b - a), spread(sort_tile[:, a:b], 2, NT), ALU.is_equal))

    def sort_end():
        m = V.done(V.need(buckets.m_pos).tensor_tensor(sort_pos, sort_pos, sort_void, ALU.subtract))
        sort["m"] = split(sort_pos, sort_src, edge_to_tile, edge_to_row, m)
        sort["row"] = buckets.tile_row(NI, sort_cmp, sort_tiles_f, sort_tiles_i, sorted_tile, sorted_tile_row, sort_dma)

    sort_todo = [sort_begin]
    for a, b in buckets.chunks:
        sort_todo.append(lambda a=a, b=b: sort_members(a, b))
    for q in range(len(buckets.chunks)):
        sort_todo.append(lambda q=q: buckets.totals(q, sort["m"]))
    sort_todo.append(buckets.scan)
    for q in range(len(buckets.chunks)):
        sort_todo.append(lambda q=q: buckets.positions(q, sort_pos))
    sort_todo.append(sort_end)
    assert len(sort_todo) + 4 <= NG

    def sort_step(g):
        if g >= 4 and sort_todo:
            sort_todo.pop(0)()

    arena.used = gat_base + NT * D + 64
    to_row = arena.take(8, P)
    to_tile = arena.take(8, NI)
    iota_tiles = arena.take(NI)
    assert arena.used <= after_idle
    arena.used = keep
    INV = 3

    def invert_step(g):
        if g == 0:
            sort["iota"] = L.done(L.need(h1[0]).iota(iota_tiles, [[1, NI]], base=0, channel_multiplier=0,
                                                     allow_small_or_imprecise_dtypes=True))
            return
        per = ceil_div(N_COL, NG - 4)
        for c in range((g - 1) * per, min(N_COL, g * per)):
            s = c % 8
            m1 = V.done(V.need(sort["m"], sort["iota"], sort.get(("inv", s))).tensor_scalar(
                to_row[:, s, :], iota, edge_to_row[:, c:c + 1], None, ALU.is_equal))
            m = V.done(V.raw.tensor_scalar(to_tile[:, s, :], iota_tiles, edge_to_tile[:, c:c + 1],
                                           edge_value[:, c:c + 1], ALU.is_equal, ALU.mult))
            sort[("inv", s)] = m = T.done(T.need(m, bank_free[INV]).matmul(
                bank[INV][:, 0:NI], to_row[:, s, :], to_tile[:, s, :], start=(c == 0), stop=(c == N_COL - 1)))
            if c == N_COL - 1:
                sort["sorted"] = bank_free[INV] = V.done(V.need(m).tensor_copy(sorted_value, bank[INV][:, 0:NI]))

    h1 = gat(0, t["L0_gnn_W1"], t["L0_gnn_al1"], t["L0_gnn_ar1"], t["L0_gnn_b1"], ln_tile,
             [m_fence, m_any, m_item_local, m_lane, stream_dma.all(), ], sort_step)
    h2 = gat(1, t["L0_gnn_W2"], t["L0_gnn_al2"], t["L0_gnn_ar2"], t["L0_gnn_b2"],
             lambda j: (hidden[:, j, :], h1[j]), list(h1.values()), invert_step)
    m_x = {}
    for j in range(NT):
        m_x[j] = V.done(V.need(h2[j]).tensor_tensor(x[:, j, :], x[:, j, :], hidden[:, j, :], ALU.add))

    arena.used = 0
    probs_dma = Landing(nc, "router_landed")
    wide_dma = Landing(nc, "expert_weights_landed")
    shared_dma = Landing(nc, "shared_weights_landed")
    wide2_dma = Landing(nc, "expert_weights2_landed")
    token_dma = Landing(nc, "token_rows_written", 4)
    tile_in_dma = Landing(nc, "expert_tile_in", 4)
    tile_out_dma = Landing(nc, "expert_tile_out", 2)
    pick_dma = Landing(nc, "expert_rows_picked", 4)
    misc_dma = Landing(nc, "tile_rows_moved")

    def experts(layer, m_x, n_exp, F, w1_dram, b1_dram, w2_dram, b2_dram, router, router_bias,
                shared, base, w1_ready, act, m_space, finish):
        FC = F // P
        ntiles, expert_out = max_tiles[layer], expert_rows[layer]
        free = {}
        arena.used = base[0]
        w1 = arena.take(n_exp, K, F) if w1_ready is None else w1_ready[0]
        w2_at = arena.used
        w2 = arena.take(n_exp, FC, D)
        w2_end = arena.used
        now_at = arena.used
        w1_now = arena.take(2, K, F)
        if shared:
            arena.used = now_at
            w1s, w2s = arena.take(K, F), arena.take(FC, D)
            b1s = arena.take(FC)
        b1 = arena.take(n_exp, FC)
        b2 = arena.take(D)
        wr = arena.take(K, n_exp)
        mask = arena.take(NT, n_exp + 1)
        mask_T = arena.take(2, P)
        pair_w = arena.take(2, NT)
        pair_at = arena.take(2 * NT, dtype=U32)
        tile_row = arena.take(max(max_tiles), dtype=I32)[0:1, :]
        slot_token = arena.take(max(max_tiles), dtype=U32)
        work_at = arena.used
        rows = arena.take(4, D)
        rows_T = arena.take(2, K, 2 * P)
        hid_s = arena.take(FC, 2 * P) if shared else None
        arena.used = w2_at
        logits = arena.take(NT, n_exp)
        hit = arena.take(2, NT, n_exp)
        probs = arena.take(NT, n_exp)
        tmp = arena.take(NT, n_exp)
        one = arena.take(4, NT)
        member = arena.take(2 * NT, n_exp, dtype=BF16)
        prefix = arena.take(2 * NT * n_exp + 1)
        work = arena.take(2, 512)
        small = arena.take(4, n_exp)
        compare = arena.take(1, n_exp)
        tiles_f, tiles_i = arena.take(1), arena.take(1, dtype=I32)
        pos = arena.take(2 * NT)
        bias_r = arena.take(n_exp)
        pos_i = arena.take(2 * NT, dtype=I32)
        at_tile, at_row = arena.take(2 * NT), arena.take(2 * NT)
        token = arena.take(2, NT)
        to_row = arena.take(2 * NT, P)
        to_tile = arena.take(2 * NT, ntiles)
        assert arena.used <= w2_end

        Q.need(m_space)
        m_wr = probs_dma.sent(Q.raw.dma_start(wr, router.rearrange("(k p) e -> p k e", p=P)))
        probs_dma.sent(Q.raw.dma_start(b2[0:n_exp, :], b2_dram))
        if shared:
            probs_dma.sent(Q.raw.dma_start(b2[n_exp:n_exp + 1, :], shared[3].unsqueeze(0)))
        if router_bias is not None:
            probs_dma.sent(Q.raw.dma_start(bias_r, router_bias.partition_broadcast(P)))
        with nc.allow_non_contiguous_dma(reason="the first biases, one column per 128 units"):
            if shared:
                probs_dma.sent(Q.raw.dma_start(b1s, shared[1].rearrange("(c p) -> p c", p=P)))
            for e in range(n_exp):
                m_wr = probs_dma.sent(Q.raw.dma_start(b1[:, e, :], b1_dram[e].rearrange("(c p) -> p c", p=P)))
        if shared:
            shared_dma.sent(Q.raw.dma_start(w1s, shared[0].rearrange("(k p) f -> p k f", p=P)))
            m_ws = shared_dma.sent(Q.raw.dma_start(w2s, shared[2].rearrange("(c p) d -> p c d", p=P)))
        if w1_ready is None:
            for e in range(n_exp):
                m_w1 = wide_dma.sent(Q.raw.dma_start(w1[:, e, :, :], w1_dram[e].rearrange("(k p) f -> p k f", p=P)))
        else:
            m_w1 = w1_ready[1]

        m_ln = ln_stats(m_x)
        lb = 2
        turned = {}
        for j in range(NT + 1):
            if j < NT:
                m = ln_rows(rows[:, j % 4, :], j, [m_ln, m_space], free.get(("rows", j % 4)))
                for k in range(K):
                    m2 = T.done(T.need(m, bank_free[j % 2]).transpose(bank[j % 2][:, k * P:(k + 1) * P],
                                                                      rows[:, j % 4, k * P:(k + 1) * P], ident))
                n = P if j < NT - 1 else LAST
                free[("rows", j % 4)] = [m2, token_dma.sent(Q.need(m).dma_start(
                    token_rows[layer][j * P:j * P + n, :], rows[0:n, j % 4, :]), j % 4)]
                turned[j] = bank_free[j % 2] = S.done(S.need(m2, free.get(("rows_T", j % 2))).activation(
                    rows_T[:, j % 2, :, 0:P], bank[j % 2][:, 0:K * P].rearrange("p (k n) -> p k n", k=K), ACT.Copy))
            if j:
                i = j - 1
                for k in range(K):
                    m = T.done(T.need(turned[i], m_wr, bank_free[lb]).matmul(
                        bank[lb][:, i * n_exp:(i + 1) * n_exp], rows_T[:, i % 2, k, 0:P], wr[:, k, :],
                        start=(k == 0), stop=(k == K - 1)))
                free[("rows_T", i % 2)] = m
        m = V.done(V.need(m, m_space).tensor_copy(logits, bank[lb][:, 0:NT * n_exp].rearrange("p (j e) -> p j e", e=n_exp)))
        bank_free[lb] = m
        if router_bias is not None:
            m = V.done(V.need(m, m_wr).tensor_tensor(logits, logits, spread(bias_r, 1, NT), ALU.add))
        top1, top2, den, s4 = (one[:, i, :] for i in range(4))

        def over(v):
            return spread(v, 2, n_exp)

        if shared:
            m = V.done(V.need(m).tensor_reduce(top1, logits, AX.X, ALU.max))
            m = V.done(V.need(m).tensor_tensor(probs, logits, over(top1), ALU.subtract))
            m = S.done(S.need(m).activation(probs, probs, ACT.Exp))
            m = V.done(V.need(m).tensor_reduce(den, probs, AX.X, ALU.add))
            m = V.done(V.need(m).reciprocal(den, den))
            m = V.done(V.need(m).tensor_tensor(probs, probs, over(den), ALU.mult))
            score = probs
        else:
            score = logits
        m_score = m
        experts_iota = iota[:, 0:n_exp]
        for k, best in ((0, top1), (1, top2)):
            src_ = score if k == 0 else tmp
            m = V.done(V.need(m).tensor_reduce(best, src_, AX.X, ALU.max))
            h_ = hit[:, k, :, :]
            m = V.done(V.need(m).tensor_tensor(h_, src_, over(best), ALU.is_lt))
            m = V.done(V.need(m).scalar_tensor_tensor(h_, h_, float(P), spread(experts_iota, 1, NT), ALU.mult, ALU.add))
            m = V.done(V.need(m).tensor_reduce(s4, h_, AX.X, ALU.min))
            m = V.done(V.need(m).tensor_tensor(h_, spread(experts_iota, 1, NT), over(s4), ALU.is_equal))
            if k == 0:
                m = V.done(V.need(m).scalar_tensor_tensor(tmp, h_, -BIG, score, ALU.mult, ALU.add))
        m_hit = m
        if shared:
            m = V.done(V.need(m).tensor_tensor(den, top1, top2, ALU.add))
            m = V.done(V.need(m).reciprocal(den, den))
            V.done(V.need(m).tensor_tensor(pair_w[:, 0, :], top1, den, ALU.mult))
            m = V.done(V.raw.tensor_tensor(pair_w[:, 1, :], top2, den, ALU.mult))
        else:
            m = V.done(V.need(m).tensor_tensor(top2, top2, top1, ALU.subtract))
            m = S.done(S.need(m).activation(top2, top2, ACT.Exp))
            m = V.done(V.need(m).tensor_scalar(den, top2, 1.0, None, ALU.add))
            m = V.done(V.need(m).reciprocal(pair_w[:, 0, :], den))
            m = V.done(V.need(m).tensor_tensor(pair_w[:, 1, :], top2, pair_w[:, 0, :], ALU.mult))
        for k in range(2):
            m = V.done(V.need(m, m_valid).tensor_scalar(hit[:, k, NT - 1, :], hit[:, k, NT - 1, :],
                                                        valid_row, None, ALU.mult))
        V.need(m)
        m = V.done(V.raw.tensor_copy(member, hit.rearrange("p k j e -> p (k j) e")))
        m_mask = V.done(V.raw.memset(mask, 1.0))
        V.done(V.need(m).tensor_tensor(hit[:, 0, :, :], hit[:, 0, :, :], over(pair_w[:, 0, :]), ALU.mult))
        m2 = V.done(V.raw.tensor_tensor(hit[:, 1, :, :], hit[:, 1, :, :], over(pair_w[:, 1, :]), ALU.mult))
        m_mask = V.done(V.need(m2, m_mask).tensor_tensor(mask[:, :, 0:n_exp], hit[:, 0, :, :], hit[:, 1, :, :], ALU.add))
        bk = Buckets(member, 2 * NT, n_exp, prefix, work, small, (2, 3))
        for q in range(len(bk.chunks)):
            bk.totals(q, m)
        bk.scan()
        for q in range(len(bk.chunks)):
            bk.positions(q, pos)
        m = bk.m_pos
        m_pos = V.done(V.need(m).tensor_copy(pair_at, pos))
        m2 = V.done(V.need(m_valid, m).tensor_scalar(s4[:, 0:1], valid_row, -1.0, None, ALU.add))
        m = m_pos
        for k in range(2):
            at = k * NT + NT - 1
            m = V.done(V.need(m, m2).tensor_tensor(pos[:, at:at + 1], pos[:, at:at + 1], s4[:, 0:1], ALU.add))
        m = split(pos, pos_i, at_tile, at_row, m)
        V.done(V.need(m).tensor_tensor(to_row, spread(iota, 1, 2 * NT), spread(at_row, 2, P), ALU.is_equal))
        m1 = V.done(V.raw.tensor_tensor(to_tile, spread(iota[:, 0:ntiles], 1, 2 * NT), spread(at_tile, 2, ntiles),
                                        ALU.is_equal))
        for k in range(2):
            m2 = V.done(V.raw.tensor_scalar(token[:, k, :], iota[:, 0:NT], float(P), iota_item[:, 0:1], ALU.mult, ALU.add))
        m = V.done(V.need(m1, m2).tensor_tensor(to_tile, to_tile, spread(token.rearrange("p k j -> p (k j)"), 2, ntiles), ALU.mult))
        for q in range(2 * NT):
            mt = T.need(m, bank_free[4]).matmul(bank[4][:, 0:ntiles], to_row[:, q, :], to_tile[:, q, :],
                                                start=(q == 0), stop=(q == 2 * NT - 1))
        mt = T.done(mt)
        m_slots = bank_free[4] = V.done(V.need(mt).tensor_copy(slot_token[:, 0:ntiles], bank[4][:, 0:ntiles]))
        m_row = bk.tile_row(ntiles, compare, tiles_f, tiles_i, misc_row[layer], tile_row[:, 0:ntiles], misc_dma)
        for e in range(n_exp):
            m_w2 = wide2_dma.sent(Q.need(m_row, m_slots, m_mask).dma_start(
                w2[:, e, :, :], w2_dram[e].rearrange("(c p) d -> p c d", p=P)))

        m_tokens = token_dma.all()
        pairs = [list(range(a, min(NT, a + 2))) for a in range(0, NT, 2)] if shared else []
        turned, masks = {}, {}

        def shared_turn(c):
            half = c % 2
            for i, j in enumerate(pairs[c]):
                s = half * 2 + i
                m = ln_rows(rows[:, s, :], j, m_ln, free.get(("rows", s)))
                for k in range(K):
                    m2 = T.done(T.need(m, bank_free[i]).transpose(bank[i][:, k * P:(k + 1) * P],
                                                                  rows[:, s, k * P:(k + 1) * P], ident))
                free[("rows", s)] = m2
                turned[c] = bank_free[i] = S.done(S.need(m2, free.get(("rows_T", half))).activation(
                    rows_T[:, half, :, i * P:(i + 1) * P],
                    bank[i][:, 0:K * P].rearrange("p (k n) -> p k n", k=K), ACT.Copy))

        def shared_first(c):
            half, n = c % 2, len(pairs[c]) * P
            for f in range(FC):
                hb = 2 + f % 4
                for k in range(K):
                    m = T.done(T.need(turned[c], m_ws, bank_free[hb]).matmul(
                        bank[hb][:, 0:n], w1s[:, k, f * P:(f + 1) * P], rows_T[:, half, k, 0:n],
                        start=(k == 0), stop=(k == K - 1)))
                masks[f] = bank_free[hb] = S.done(S.need(m, free.get("hid_s"), m_wr).activation(
                    hid_s[:, f, 0:n], bank[hb][:, 0:n], act, bias=b1s[:, f:f + 1]))
            free[("rows_T", half)] = m

        def shared_mask(c):
            for i, j in enumerate(pairs[c]):
                m = T.done(T.need(m_mask, bank_free[i]).transpose(bank[i][0:n_exp + 1, 0:P], mask[:, j, :], ident))
                masks[("T", i)] = bank_free[i] = S.done(S.need(m, free.get(("mask_T", i))).activation(
                    mask_T[0:n_exp + 1, i, :], bank[i][0:n_exp + 1, 0:P], ACT.Copy))

        def shared_second(c):
            for i, j in enumerate(pairs[c]):
                yb = 6 + i
                T.need(masks[("T", i)], m_wr, bank_free[yb]).matmul(
                    bank[yb][:, 0:D], mask_T[0:n_exp + 1, i, :], b2[0:n_exp + 1, :], start=True, stop=False)
                for f in range(FC):
                    m = T.done(T.need(masks[f]).matmul(bank[yb][:, 0:D], hid_s[:, f, i * P:(i + 1) * P], w2s[:, f, :],
                                                       start=False, stop=(f == FC - 1)))
                free[("mask_T", i)] = m
                m_x[j] = bank_free[yb] = V.done(V.need(m).tensor_tensor(x[:, j, :], x[:, j, :], bank[yb][:, 0:D], ALU.add))
            free["hid_s"] = m

        for c in range(len(pairs)):
            if c == 0:
                shared_turn(0)
            shared_first(c)
            shared_mask(c)
            if c + 1 < len(pairs):
                shared_turn(c + 1)
            shared_second(c)
        m_shared = [free.get("hid_s"), m_tokens, bank_free[0], bank_free[1], m_slots, m_x[NT - 1] if shared else None]

        arena.used = work_at
        tin = arena.take(4, D)
        tin_T = arena.take(2, K, P)
        hid = arena.take(2, FC, P)
        tout = arena.take(2, D)
        bcol = arena.take(2, FC)
        assert arena.used <= arena.words
        pre = ("first_w", layer)
        w1_flat = w1.rearrange("p e k f -> p (e k f)")
        w2_flat = w2.rearrange("p e c d -> p (e c d)")
        b1_flat = b1.rearrange("p e c -> p (e c)")
        m_hid, m_b = {}, {}

        def second(q):
            s = q % 2
            T.need(m_hid[q], m_w2, bank_free[6 + s])
            T.raw.reg_load(exp_t2, tile_row[:, q:q + 1])
            r = T.raw.snap(exp_t2, min_val=0, max_val=n_exp - 1)
            for f in range(FC):
                m = T.raw.matmul(bank[6 + s][:, 0:D], hid[:, s, f, :], w2_flat[:, bass.ds(r * (FC * D) + f * D, D)],
                                 start=(f == 0), stop=(f == FC - 1))
            m = T.done(m)
            free[("hid", s)] = m
            m = V.done(V.need(m, free.get(("tout", s))).tensor_copy(tout[:, s, :], bank[6 + s][:, 0:D]))
            bank_free[6 + s] = m
            free[("tout", s)] = tile_out_dma.sent(Q.need(m).dma_start(expert_out[q * P:(q + 1) * P, :], tout[:, s, :]), s)

        def load(q):
            m_in[q] = tile_in_dma.sent(L.need(m_tokens, m_shared, m_slots, free.get(("tin", q % 4))).indirect_dma_start(
                out=tin[:, q % 4, :], out_offset=None, in_=token_rows[layer],
                in_offset=bass.IndirectOffsetOnAxis(ap=slot_token[:, q:q + 1], axis=0)), q % 4)

        m_in = {}
        for q in range(3):
            load(q)
        S.need(m_shared)
        V.need(m_shared)
        prepared = {}

        def prepare(q):
            s = q % 2
            if q + 3 < ntiles:
                load(q + 3)
            for k in range(K):
                m = T.done(T.need(m_in[q], bank_free[s]).transpose(bank[s][:, k * P:(k + 1) * P],
                                                                   tin[:, q % 4, k * P:(k + 1) * P], ident))
            free[("tin", q % 4)] = m
            V.need(m_w1, m_row, free.get(("w1_now", s)))
            V.raw.reg_load(exp_v, tile_row[:, q:q + 1])
            r = V.raw.snap(exp_v, min_val=0, max_val=n_exp - 1)
            m_now = V.done(V.raw.tensor_copy(w1_now[:, s, :, :].rearrange("p k f -> p (k f)"),
                                             w1_flat[:, bass.ds(r * (K * F), K * F)]))
            bank_free[s] = V.done(V.need(m, free.get(("tin_T", s))).tensor_copy(
                tin_T[:, s, :, :], bank[s][:, 0:K * P].rearrange("p (k n) -> p k n", k=K)))
            S.need(m_row, m_wr, free.get(("bcol", s)))
            S.raw.reg_load(exp_s, tile_row[:, q:q + 1])
            r = S.raw.snap(exp_s, min_val=0, max_val=n_exp - 1)
            m_b = S.done(S.raw.activation(bcol[:, s, :], b1_flat[:, bass.ds(r * FC, FC)], ACT.Copy))
            prepared[q] = ([bank_free[s], m_now], m_b)

        def first(q):
            s, per = q % 2, 4
            m_ready, m_b = prepared[q]
            for f0 in range(0, FC, per):
                hb = 2 + s * 2 + f0 // per
                T.need(m_ready, bank_free[hb])
                for f in range(f0, min(FC, f0 + per)):
                    for k in range(K):
                        m = T.raw.matmul(bank[hb][:, (f - f0) * P:(f - f0 + 1) * P],
                                         w1_now[:, s, k, f * P:(f + 1) * P], tin_T[:, s, k, :],
                                         start=(k == 0), stop=(k == K - 1))
                m = T.done(m)
                for f in range(f0, min(FC, f0 + per)):
                    m2 = S.done(S.need(m, m_b, free.get(("hid", s))).activation(
                        hid[:, s, f, :], bank[hb][:, (f - f0) * P:(f - f0 + 1) * P], act, bias=bcol[:, s, f:f + 1]))
                bank_free[hb] = m2
            free[("tin_T", s)] = free[("w1_now", s)] = m
            m_hid[q] = free[("bcol", s)] = m2

        prepare(0)
        for q in range(ntiles):
            if q + 1 < ntiles:
                prepare(q + 1)
            first(q)
            if q:
                second(q - 1)
        second(ntiles - 1)
        m_tiles = tile_out_dma.all()

        arena.used = base[0]
        picked = arena.take(4, 2, D)
        finish_space = arena.used
        L.need(m_tiles)
        for j in range(NT):
            s = j % 4
            for k in range(2):
                at = k * NT + j
                m = pick_dma.sent(L.need(free.get(("picked", s)), free[("hid", 0)], free[("hid", 1)]).indirect_dma_start(
                    out=picked[:, s, k, :], out_offset=None, in_=expert_out,
                    in_offset=bass.IndirectOffsetOnAxis(ap=pair_at[:, at:at + 1], axis=0)), s)
            free[("picked", s)] = finish(j, m, picked[:, s, :, :], pair_w, mask, mask_T, b2, m_ln, finish_space, m_x)
        return free

    exp_v, exp_t2, exp_s = (e.raw.alloc_register(n) for e, n in ((V, "expert_first"), (T, "expert_second"), (S, "expert_bias")))
    token_rows = [dram(f"token_rows{n}", (N, D)) for n in range(2)]
    expert_rows = [dram(f"expert_rows{n}", (max_tiles[n] * P, D)) for n in range(2)]
    misc_row = [dram(f"expert_of_tile{n}", (P,), I32) for n in range(2)]

    def finish_shared(j, m, rows, pair_w, mask, mask_T, b2, m_ln, space, m_x):
        for k in range(2):
            m = V.done(V.need(m, m_x[j]).scalar_tensor_tensor(
                x[:, j, :], rows[:, k, :], pair_w[:, k, j:j + 1], x[:, j, :], ALU.mult, ALU.add))
        m_x[j] = m
        return m

    m_space0 = [list(h2.values()), list(m_x.values())]
    experts(0, m_x, E0, F0, t["L0_ffn_W1p"], t["L0_ffn_b1p"], t["L0_ffn_W2p"], t["L0_ffn_b2p"], t["L0_ffn_Wr"], None,
            (t["L0_ffn_W1s"], t["L0_ffn_b1s"], t["L0_ffn_W2s"], t["L0_ffn_b2s"]), [0], None, ACT.Gelu,
            m_space0, finish_shared)

    arena.used = 0
    w1_next = arena.take(E1, K, F1)
    next_base = 0
    space = list(m_x.values())
    sums = arena.take(NT, D + 2)
    g_ring = arena.take(16, D + 2)
    g_hot = arena.take(2 * G, P)
    s_dst_i = arena.take(NI, dtype=I32)
    s_dst_f = arena.take(NI)
    s_dst = arena.take(NI, dtype=U32)
    s_loc = arena.take(NI)
    wa = arena.take(2, K, D)
    wT = arena.take(2, K, D)
    b12 = arena.take(2, D)
    n_rows = arena.take(4, D)
    n_T = arena.take(2, K * P)
    means = arena.take(2, D)
    r_cnt = arena.take(NT)
    norm_table = dram("norm_table", (N, D))
    l1_dma = Landing(nc, "second_graph_landed")
    norm_dma = Landing(nc, "norm_rows_written", 4)
    g_dma = Landing(nc, "neighbours_gathered", 4)
    next_dma = Landing(nc, "next_weights_landed")
    Q.need(space)
    for n, name in ((0, "L1_gnn_W1"), (1, "L1_gnn_W2")):
        l1_dma.sent(Q.raw.dma_start(wa[:, n, :, :], t[name].rearrange("(o p) i -> p o i", p=P)))
    for n, name in ((0, "L1_gnn_b1"), (1, "L1_gnn_b2")):
        m_in = l1_dma.sent(Q.raw.dma_start(b12[:, n, :], t[name].partition_broadcast(P)))
    V.need(space)
    m_ln = ln_stats(m_x)
    m = V.done(V.need(m_in).tensor_tensor(b12[:, 0, :], b12[:, 0, :], b12[:, 1, :], ALU.add))
    m_b12 = m
    for n in range(2):
        for o in range(K):
            for i in range(K):
                mt = T.done(T.need(m_in, bank_free[4 + n]).transpose(
                    bank[4 + n][:, (i * K + o) * P:(i * K + o + 1) * P], wa[:, n, o, i * P:(i + 1) * P], ident))
        m_wT = V.done(V.need(mt).tensor_copy(wT[:, n, :, :].rearrange("p i o -> p (i o)"), bank[4 + n][:, 0:K * D]))
        bank_free[4 + n] = m_wT
    m = V.done(V.need(sort["sorted"]).tensor_scalar(s_loc, sorted_value, -1.0, None, ALU.add))
    m = V.done(V.need(m).tensor_copy(s_dst_i, s_loc))
    m = V.done(V.need(m).tensor_scalar(s_dst_i, s_dst_i, 7, None, ALU.arith_shift_right))
    m = V.done(V.need(m).tensor_copy(s_dst_f, s_dst_i))
    m = V.done(V.need(m).tensor_scalar(s_dst_f, s_dst_f, 0.0, None, ALU.max))
    m = V.done(V.need(m).scalar_tensor_tensor(s_loc, s_dst_f, -float(P), s_loc, ALU.mult, ALU.add))
    m_sd = V.done(V.raw.tensor_copy(s_dst, s_dst_f))
    m_own = V.done(V.raw.memset(sums, 0.0))
    m_one = V.done(V.raw.memset(g_ring[:, :, D:D + 2], 1.0))
    lfree, turned = {}, {}
    for j in range(NT):
        s = j % 4
        m = ln_rows(n_rows[:, s, :], j, m_ln, lfree.get(("n_rows", s)))
        n = P if j < NT - 1 else LAST
        lfree[("n_rows", s)] = norm_dma.sent(Q.need(m).dma_start(norm_table[j * P:j * P + n, :], n_rows[0:n, s, :]), s)

    def turn_rows(j, rows, m, name):
        b_ = j % 2
        for k in range(K):
            m = T.done(T.need(m, bank_free[b_]).transpose(bank[b_][:, k * P:(k + 1) * P], rows[:, k * P:(k + 1) * P], ident))
        lfree[name] = m
        turned[j] = bank_free[b_] = S.done(S.need(m, lfree.get(("n_T", b_))).activation(
            n_T[:, b_, :], bank[b_][:, 0:K * P], ACT.Copy))

    def add_product(j, which):
        b_ = j % 2
        for k in range(K):
            m = T.done(T.need(turned[j], m_wT, bank_free[2 + b_]).matmul(
                bank[2 + b_][:, 0:D], n_T[:, b_, k * P:(k + 1) * P], wT[:, which, k, :], start=(k == 0), stop=(k == K - 1)))
        lfree[("n_T", b_)] = m
        m_x[j] = bank_free[2 + b_] = V.done(V.need(m, m_x[j]).tensor_tensor(x[:, j, :], x[:, j, :], bank[2 + b_][:, 0:D], ALU.add))

    def own_product(step):
        j = step // 2
        if step % 2 == 0:
            m = ln_rows(n_rows[:, j % 4, :], j, m_ln, lfree.get(("n_rows", j % 4)))
            turn_rows(j, n_rows[:, j % 4, :], m, ("n_rows", j % 4))
        else:
            add_product(j, 0)
            m_x[j] = V.done(V.need(m_x[j], m_b12).tensor_tensor(x[:, j, :], x[:, j, :], b12[:, 0, :], ALU.add))

    for e in range(E1):
        m_w1n = next_dma.sent(Q.raw.dma_start(w1_next[:, e, :, :], t["L1_ffn_w1"][e].rearrange("(k p) f -> p k f", p=P)))
    L.need(norm_dma.all())
    sums_flat = sums.rearrange("p a b -> p (a b)")
    m_acc = m_own
    for g in range(NG):
        n = min(G, NI - g * G)
        s0, half = (g % 4) * G, (g % 2) * G
        for k in range(n):
            c = g * G + k
            m_g = g_dma.sent(L.need(m_sd, lfree.get(("ring", g % 4)), m_one).indirect_dma_start(
                out=g_ring[:, s0 + k, 0:D], out_offset=None, in_=norm_table,
                in_offset=bass.IndirectOffsetOnAxis(ap=s_dst[:, c:c + 1], axis=0)), g % 4)
        m_oh = V.done(V.need(lfree.get(("hot", g % 2))).tensor_tensor(
            g_hot[:, half:half + n, :], spread(iota, 1, n),
            spread(s_loc[:, g * G:g * G + n], 2, P), ALU.is_equal))
        if g < 2 * NT:
            own_product(g)
        for k in range(n):
            ob = 4 + (g * G + k) % 4
            m = T.done(T.need(m_g, m_oh, m_one, bank_free[ob]).matmul(
                bank[ob][:, 0:D + 2], g_hot[:, half + k, :], g_ring[:, s0 + k, :], start=True, stop=True))
            bank_free[ob] = m
        lfree[("hot", g % 2)] = lfree[("ring", g % 4)] = m
        V.need(sort["row"])
        V.raw.reg_load(tile_regs_v[0:n], sorted_tile_row[:, g * G:g * G + n])
        for k in range(n):
            ob = 4 + (g * G + k) % 4
            r = V.raw.snap(tile_regs_v[k], min_val=0, max_val=NT - 1)
            V.need(bank_free[ob], m_acc)
            at = bass.ds(r * (D + 2), D + 2)
            m_acc = V.done(V.raw.tensor_tensor(sums_flat[:, at], sums_flat[:, at], bank[ob][:, 0:D + 2], ALU.add))
            bank_free[ob] = m_acc
    m = V.done(V.need(m_acc).tensor_scalar(r_cnt, sums[:, :, D], 1.0, None, ALU.max))
    m_rc = V.done(V.need(m).reciprocal(r_cnt, r_cnt))
    for j in range(NT + 1):
        if j < NT:
            b_ = j % 2
            m = V.done(V.need(m_rc, lfree.get(("means", b_))).tensor_scalar(
                means[:, b_, :], sums[:, j, 0:D], r_cnt[:, j:j + 1], None, ALU.mult))
            turn_rows(j, means[:, b_, :], m, ("means", b_))
        if j:
            add_product(j - 1, 1)

    out_dma = Landing(nc, "out_written")
    efree = {}

    def finish_last(j, m, rows, pair_w, mask, mask_T, b2, m_ln, space, m_x):
        if "y" not in efree:
            arena.used = space
            efree["y"] = arena.take(2, D)
            efree["st"] = arena.take(2, 10)
            efree["gb"] = arena.take(2, D)
            for n, name in ((0, "L1_ffn_gamma"), (1, "L1_ffn_beta")):
                efree["m_gb"] = l1_dma.sent(Q.need(m).dma_start(efree["gb"][:, n, :], t[name].partition_broadcast(P)))
        y, st = efree["y"][:, j % 2, :], efree["st"][:, j % 2, :]
        gamma_beta, m_gb = efree["gb"], efree["m_gb"]
        b_ = j % 2
        mt = T.done(T.need(bank_free[b_]).transpose(bank[b_][0:E1, 0:P], mask[:, j, 0:E1], ident))
        mt = S.done(S.need(mt, efree.get(("mask_T", b_))).activation(mask_T[0:E1, b_, :], bank[b_][0:E1, 0:P], ACT.Copy))
        bank_free[b_] = mt
        mt = T.done(T.need(mt, bank_free[2 + b_]).matmul(bank[2 + b_][:, 0:D], mask_T[0:E1, b_, :], b2[0:E1, :],
                                                         start=True, stop=True))
        efree[("mask_T", b_)] = mt
        my = ln_rows(y, j, [m_ln, m], efree.get(("y", b_)))
        my = V.done(V.need(my, mt).tensor_tensor(y, y, bank[2 + b_][:, 0:D], ALU.add))
        bank_free[2 + b_] = my
        for k in range(2):
            my = V.done(V.need(my, m).scalar_tensor_tensor(y, rows[:, k, :], pair_w[:, k, j:j + 1], y, ALU.mult, ALU.add))
        m_free = my
        my = V.done(V.need(my).bn_stats(st[:, 0:6], y))
        my = V.done(V.need(my).bn_aggr(st[:, 6:8], st[:, 0:6]))
        my = V.done(V.need(my).tensor_scalar(st[:, 8:9], st[:, 7:8], EPS, None, ALU.add))
        my = S.done(S.need(my).activation(st[:, 8:9], st[:, 8:9], ACT.Sqrt))
        my = V.done(V.need(my).reciprocal(st[:, 8:9], st[:, 8:9]))
        my = V.done(V.need(my).tensor_scalar(y, y, st[:, 6:7], st[:, 8:9], ALU.subtract, ALU.mult))
        my = V.done(V.need(my, m_gb).tensor_tensor(y, y, gamma_beta[:, 0, :], ALU.mult))
        my = V.done(V.need(my).tensor_tensor(y, y, gamma_beta[:, 1, :], ALU.add))
        efree[("y", b_)] = m_x[j] = V.done(V.need(my, m_x[j]).tensor_tensor(x[:, j, :], x[:, j, :], y, ALU.add))
        n = P if j < NT - 1 else LAST
        out_dma.sent(Q.need(m_x[j]).dma_start(out[j * P:j * P + n, :], x[0:n, j, :]))
        return m_free

    arena.used = 0
    w1_ready = (arena.take(E1, K, F1), m_w1n)
    experts(1, m_x, E1, F1, None, t["L1_ffn_b1"], t["L1_ffn_w2"], t["L1_ffn_b2"], t["L1_ffn_gate_w"],
            t["L1_ffn_gate_b"], None, [arena.used], w1_ready, ACT.Relu,
            list(m_x.values()), finish_last)
    Q.need(out_dma.all())
    return

    out_dma = Landing(nc, "out_written")
    for j in range(NT):
        n = P if j < NT - 1 else LAST
        out_dma.sent(Q.need(m_x[j]).dma_start(out[j * P:j * P + n, :], x[0:n, j, :]))
    Q.need(out_dma.all())


_INS = ['x', 'src', 'dst', 'L0_gnn_W1', 'L0_gnn_al1', 'L0_gnn_ar1', 'L0_gnn_b1', 'L0_gnn_W2', 'L0_gnn_al2',
        'L0_gnn_ar2', 'L0_gnn_b2', 'L0_ffn_Wr', 'L0_ffn_W1s', 'L0_ffn_b1s', 'L0_ffn_W2s', 'L0_ffn_b2s',
        'L0_ffn_W1p', 'L0_ffn_b1p', 'L0_ffn_W2p', 'L0_ffn_b2p', 'L1_gnn_W1', 'L1_gnn_b1', 'L1_gnn_W2',
        'L1_gnn_b2', 'L1_ffn_gate_w', 'L1_ffn_gate_b', 'L1_ffn_w1', 'L1_ffn_b1', 'L1_ffn_w2', 'L1_ffn_b2',
        'L1_ffn_gamma', 'L1_ffn_beta']


def kernel(**inputs):
    import numpy as _np
    import concourse.bacc as _bacc
    from concourse.bass_utils import run_bass_kernel_spmd as _run

    nc = _bacc.Bacc("TRN2", target_bir_lowering=False, num_devices=1)
    arrays, tensors = {}, {}
    for name in _INS:
        a = _np.ascontiguousarray(inputs[name])
        arrays[f"in_{name}"] = a
        tensors[name] = nc.dram_tensor(f"in_{name}", a.shape, mybir.dt.from_np(a.dtype), kind="ExternalInput").ap()
    out = nc.dram_tensor("out_0", tuple(inputs["x"].shape), F32, kind="ExternalOutput").ap()
    build(nc, tensors, out)
    r = _run(nc, [arrays], core_ids=[0])
    return r.results[0]["out_0"]
```

```python
import concourse.bass as bass
from concourse import mybir

F32, BF16 = mybir.dt.float32, mybir.dt.bfloat16
I32, U32 = mybir.dt.int32, mybir.dt.uint32
ALU, ACT, AX = mybir.AluOpType, mybir.ActivationFunctionType, mybir.AxisListType

P = 128
BIG = 1.0e30
EPS = 1.0e-5
NEG_SLOPE = 0.2




def ceil_div(a, b):
    return -(-a // b)


class Engine:

    def __init__(self, nc, raw, name):
        self.raw, self.sem, self.count, self.waited = raw, nc.alloc_semaphore(name), 0, {}

    def done(self, instruction):
        self.count += 1
        instruction.then_inc(self.sem, 1)
        return (self.sem, self.count)

    def after(self, mark, instruction):
        sem, value = mark
        if self.waited.get(sem.name, 0) < value:
            instruction.wait_op(sem, value, "sem-ge")
            self.waited[sem.name] = value
        return instruction

    def need(self, *marks):
        for mark in marks:
            if mark is None:
                continue
            if isinstance(mark, list):
                self.need(*mark)
                continue
            sem, value = mark
            if self.waited.get(sem.name, 0) < value:
                self.raw.wait_ge(sem, value)
                self.waited[sem.name] = value
        return self.raw


class Landing:

    def __init__(self, nc, name, n=1):
        self.sems, self.counts = [nc.alloc_semaphore(f"{name}{i}") for i in range(n)], [0] * n

    def sent(self, instruction, slot=0):
        self.counts[slot] += 16
        instruction.then_inc(self.sems[slot], 16)
        return (self.sems[slot], self.counts[slot])

    def all(self):
        return [(s, c) for s, c in zip(self.sems, self.counts) if c]


class Arena:

    def __init__(self, nc, nbytes):
        self.words = nbytes // 4
        self.whole = nc.alloc_sbuf_tensor("arena", [P, self.words], F32)
        self.used = 0

    def take(self, *dims, dtype=F32):
        n = 1
        for d in dims:
            n *= d
        size = 2 if dtype == BF16 else 4
        words = ceil_div(n * size, 4)
        words += words % 2
        assert self.used + words <= self.words, (self.used, words, self.words)
        view = self.whole[:, self.used:self.used + words]
        self.used += words
        if dtype != F32:
            view = view.bitcast(dtype)
        view = view[:, 0:n]
        if len(dims) == 2:
            return view.rearrange("p (a b) -> p a b", a=dims[0])
        if len(dims) == 3:
            return view.rearrange("p (a b c) -> p a b c", a=dims[0], b=dims[1])
        return view


def spread(ap, axis, n):
    v = ap.unsqueeze(axis)
    shape = list(v.shape)
    shape[axis] = n
    return v.to_broadcast(shape)


def build(nc, t, out):
    N, D = t["x"].shape
    E = t["src"].shape[0]
    H, HD = t["L0_gnn_al1"].shape
    NT, ET = ceil_div(N, P), ceil_div(E, P)
    NI = ET + NT - 1
    NIC = ceil_div(NI, P)
    LAST = N - (NT - 1) * P
    K = D // P
    ROW = D + H
    G = 4
    NG = ceil_div(NI, G)
    CG = 4
    CI = CG * G
    NC = ceil_div(NI, CI)
    RINGS = (12, 16)

    V = Engine(nc, nc.vector, "vector_done")
    S = Engine(nc, nc.scalar, "scalar_done")
    T = Engine(nc, nc.tensor, "tensor_done")
    L = Engine(nc, nc.gpsimd, "gpsimd_done")
    Q = Engine(nc, nc.sync, "sync_done")

    def dram(name, shape, dtype=F32):
        return nc.dram_tensor(name, shape, dtype, kind="Internal").ap()

    def sbuf(name, shape, dtype=F32):
        return nc.alloc_sbuf_tensor(name, shape, dtype)[tuple(slice(None) for _ in shape)]

    bank = [nc.alloc_psum_tensor(f"bank{i}", [P, 512], F32)[:, :] for i in range(8)]
    bank_free = [None] * 8

    x = sbuf("x_nodes", [P, NT, D])
    ident = sbuf("ident", [P, P])
    iota = sbuf("iota_free", [P, P])
    ones = sbuf("ones", [P, P])
    ones16 = sbuf("ones16", [P, P], BF16)
    tri16 = sbuf("tri16", [P, P], BF16)
    iota_item = sbuf("iota_item", [P, 4])
    valid_row = sbuf("valid_row", [P, 1])
    stats = sbuf("ln_stats", [P, NT, 6])
    mean_var = sbuf("ln_mean_var", [P, NT, 2])
    rstd = sbuf("ln_rstd", [P, NT])
    item_tile_row = sbuf("item_tile_row", [1, NI], I32)
    N_COL = E // P + 1
    edge_to_tile = sbuf("edge_to_tile", [P, N_COL])
    edge_to_row = sbuf("edge_to_row", [P, N_COL])
    edge_value = sbuf("edge_value", [P, N_COL])
    sorted_value = sbuf("sorted_value", [P, NI])
    arena = Arena(nc, 168 * 1024)
    item_local = arena.take(NIC * P)
    item_src = arena.take(NIC * P, dtype=U32)
    fence = arena.take(NC, CI + 3)
    any_fence = arena.take(2, NC)
    gat_base = arena.used

    constants = Landing(nc, "constants_landed")
    index_dma = Landing(nc, "index_landed")
    x_dma = Landing(nc, "x_landed")

    m_ident0 = L.done(L.raw.memset(ident, 0.0))
    m_ones = L.done(L.raw.memset(ones, 1.0))
    m_ident = L.done(L.need(m_ident0).affine_select(
        out=ident, in_=ident, compare_op=ALU.not_equal, fill=1.0, base=0, pattern=[[-1, P]],
        channel_multiplier=1))
    m_iota = L.done(L.raw.iota(iota, [[1, P]], base=0, channel_multiplier=0,
                               allow_small_or_imprecise_dtypes=True))
    m_iota = L.done(L.raw.iota(iota_item, [[P, 4]], base=0, channel_multiplier=1,
                               allow_small_or_imprecise_dtypes=True))
    m_ones16 = V.done(V.need(m_ones).tensor_copy(ones16, ones))
    m_tri = V.done(V.need(m_iota).tensor_scalar(tri16, iota, iota_item[:, 0:1], None, ALU.is_gt))
    m_valid = V.done(V.raw.tensor_scalar(valid_row, iota_item[:, 0:1], float(LAST), None, ALU.is_lt))
    m_const = [m_ident, m_iota, m_ones16, m_tri, m_valid]

    m_x0 = V.done(V.raw.memset(x[:, NT - 1, :], 0.0))
    half = (NT - 1) // 2
    for a, b in ((0, half), (half, NT - 1)):
        m_x = x_dma.sent(Q.raw.dma_start(
            x[:, a:b, :], t["x"][a * P:b * P, :].rearrange("(t p) d -> p t d", p=P)))
    m_x = x_dma.sent(Q.need(m_x0).dma_start(x[0:LAST, NT - 1, :], t["x"][(NT - 1) * P:N, :]))

    pad_node, pad_far, pad_key = (arena.take(P, dtype=d)[0:1, :] for d in (I32, I32, F32))
    src_rows = dram("src_rows", (ET * P,), I32)
    dst_rows = dram("dst_rows", (ET * P,), I32)
    key_stream = dram("key_stream", (NI * P + 2,))
    item_tile = dram("item_tile", (NIC * P,), I32)

    m_pad = [V.done(V.raw.memset(pad_node, 0)), V.done(V.raw.memset(pad_far, 1 << 20)),
             V.done(V.raw.memset(pad_key, -5.0))]
    A = S
    n_pad = ET * P - E
    for rows, whole, pad in ((src_rows, t["src"], pad_node), (dst_rows, t["dst"], pad_far)):
        index_dma.sent(A.raw.dma_start(rows[0:E].rearrange("(a b) -> a b", a=16),
                                       whole.rearrange("(a b) -> a b", a=16)))
        m_rows = index_dma.sent(A.need(m_pad).dma_start(rows[E:ET * P].unsqueeze(0),
                                                        pad[:, 0:n_pad]))
    first_i = arena.take(ET, dtype=I32)[0:1, :]
    first_f = arena.take(ET)[0:1, :]
    tile_no = arena.take(ET)[0:1, :]
    with nc.allow_non_contiguous_dma(reason="the first dst of each edge tile"):
        m_rows = index_dma.sent(A.raw.dma_start(first_i, t["dst"][0:(ET - 1) * P + 1:P].unsqueeze(0)))
    m_tile_no = L.done(L.raw.iota(tile_no, [[1, ET]], base=0, channel_multiplier=0,
                                  allow_small_or_imprecise_dtypes=True))
    m = V.done(V.need(m_rows).tensor_scalar(first_i, first_i, 7, None, ALU.arith_shift_right))
    m = V.done(V.need(m).tensor_copy(first_f, first_i))
    m = V.done(V.need(m, m_tile_no).tensor_tensor(first_f, first_f, tile_no, ALU.add))
    m_bc = T.done(T.need(m, m_ones).matmul(bank[0][:, 0:ET], ones[0:1, :], first_f, start=True, stop=True))
    before = arena.take(NIC, ET)
    edge_tile = arena.take(NIC)
    node_tile = arena.take(NIC)
    minus_base = arena.take(NIC)
    edge_tile_u = arena.take(NIC, dtype=U32)
    node_tile_i = arena.take(NIC, dtype=I32)
    for c in range(NIC):
        m = V.done(V.need(m_bc, m_iota).tensor_scalar(before[:, c, :], bank[0][:, 0:ET],
                                                      iota_item[:, c:c + 1], None, ALU.is_le))
    bank_free[0] = m
    m = V.done(V.need(m).tensor_reduce(edge_tile, before, AX.X, ALU.add))
    m = V.done(V.need(m).tensor_scalar(edge_tile, edge_tile, -1.0, None, ALU.add))
    m_eu = V.done(V.need(m).tensor_copy(edge_tile_u, edge_tile))
    m = V.done(V.raw.tensor_tensor(node_tile, iota_item[:, 0:NIC], edge_tile, ALU.subtract))
    m_nb = V.done(V.need(m).tensor_scalar(minus_base, node_tile, -float(P), None, ALU.mult))
    m_ni = V.done(V.raw.tensor_copy(node_tile_i, node_tile))
    with nc.allow_non_contiguous_dma(reason="one word per item"):
        m_it = index_dma.sent(Q.need(m_ni).dma_start(item_tile.rearrange("(c p) -> p c", p=P), node_tile_i))
        m_item_row = index_dma.sent(Q.need(m_it, m_rows).dma_start(item_tile_row, item_tile[0:NI].unsqueeze(0)))

    src_i = arena.take(NIC, P, dtype=U32)
    dst_i = arena.take(NIC, P, dtype=I32)
    gather_dma = Landing(nc, "item_rows_landed")
    for c in range(NIC):
        for rows, into in ((src_rows, src_i), (dst_rows, dst_i)):
            m_rows_in = gather_dma.sent(L.need(m_eu, m_rows, m_item_row).indirect_dma_start(
                out=into[:, c, :].bitcast(I32), out_offset=None, in_=rows.rearrange("(a b) -> a b", b=P),
                in_offset=bass.IndirectOffsetOnAxis(ap=edge_tile_u[:, c:c + 1], axis=0)))
    dst_f = arena.take(NIC, P)
    local = arena.take(NIC, P)
    inside = arena.take(NIC, P)
    m_df = V.done(V.need(m_rows_in).tensor_copy(dst_f, dst_i))
    for c in range(NIC):
        m = V.done(V.need(m_df, m_nb).tensor_scalar(local[:, c, :], dst_f[:, c, :],
                                                    minus_base[:, c:c + 1], None, ALU.add))
    m_local = m
    m = V.done(V.need(m).tensor_scalar(inside, local, 0.0, None, ALU.is_ge))
    m = V.done(V.need(m).scalar_tensor_tensor(inside, local, float(P), inside, ALU.is_lt, ALU.mult))
    m = V.done(V.need(m).scalar_tensor_tensor(dst_f, dst_f, 1.0, inside, ALU.add, ALU.mult))
    m_key = V.done(V.need(m).tensor_scalar(dst_f, dst_f, -1.0, None, ALU.add))
    stream_dma = Landing(nc, "stream_written")
    for c in range(NIC):
        n = min(P, NI - c * P)
        m_st = stream_dma.sent(Q.need(m_key).dma_start(
            key_stream[1 + c * P * P:1 + (c * P + n) * P].rearrange("(a b) -> a b", b=P), dst_f[0:n, c, :]))
    m_st = stream_dma.sent(Q.need(m_pad).dma_start(key_stream[0:1].unsqueeze(0), pad_key[:, 0:1]))
    m_st = stream_dma.sent(Q.raw.dma_start(key_stream[NI * P + 1:NI * P + 2].unsqueeze(0), pad_key[:, 1:2]))
    keys = arena.take(NC, CI + 2)
    m_keys0 = V.done(V.raw.memset(keys, 0.0))
    lane_dma = Landing(nc, "lanes_landed")
    Q.need(m_st, m_keys0)
    with nc.allow_non_contiguous_dma(reason="the neighbours of each lane's ends"):
        for k0, k1, n in ((0, NC - 1, CI), (NC - 1, NC, NI - (NC - 1) * CI)):
            for at, lo, hi in ((0, 0, 1), (1, 0, n), (2, n - 1, n)):
                first = at + k0 * CI * P
                view = key_stream[first:first + (k1 - k0) * n * P].rearrange("(k p c) -> p k c", p=P, c=n)
                m_lane = lane_dma.sent(Q.raw.dma_start(keys[:, k0:k1, at + lo:at + hi], view[:, :, lo:hi]))
    m = V.done(V.raw.memset(fence, 1.0))
    m = V.done(V.need(m_lane, m).tensor_tensor(fence[:, :, 1:CI + 2], keys[:, :, 1:CI + 2], keys[:, :, 0:CI + 1],
                                               ALU.not_equal))
    n_last = NI - (NC - 1) * CI
    m = V.done(V.need(m).memset(fence[:, NC - 1, n_last + 2:n_last + 3], 1.0))
    m = V.done(V.need(m).tensor_scalar(fence, fence, -BIG, None, ALU.mult))
    m_fence = m
    V.need(m_fence)
    for k0, k1, n in ((0, NC - 1, CI), (NC - 1, NC, n_last)):
        V.done(V.raw.tensor_reduce(any_fence[:, 0, k0:k1], fence[:, k0:k1, 1:n + 1], AX.X, ALU.min))
        m_any = V.done(V.raw.tensor_reduce(any_fence[:, 1, k0:k1], fence[:, k0:k1, 2:n + 2], AX.X, ALU.min))
    src_f = arena.take(NIC, P)
    m = V.done(V.need(m_rows_in).tensor_copy(src_f, src_i))
    for c in range(NIC):
        mt = T.done(T.need(m, m_ident).transpose(bank[3][:, c * P:(c + 1) * P], src_f[:, c, :], ident))
    m_src = V.done(V.need(mt).tensor_copy(item_src, bank[3][:, 0:NIC * P]))
    bank_free[3] = m_src
    for c in range(NIC):
        mt = T.done(T.need(m_local, m_ident).transpose(bank[2][:, c * P:(c + 1) * P], local[:, c, :], ident))
    m_item_local = V.done(V.need(mt).tensor_copy(item_local, bank[2][:, 0:NIC * P]))
    bank_free[2] = m_item_local
    m_items = [m_item_local, m_fence, m_any, m_src, m_item_row]

    E0, F0 = t["L0_ffn_b1p"].shape
    E1, F1 = t["L1_ffn_b1"].shape
    max_tiles = [(2 * N + e * (P - 1)) // P for e in (E0, E1)]

    def ln_stats(m_in):
        for j in range(NT):
            m = V.done(V.need(m_in if not isinstance(m_in, dict) else m_in[j]).bn_stats(stats[:, j, :], x[:, j, :]))
        V.need(m)
        for j in range(NT):
            m = V.done(V.raw.bn_aggr(mean_var[:, j, :], stats[:, j, :]))
        m = V.done(V.need(m).tensor_scalar(rstd, mean_var[:, :, 1], EPS, None, ALU.add))
        m = S.done(S.need(m).activation(rstd, rstd, ACT.Sqrt))
        return V.done(V.need(m).reciprocal(rstd, rstd))

    def ln_rows(into, j, m_stats, m_free=None):
        return V.done(V.need(m_stats, m_free).tensor_scalar(
            into, x[:, j, :], mean_var[:, j, 0:1], rstd[:, j:j + 1], ALU.subtract, ALU.mult))

    class Buckets:

        def __init__(self, member, groups, n, prefix, work, small, banks):
            self.member, self.groups, self.n, self.prefix, self.banks = member, groups, n, prefix, banks
            self.chunk = 512 // n
            self.chunks = [(a, min(groups, a + self.chunk)) for a in range(0, groups, self.chunk)]
            self.work, self.small, self.free = work, small, {}

        def totals(self, q, m_member):
            self.totals_product(q, m_member)
            self.totals_kept(q)

        def totals_product(self, q, m_member):
            a, b = self.chunks[q]
            bk = self.banks[q % 2]
            self.m_product = T.done(T.need(m_member, bank_free[bk]).matmul(
                bank[bk][:, 0:(b - a) * self.n], ones16,
                self.member[:, a:b, :].rearrange("p g b -> p (g b)"), start=True, stop=True))

        def totals_kept(self, q):
            a, b = self.chunks[q]
            bk, m = self.banks[q % 2], self.m_product
            by_bucket = self.prefix[:, 1:1 + self.groups * self.n].rearrange("p (b g) -> p b g", b=self.n)
            self.m = V.done(V.need(m).tensor_copy(
                by_bucket[:, :, a:b], bank[bk][:, 0:(b - a) * self.n].rearrange("p (g b) -> p b g", b=self.n)))
            bank_free[bk] = self.m

        def scan(self):
            g, n, s, pre = self.groups, self.n, self.small, self.prefix
            m0 = V.done(V.raw.memset(pre[:, 0:1], 0.0))
            run = pre[:, 1:1 + g * n]
            m = V.done(V.need(self.m, m0).tensor_tensor_scan(run, run, run, 0.0, ALU.add, ALU.max))
            first = pre[:, 0:g * n].rearrange("p (b g) -> p b g", b=n)[:, :, 0]
            last = run.rearrange("p (b g) -> p b g", b=n)[:, :, g - 1]
            padded, self.end, shift, whole = s[:, 0, :], s[:, 1, :], s[:, 2, :], s[:, 3, :].bitcast(I32)
            m = V.done(V.need(m).tensor_tensor(padded, last, first, ALU.subtract))
            m = V.done(V.need(m).tensor_scalar(padded, padded, float(P - 1), None, ALU.add))
            m = V.done(V.need(m).tensor_copy(whole, padded))
            m = V.done(V.need(m).tensor_scalar(whole, whole, 7, 7, ALU.arith_shift_right, ALU.logical_shift_left))
            m = V.done(V.need(m).tensor_copy(padded, whole))
            m = V.done(V.need(m).tensor_tensor_scan(self.end, padded, padded, 0.0, ALU.add, ALU.max))
            m = V.done(V.need(m).tensor_tensor(shift, self.end, padded, ALU.subtract))
            m = V.done(V.need(m).tensor_tensor(shift, shift, first, ALU.subtract))
            base = pre[:, 0:g * n].rearrange("p (b g) -> p b g", b=n)
            self.m = V.done(V.need(m).tensor_tensor(base, base, spread(shift, 2, g), ALU.add))

        def positions(self, q, to):
            self.positions_product(q)
            self.positions_kept(q, to)

        def positions_product(self, q):
            a, b = self.chunks[q]
            bk = self.banks[q % 2]
            self.m_product = T.done(T.need(bank_free[bk]).matmul(
                bank[bk][:, 0:(b - a) * self.n], tri16,
                self.member[:, a:b, :].rearrange("p g b -> p (g b)"), start=True, stop=True))

        def positions_kept(self, q, to):
            a, b = self.chunks[q]
            bk, m = self.banks[q % 2], self.m_product
            base = self.prefix[:, 0:self.groups * self.n].rearrange("p (b g) -> p g b", b=self.n)[:, a:b, :]
            w = self.work[:, q % 2, 0:(b - a) * self.n].rearrange("p (g b) -> p g b", b=self.n)
            m = V.done(V.need(m, self.m, self.free.get(q % 2)).tensor_tensor(
                w, bank[bk][:, 0:(b - a) * self.n].rearrange("p (g b) -> p g b", b=self.n), base, ALU.add))
            bank_free[bk] = m
            m = V.done(V.need(m).tensor_tensor(w, w, self.member[:, a:b, :], ALU.mult))
            self.m_pos = self.free[q % 2] = V.done(V.need(m).tensor_reduce(to[:, a:b], w, AX.X, ALU.add))

        def tile_row(self, n_tiles, compare, tiles_f, tiles_i, dram_row, row, landing):
            cols = ceil_div(n_tiles, P)
            m = V.done(V.need(m_iota).tensor_scalar(tiles_f, iota_item[:, 0:cols], float(P), None, ALU.mult))
            m = V.done(V.need(m, self.m).tensor_tensor(
                compare, spread(self.end, 1, cols), spread(tiles_f, 2, self.n), ALU.is_le))
            m = V.done(V.need(m).tensor_reduce(tiles_f, compare, AX.X, ALU.add))
            m = V.done(V.need(m).tensor_scalar(tiles_f, tiles_f, float(self.n - 1), None, ALU.min))
            m = V.done(V.need(m).tensor_copy(tiles_i, tiles_f))
            with nc.allow_non_contiguous_dma(reason="one word per tile"):
                m = landing.sent(Q.need(m).dma_start(dram_row.rearrange("(c p) -> p c", p=P), tiles_i))
            return landing.sent(Q.need(m).dma_start(row, dram_row[0:n_tiles].unsqueeze(0)))


    arena.used = gat_base
    el_slots = dram("el_slots", (NC * CI * P, H))
    top_slots = dram("top_slots", (NC * CI * P, H))
    tables = [dram(f"table{n}", (N, ROW)) for n in range(2)]
    acc = arena.take(NT, ROW)
    messages_at = arena.used
    messages = arena.take(3 * G, ROW)
    one_hot = arena.take(2 * G, P)
    one_hot_T = arena.take(2 * G, P)
    sum_hot = arena.take(3 * G, P)
    after_messages, arena.used = arena.used, messages_at
    a_rows = arena.take(2, D)
    a_prod = arena.take(K, D)
    rows_in = arena.take(4, D)
    rows_T = arena.take(2, K * P)
    feats = arena.take(3, ROW)
    r_den = arena.take(NT, H)
    assert arena.used <= after_messages
    arena.used = after_messages
    w_ext = arena.take(K, D + 2 * H)
    bias = arena.take(D)
    er_nodes = arena.take(NT, H)
    er_item = arena.take(3 * CI, H)
    w_item = arena.take(2 * CI, H)
    top_item = arena.take(CI, H)
    slot_in = arena.take(CI, H)
    slot_out = arena.take(CI, H)
    el_flat = arena.take(H * (CI + 2))
    fwd_flat = arena.take(H * (CI + 2))
    top_flat = arena.take(H * (CI + 2))
    mask_f_flat = arena.take(H * (CI + 2))
    mask_b_flat = arena.take(H * (CI + 2))
    carry = arena.take(2 * H)
    carry_T = arena.take(P + 1)
    any_T = arena.take(P)
    enters = arena.take(2, H)
    past = arena.take(2)
    seam = arena.take(6, H + 2)
    match = arena.take(2)
    factors = arena.take(2, H)
    ring_at = arena.used
    rings = []
    for groups in RINGS:
        arena.used = ring_at
        rings.append(arena.take(groups * G, ROW))
    hidden = rings[0].rearrange("p a b -> p (a b)")[:, 0:NT * D].rearrange("p (a b) -> p a b", b=D)
    ring_end = [ring_at + groups * G * ROW for groups in RINGS]

    table_dma = Landing(nc, "table_rows_written", 3)
    weight_dma = Landing(nc, "gat_weights_landed")
    gathered = Landing(nc, "rows_gathered", max(RINGS))
    el_out_dma = Landing(nc, "el_slots_written", 2)
    el_in_dma = Landing(nc, "el_lanes_landed")
    top_out_dma = Landing(nc, "top_slots_written")
    top_in_dma = Landing(nc, "top_items_landed")

    tile_regs_v = [nc.vector.alloc_register(f"node_tile_v{i}") for i in range(G)]
    tile_regs_t = [nc.tensor.alloc_register(f"node_tile_t{i}") for i in range(G)]
    free = {}

    def gat(layer, W, al, ar, b, rows_of, before_slots, background):
        Q.need(before_slots)
        weight_dma.sent(Q.raw.dma_start(w_ext[:, :, 0:D], W.rearrange("(k p) n -> p k n", p=P)))
        for n, a in ((0, al), (1, ar)):
            weight_dma.sent(Q.raw.dma_start(a_rows[:, n, :], a.rearrange("h d -> (h d)").partition_broadcast(P)))
        m_w = weight_dma.sent(Q.raw.dma_start(bias, b.partition_broadcast(P)))
        for n in range(2):
            m = V.done(V.need(m_w, before_slots).tensor_tensor(a_prod, w_ext[:, :, 0:D],
                                                               spread(a_rows[:, n, :], 1, K), ALU.mult))
            m_wext = V.done(V.need(m).tensor_reduce(
                w_ext[:, :, D + n * H:D + (n + 1) * H],
                a_prod.rearrange("p k (h d) -> p k h d", h=H), AX.X, ALU.add))
            V.need(m_wext)
        def feat_transpose(j):
            if j == 0:
                rows_ready[0] = rows_of(0)
            if j + 1 < NT:
                rows_ready[j + 1] = rows_of(j + 1)
            rows, m_rows = rows_ready[j]
            tb = bank[j % 2]
            for k in range(K):
                m = T.done(T.need(m_rows, bank_free[j % 2]).transpose(tb[:, k * P:(k + 1) * P],
                                                                      rows[:, k * P:(k + 1) * P], ident))
            free[("rows", j % 4)] = m
            m = S.done(S.need(m, free.get(("rows_T", j % 2))).activation(rows_T[:, j % 2, :], tb[:, 0:K * P], ACT.Copy))
            bank_free[j % 2] = m_rows_T[j] = m

        def feat_product(j):
            fb = bank[2 + j % 2]
            for k in range(K):
                m2 = T.done(T.need(m_rows_T[j], m_wext, bank_free[2 + j % 2]).matmul(
                    fb[:, 0:D + 2 * H], rows_T[:, j % 2, k * P:(k + 1) * P], w_ext[:, k, :],
                    start=(k == 0), stop=(k == K - 1)))
            free[("rows_T", j % 2)] = m2
            V.need(m2, free.get(("feats", j % 3)))
            m3 = V.done(V.raw.tensor_copy(feats[:, j % 3, :], fb[:, 0:ROW]))
            m4 = V.done(V.raw.tensor_copy(er_nodes[:, j, :], fb[:, ROW:ROW + H]))
            bank_free[2 + j % 2] = m4
            n = P if j < NT - 1 else LAST
            free[("feats", j % 3)] = table_dma.sent(Q.need(m3).dma_start(
                tables[layer][j * P:j * P + n, :], feats[0:n, j % 3, :]), j % 3)
            return m4

        m_rows_T, rows_ready = {}, {}
        for j in range(NT + 1):
            if j < NT:
                feat_transpose(j)
            if j:
                m4 = feat_product(j - 1)
        m_er_nodes = m4
        m_table = table_dma.all()

        ring, RING, LAG = rings[layer], RINGS[layer], RINGS[layer] - 1
        L.need(m_table)
        V.need(m_table)
        S.need(m_table)
        sum_banks = ((6, 7, 3, 1), (6, 7, 0, 1))[layer]
        m_acc0 = V.done(V.raw.memset(acc, 0.0))
        acc_flat = acc.rearrange("p a b -> p (a b)")
        by_head = lambda rows_: rows_.rearrange("p c h -> p h c")
        heads = lambda flat, n: flat[:, 0:H * (n + 2)].rearrange("p (h c) -> p h c", h=H)
        marks = {}

        def gather_group(g):
            n, s0 = min(G, NI - g * G), (g % RING) * G
            for k in range(n):
                c = g * G + k
                m_g = gathered.sent(L.need(m_items, free.get(("ring", g % RING))).indirect_dma_start(
                    out=ring[:, s0 + k, :], out_offset=None, in_=tables[layer],
                    in_offset=bass.IndirectOffsetOnAxis(ap=item_src[:, c:c + 1], axis=0)), g % RING)
            marks[("gathered", g)] = m_g

        def el_out(g):
            n, s0 = min(G, NI - g * G), (g % RING) * G
            k = g // CG
            marks[("el_out", k)] = el_out_dma.sent(Q.need(marks[("gathered", g)], marks.get(("el_in", k - 2))).dma_start(
                el_slots[g * G * P:(g * G + n) * P, :].rearrange("(i p) h -> p i h", p=P),
                ring[:, s0:s0 + n, D:ROW]), k % 2)

        def er_one_hot(g):
            n, half, tb = min(G, NI - g * G), (g % 2) * G, bank[4]
            m_oh = V.done(V.need(m_items, free.get(("one_hot", g % 2))).tensor_tensor(
                one_hot[:, half:half + n, :], spread(iota, 1, n),
                spread(item_local[:, g * G:g * G + n], 2, P), ALU.is_equal))
            for k in range(n):
                m = T.done(T.need(m_oh, bank_free[4]).transpose(
                    tb[:, k * P:(k + 1) * P], one_hot[:, half + k, :], ident))
            free[("one_hot", g % 2)] = m
            m = S.done(S.need(m, free.get(("one_hot_T", g % 2))).activation(
                one_hot_T[:, half:half + n, :], tb[:, 0:n * P].rearrange("p (a b) -> p a b", b=P), ACT.Copy))
            bank_free[4] = marks[("turned", g)] = m

        def er_product(g):
            n, half, eb = min(G, NI - g * G), (g % 2) * G, bank[5]
            T.need(m_er_nodes, m_item_row)
            T.raw.reg_load(tile_regs_t[0:n], item_tile_row[:, g * G:g * G + n])
            T.need(marks[("turned", g)], bank_free[5])
            for k in range(n):
                r = T.raw.snap(tile_regs_t[k], min_val=0, max_val=NT - 1)
                m = T.raw.matmul(eb[:, k * H:(k + 1) * H], one_hot_T[:, half + k, :],
                                 er_nodes.rearrange("p a b -> p (a b)")[:, bass.ds(r * H, H)],
                                 start=True, stop=True)
            free[("one_hot_T", g % 2)] = marks[("er", g)] = T.done(m)

        def er_keep(g):
            n, at = min(G, NI - g * G), (g * G) % (3 * CI)
            bank_free[5] = marks[("er_kept", g // CG)] = V.done(
                V.need(marks[("er", g)], marks.get(("weights", g // CG - 3))).tensor_copy(
                    er_item[:, at:at + n, :], bank[5][:, 0:n * H].rearrange("p (a b) -> p a b", b=H)))

        def size(k):
            return min(CI, NI - k * CI)

        def el_in(k):
            n = size(k)
            marks[("el_in", k)] = el_in_dma.sent(Q.need(marks[("el_out", k)], marks.get(("el_turned", k - 1))).dma_start(
                slot_in[:, 0:n, :], el_slots[k * CI * P:(k * CI + n) * P, :].rearrange("(p c) h -> p c h", p=P)))

        def carries(k, ends, backwards, m):
            d = 1 if backwards else 0
            free["carry_copied"] = V.done(V.need(m, free.get("carry")).tensor_copy(carry[:, 0:H], ends))
            m = V.done(V.raw.tensor_copy(carry[:, H:2 * H], any_fence[:, d, k:k + 1].to_broadcast([P, H])))
            T.need(m, bank_free[2]).transpose(bank[2][0:H, 0:P], carry[:, 0:H], ident)
            m = free["carry"] = T.done(T.raw.transpose(bank[2][0:H, P:2 * P], carry[:, H:2 * H], ident))
            marks["turned_ends"] = [m, S.done(S.need(m, free.get("any_T")).activation(
                any_T[0:H, :], bank[2][0:H, P:2 * P], ACT.Copy))]

        def carries_in(k, backwards):
            first = k == 0 or backwards
            ends_T, any_ = bank[2][0:H, 0:P], any_T[0:H, :]
            edge = P if backwards else 0
            if first:
                m = V.done(V.need(free.get("carry_T")).memset(carry_T[0:H, edge:edge + 1], -BIG))
                start = -BIG
            else:
                m = V.done(V.need(free.get("carry_T"), marks["past"]).tensor_copy(carry_T[0:H, 0:1], past[0:H, 0:1]))
                start = past[0:H, 0:1]
            to = carry_T[0:H, 0:P] if backwards else carry_T[0:H, 1:P + 1]
            if backwards:
                to, ends_T, any_ = to[:, ::-1], ends_T[:, ::-1], any_[:, ::-1]
            m = free["any_T"] = V.done(V.need(m, marks["turned_ends"]).tensor_tensor_scan(
                to, any_, ends_T, start, ALU.add, ALU.max))
            if not backwards:
                marks["past"] = V.done(V.need(m).tensor_copy(past[0:H, 0:1], carry_T[0:H, P:P + 1]))
            at = 1 if backwards else 0
            free["carry_T"] = m = T.done(T.need(m).transpose(bank[2][:, 2 * P:2 * P + H], carry_T[0:H, at:at + P],
                                                             ident[0:H, 0:H]))
            marks["entering"] = m

        def chunk_steps(k):
            n = size(k)
            el_h, fwd, top = heads(el_flat, n), heads(fwd_flat, n), heads(top_flat, n)
            whole = slice(0, H * (n + 2))
            forwards = lambda: V.done(V.raw.tensor_tensor_scan(
                fwd_flat[:, whole], mask_f_flat[:, whole], el_flat[:, whole], -BIG, ALU.add, ALU.max))
            backwards = lambda: V.done(V.raw.tensor_tensor_scan(
                top_flat[:, whole][:, ::-1], mask_b_flat[:, whole][:, ::-1], fwd_flat[:, whole][:, ::-1], -BIG,
                ALU.add, ALU.max))

            def lanes():
                S.need(marks[("el_in", k)], marks.get("fwd_scanned"))
                marks[("el_turned", k)] = S.done(S.raw.activation(el_h[:, :, 1:n + 1], by_head(slot_in[:, 0:n, :]), ACT.Copy))
                marks["lanes"] = S.done(S.raw.activation(heads(mask_f_flat, n), spread(fence[:, k, 0:n + 2], 1, H),
                                                         ACT.Copy))

            def forward_scan():
                V.need(marks.get("fwd_scanned"))
                V.done(V.raw.memset(el_h[:, :, n + 1], -BIG))
                m = V.done(V.raw.memset(el_h[:, :, 0], -BIG))
                V.need(m, marks["lanes"], marks.get("bwd_scanned"))
                carries(k, fwd[:, :, n], False, forwards())

            def forward_carry():
                carries_in(k, False)
                marks["mask_b"] = S.done(S.need(marks.get("bwd_scanned")).activation(
                    heads(mask_b_flat, n), spread(fence[:, k, 1:n + 3], 1, H), ACT.Copy))

            def backward_scan():
                enter = enters[:, k % 2, :]
                m = V.done(V.need(marks["entering"], marks.get(("seam_read", k - 2))).tensor_copy(enter, bank[2][:, 2 * P:2 * P + H]))
                bank_free[2] = m
                m = V.done(V.need(m).tensor_copy(el_h[:, :, 0], enter))
                marks["fwd_scanned"] = m = forwards() if V.need(m) else None
                m = V.done(V.need(m).memset(fwd[:, :, n + 1], -BIG))
                V.need(m, marks["mask_b"], marks.get(("top_turned", k - 1)))
                carries(k, top[:, :, 1], True, backwards())

            def backward_carry():
                carries_in(k, True)

            def to_items():
                m = V.done(V.need(marks["entering"]).tensor_copy(fwd[:, :, n + 1], bank[2][:, 2 * P:2 * P + H]))
                bank_free[2] = m
                V.need(m, free["carry_copied"])
                marks["bwd_scanned"] = m = backwards()
                m = marks[("top_turned", k)] = S.done(S.need(m, marks.get(("top_out", k - 1)),
                                                                      marks.get(("seam_read", k - 1))).activation(
                    slot_out[:, 0:n, :], top[:, :, 1:n + 1].rearrange("p h c -> p c h"), ACT.Copy))
                slots = top_slots[k * CI * P:(k * CI + n) * P, :]
                m = marks[("top_out", k)] = top_out_dma.sent(Q.need(m).dma_start(
                    slots.rearrange("(p c) h -> p c h", p=P), slot_out[:, 0:n, :]))
                marks[("top_in", k)] = top_in_dma.sent(Q.need(m, marks.get(("weights", k - 1))).dma_start(
                    top_item[:, 0:n, :], slots.rearrange("(i p) h -> p i h", p=P)))

            def weights():
                at, row0, er0 = (k * CI) % (2 * CI), (k * CI) % (RING * G), (k * CI) % (3 * CI)
                er, w, tp = er_item[:, er0:er0 + n, :], w_item[:, at:at + n, :], top_item[:, 0:n, :]
                V.need(marks[("er_kept", k)], [marks[("gathered", g)] for g in range(k * CG, min(NG, (k + 1) * CG))],
                       free.get(("w_item", k % 2)))
                V.done(V.raw.tensor_tensor(w, ring[:, row0:row0 + n, D:ROW], er, ALU.add))
                m = V.done(V.need(marks[("top_in", k)]).tensor_tensor(tp, tp, er, ALU.add))
                V.need(m)
                V.done(V.raw.scalar_tensor_tensor(w, w, NEG_SLOPE, w, ALU.mult, ALU.max))
                m = V.done(V.raw.scalar_tensor_tensor(tp, tp, NEG_SLOPE, tp, ALU.mult, ALU.max))
                m = V.done(V.need(m).tensor_tensor(w, w, tp, ALU.subtract))
                marks[("w", k)] = S.done(S.need(m).activation(w, w, ACT.Exp))
                if k:
                    seam_factor(k, er)
                marks[("weights", k)] = m

            return [lanes, forward_scan, forward_carry, backward_scan, backward_carry, to_items, weights]

        def seam_factor(k, er):
            old, new, same, row = seam[0:1, 0, 0:H], seam[0:1, 1, 0:H], seam[0:1, 2, 0:1], seam[0:1, 3, 0:H + 1]
            V.need(marks[("top_turned", k)])
            V.done(V.raw.tensor_tensor(old, enters[0:1, k % 2, :], er[0:1, 0, :], ALU.add))
            marks[("seam_read", k)] = V.done(V.raw.tensor_tensor(new, slot_out[0:1, 0, :], er[0:1, 0, :], ALU.add))
            m = V.done(V.raw.tensor_scalar(same, fence[0:1, k, 1:2], 0.0, None, ALU.is_equal))
            V.need(m)
            V.done(V.raw.scalar_tensor_tensor(old, old, NEG_SLOPE, old, ALU.mult, ALU.max))
            m = V.done(V.raw.scalar_tensor_tensor(new, new, NEG_SLOPE, new, ALU.mult, ALU.max))
            m = V.done(V.need(m).tensor_tensor(old, old, new, ALU.subtract))
            m = V.done(V.need(m, free.get("seam_row")).tensor_scalar(row[:, 0:H], old, same, None, ALU.mult))
            m2 = V.done(V.raw.tensor_copy(row[:, H:H + 1], item_local[0:1, k * CI:k * CI + 1]))
            m = S.done(S.need(m).activation(row[:, 0:H], row[:, 0:H], ACT.Exp))
            marks[("seam_row", k)] = [m, m2]
            seams.append(k)

        seams = []

        def seam_spread():
            k = seams[0]
            marks["seam_spread"] = free["seam_row"] = T.done(T.need(marks[("seam_row", k)], bank_free[5]).matmul(
                bank[5][:, P:P + H + 1], ones[0:1, :], seam[0:1, 3, 0:H + 1], start=True, stop=True))

        def seam_take():
            k = seams.pop()
            V.need(marks["seam_spread"])
            m = V.done(V.raw.tensor_tensor(match[:, 0:1], iota_item[:, 0:1], bank[5][:, P + H:P + H + 1],
                                           ALU.is_equal))
            m = V.done(V.need(m).tensor_scalar(match[:, 1:2], match[:, 0:1], 0.0, None, ALU.is_equal))
            m = V.done(V.need(m, free.get(("factor", k % 2))).tensor_scalar(factors[:, k % 2, :], bank[5][:, P:P + H], match[:, 0:1], match[:, 1:2],
                                               ALU.mult, ALU.add))
            bank_free[5] = marks[("factor", k)] = m

        def rescale(k, at, m_acc):
            rows_ = acc_flat[:, at]
            V.need(marks[("factor", k)], m_acc)
            m = V.done(V.raw.tensor_tensor(rows_[:, 0:D].rearrange("p (h d) -> p h d", h=H),
                                           rows_[:, 0:D].rearrange("p (h d) -> p h d", h=H),
                                           spread(factors[:, k % 2, :], 2, HD), ALU.mult))
            m = free[("factor", k % 2)] = V.done(V.raw.tensor_tensor(rows_[:, D:ROW], rows_[:, D:ROW], factors[:, k % 2, :], ALU.mult))
            return m

        def make_messages(g):
            n, s0, half = min(G, NI - g * G), (g % RING) * G, (g % 3) * G
            k_, at = g // CG, (g * G) % (2 * CI)
            w_g = w_item[:, at:at + n, :]
            msg = messages[:, half:half + n, :]
            m1 = L.done(L.need(marks[("gathered", g)], marks[("w", k_)], free.get(("messages", g % 3))).tensor_tensor(
                msg[:, :, 0:D].rearrange("p i (h d) -> p i h d", h=H),
                ring[:, s0:s0 + n, 0:D].rearrange("p i (h d) -> p i h d", h=H),
                spread(w_g, 3, HD), ALU.mult))
            m2 = S.done(S.need(marks[("w", k_)], free.get(("messages", g % 3))).activation(msg[:, :, D:ROW], w_g, ACT.Copy))
            free[("w_item", k_ % 2)] = [m1, m2]
            free[("ring", g % RING)] = [m1, marks[("el_out", k_)], marks[("weights", k_)]]
            m_oh = marks[("sum_hot", g)]
            for k in range(n):
                ob = sum_banks[(g * G + k) % len(sum_banks)]
                m = T.done(T.need(m1, m2, m_oh, bank_free[ob]).matmul(
                    bank[ob][:, 0:ROW], sum_hot[:, half + k, :], messages[:, half + k, :], start=True, stop=True))
                bank_free[ob] = marks[("sum", g, k)] = m
            free[("sum_hot", g % 3)] = free[("messages", g % 3)] = m

        def make_sum_hot(g):
            n, half = min(G, NI - g * G), (g % 3) * G
            S.need(m_items, free.get(("sum_hot", g % 3)))
            for k in range(n):
                i = g * G + k
                m = S.done(S.raw.activation(sum_hot[:, half + k, :], iota, ACT.Square,
                                            bias=item_local[:, i:i + 1], scale=-1.0))
            marks[("sum_hot", g)] = S.done(S.need(m).activation(
                sum_hot[:, half:half + n, :], sum_hot[:, half:half + n, :], ACT.Relu, bias=1.0, scale=-1.0))

        def load_tiles(g):
            n = min(G, NI - g * G)
            V.raw.reg_load(tile_regs_v[0:n], item_tile_row[:, g * G:g * G + n])
            for k in range(n):
                marks[("at", g, k)] = bass.ds(V.raw.snap(tile_regs_v[k], min_val=0, max_val=NT - 1) * ROW, ROW)

        def add_sums(g):
            n = min(G, NI - g * G)
            for k in range(n):
                ob = sum_banks[(g * G + k) % len(sum_banks)]
                at = marks[("at", g, k)]
                m_acc = marks["acc"]
                if k == 0 and g % CG == 0 and g:
                    m_acc = rescale(g // CG, at, m_acc)
                V.need(marks[("sum", g, k)])
                marks["acc"] = bank_free[ob] = V.done(V.after(m_acc, V.raw.tensor_tensor(
                    acc_flat[:, at], acc_flat[:, at], bank[ob][:, 0:ROW], ALU.add)))

        marks["acc"] = m_acc0
        todo = {}
        for k in range(NC):
            last = min(NG, (k + 1) * CG) - 1
            for i, f in enumerate(chunk_steps(k)):
                todo.setdefault(last + (2, 3, 4, 5, 6, 7, 8 if RING == 12 else 9)[i], []).append(f)
        for s in range(NG + LAG + 1):
            if s < NG:
                background(s)
            if s > LAG:
                load_tiles(s - LAG - 1)
            if LAG <= s < NG + LAG:
                make_sum_hot(s - LAG)
            if s < NG:
                gather_group(s)
                er_one_hot(s)
            if seams:
                seam_take()
            if 2 <= s < NG + 2:
                er_keep(s - 2)
            if 1 <= s <= NG:
                er_product(s - 1)
                el_out(s - 1)
                if s % CG == 0 or s == NG:
                    el_in((s - 1) // CG)
            for f in todo.get(s, ()):
                f()
            if seams:
                seam_spread()
            if s > LAG:
                add_sums(s - LAG - 1)
            if LAG <= s < NG + LAG:
                make_messages(s - LAG)
        m_acc = marks["acc"]
        m = V.done(V.need(m_acc).tensor_scalar(r_den, acc[:, :, D:ROW], 1e-30, None, ALU.max))
        m = V.done(V.need(m).reciprocal(r_den, r_den))
        V.need(m)
        marks = {}
        for j in range(NT):
            m = V.done(V.raw.tensor_tensor(hidden[:, j, :].rearrange("p (h d) -> p h d", h=H),
                                           acc[:, j, 0:D].rearrange("p (h d) -> p h d", h=H),
                                           spread(r_den[:, j, :], 2, HD), ALU.mult))
            m = V.done(V.need(m).tensor_tensor(hidden[:, j, :], hidden[:, j, :], bias, ALU.add))
            marks[j] = S.done(S.need(m).activation(hidden[:, j, :], hidden[:, j, :], ACT.Relu))
        return marks

    w_dma = [Landing(nc, f"w_items_landed{i}_") for i in range(ceil_div(NI, 64))]

    m_ln = ln_stats([m_x, m_x0])

    def ln_tile(j):
        return rows_in[:, j % 4, :], ln_rows(rows_in[:, j % 4, :], j, m_ln, free.get(("rows", j % 4)))


    keep = arena.used
    arena.used = ring_end[0]
    x_flat = x.rearrange("p a b -> p (a b)")
    member_words = ceil_div(N_COL * NT, 2)
    sort_member = x_flat[:, 0:member_words].bitcast(BF16)[:, 0:N_COL * NT].rearrange("p (a b) -> p a b", a=N_COL)
    sort_work = x_flat[:, member_words:member_words + 1024].rearrange("p (a b) -> p a b", a=2)
    sort_tile = x_flat[:, member_words + 1024:member_words + 1024 + N_COL]
    sort_prefix = arena.take(N_COL * NT + 1)
    sort_small = arena.take(4, NT)
    sort_src = arena.take(N_COL, dtype=I32)
    sort_dst = arena.take(N_COL, dtype=I32)
    sort_local = arena.take(N_COL, dtype=I32)
    sort_pos = arena.take(N_COL)
    sort_void = arena.take(N_COL)
    sort_cmp = arena.take(NIC, NT)
    sort_tiles_f = arena.take(NIC)
    sort_tiles_i = arena.take(NIC, dtype=I32)
    arena.used = keep
    sorted_tile_row = sbuf("sorted_tile_row", [1, NI], I32)
    sorted_tile = dram("sorted_tile", (NIC * P,), I32)
    sort_dma = Landing(nc, "sort_landed")
    buckets = Buckets(sort_member, N_COL, NT, sort_prefix, sort_work, sort_small, (0, 0))
    sort = {}

    def split(pos, pos_i, tile, row, m):
        m = V.done(V.need(m).tensor_copy(pos_i, pos))
        m = V.done(V.need(m).tensor_scalar(pos_i, pos_i, 7, None, ALU.arith_shift_right))
        m = V.done(V.need(m).tensor_copy(tile, pos_i))
        return V.done(V.need(m).scalar_tensor_tensor(row, tile, -float(P), pos, ALU.mult, ALU.add))

    def sort_begin():
        full = (N_COL - 1) * P
        m = [V.done(V.raw.memset(sort_src[:, N_COL - 1:N_COL], 1 << 20)),
             V.done(V.raw.memset(sort_dst[:, N_COL - 1:N_COL], 0))]
        Q.need(m)
        for whole, to in ((t["src"], sort_src), (t["dst"], sort_dst)):
            sort_dma.sent(Q.raw.dma_start(to[:, 0:N_COL - 1], whole[0:full].rearrange("(p c) -> p c", p=P)))
            m_in = sort_dma.sent(Q.raw.dma_start(to[0:E - full, N_COL - 1:N_COL], whole[full:E].unsqueeze(1)))
        m = V.done(V.need(m_in).tensor_scalar(sort_dst, sort_dst, 7, None, ALU.logical_shift_left))
        m2 = V.done(V.raw.tensor_scalar(sort_local, sort_src, P - 1, None, ALU.bitwise_and))
        m = V.done(V.need(m, m2).tensor_tensor(sort_local, sort_local, sort_dst, ALU.bitwise_or))
        m = V.done(V.need(m).tensor_copy(edge_value, sort_local))
        sort["value"] = V.done(V.need(m).tensor_scalar(edge_value, edge_value, 1.0, None, ALU.add))
        m = V.done(V.need(m).tensor_scalar(sort_src, sort_src, 7, None, ALU.arith_shift_right))
        m = V.done(V.need(m).tensor_copy(sort_tile, sort_src))
        sort["m"] = V.done(V.need(m).tensor_scalar(sort_void, sort_tile, float(NT), None, ALU.is_ge))

    def sort_members(a, b):
        sort["m"] = V.done(V.need(sort["m"]).tensor_tensor(
            sort_member[:, a:b, :], spread(iota[:, 0:NT], 1, b - a), spread(sort_tile[:, a:b], 2, NT), ALU.is_equal))

    def sort_end():
        m = V.done(V.need(buckets.m_pos).tensor_tensor(sort_pos, sort_pos, sort_void, ALU.subtract))
        sort["m"] = split(sort_pos, sort_src, edge_to_tile, edge_to_row, m)
        sort["row"] = buckets.tile_row(NI, sort_cmp, sort_tiles_f, sort_tiles_i, sorted_tile, sorted_tile_row, sort_dma)

    sort_todo = [sort_begin]
    for a, b in buckets.chunks:
        sort_todo.append(lambda a=a, b=b: sort_members(a, b))
    n_chunks = len(buckets.chunks)
    for q in range(n_chunks + 1):
        if q:
            sort_todo.append([lambda q=q: buckets.totals_kept(q - 1)])
        if q < n_chunks:
            sort_todo.append(lambda q=q: buckets.totals_product(q, sort["m"]))
    sort_todo.append(buckets.scan)
    for q in range(n_chunks + 1):
        if q:
            sort_todo.append([lambda q=q: buckets.positions_kept(q - 1, sort_pos)])
        if q < n_chunks:
            sort_todo.append(lambda q=q: buckets.positions_product(q))
    sort_todo.append(sort_end)

    def sort_step(g):
        if g >= 4 and sort_todo:
            while sort_todo[0].__class__ is list:
                sort_todo.pop(0)[0]()
            sort_todo.pop(0)()

    arena.used = ring_end[1]
    to_row = arena.take(8, P)
    to_tile = arena.take(8, NI)
    iota_tiles = arena.take(NI)
    arena.used = keep
    INV = 3

    def invert_step(g):
        if g == 0:
            sort["iota"] = L.done(L.need(h1[0]).iota(iota_tiles, [[1, NI]], base=0, channel_multiplier=0,
                                                     allow_small_or_imprecise_dtypes=True))
            return
        per = ceil_div(N_COL, NG - 4)
        for c in range((g - 1) * per, min(N_COL, g * per)):
            s = c % 8
            m1 = S.done(S.need(sort["m"], sort.get(("inv", s))).activation(
                to_row[:, s, :], iota, ACT.Square, bias=edge_to_row[:, c:c + 1], scale=-1.0))
            m1 = S.done(S.need(m1).activation(to_row[:, s, :], to_row[:, s, :], ACT.Relu, bias=1.0, scale=-1.0))
            m = V.done(V.need(sort["m"], sort["iota"], sort.get(("inv", s))).tensor_scalar(to_tile[:, s, :], iota_tiles, edge_to_tile[:, c:c + 1],
                                           edge_value[:, c:c + 1], ALU.is_equal, ALU.mult))
            sort[("inv", s)] = m = T.done(T.need(m1, m, bank_free[INV]).matmul(
                bank[INV][:, 0:NI], to_row[:, s, :], to_tile[:, s, :], start=(c == 0), stop=(c == N_COL - 1)))
            if c == N_COL - 1:
                sort["sorted"] = bank_free[INV] = V.done(V.need(m).tensor_copy(sorted_value, bank[INV][:, 0:NI]))


    h1 = gat(0, t["L0_gnn_W1"], t["L0_gnn_al1"], t["L0_gnn_ar1"], t["L0_gnn_b1"], ln_tile,
             [m_items], sort_step)
    m_x0 = V.done(V.need(sort["m"]).memset(x[:, NT - 1, :], 0.0))
    x_back = Landing(nc, "x_back")
    x_back.sent(Q.need(m_x0).dma_start(x[:, 0:NT - 1, :], t["x"][0:(NT - 1) * P, :].rearrange("(t p) d -> p t d", p=P)))
    m_x_back = x_back.sent(Q.raw.dma_start(x[0:LAST, NT - 1, :], t["x"][(NT - 1) * P:N, :]))
    h2 = gat(1, t["L0_gnn_W2"], t["L0_gnn_al2"], t["L0_gnn_ar2"], t["L0_gnn_b2"],
             lambda j: (hidden[:, j, :], h1[j]), list(h1.values()), invert_step)
    m_x = {}
    for j in range(NT):
        m_x[j] = V.done(V.need(h2[j], m_x_back).tensor_tensor(x[:, j, :], x[:, j, :], hidden[:, j, :], ALU.add))

    arena.used = 0
    router_dma = Landing(nc, "router_landed")
    probs_dma = Landing(nc, "biases_landed")
    wide_dma = Landing(nc, "expert_weights_landed")
    shared_dma = Landing(nc, "shared_weights_landed")
    wide2_dma = Landing(nc, "expert_weights2_landed")
    token_dma = Landing(nc, "token_rows_written", 4)
    tile_in_dma = Landing(nc, "expert_tile_in", 4)
    tile_out_dma = Landing(nc, "expert_tile_out", 2)
    pick_dma = Landing(nc, "expert_rows_picked", 4)
    misc_dma = Landing(nc, "tile_rows_moved")

    def experts(layer, m_x, n_exp, F, w1_dram, b1_dram, w2_dram, b2_dram, router, router_bias,
                shared, base, w1_ready, act, m_space, finish, beside=lambda q: None):
        FC = F // P
        ntiles, expert_out = max_tiles[layer], expert_rows[layer]
        free = {}
        arena.used = base[0]
        w1 = arena.take(n_exp, K, F) if w1_ready is None else w1_ready[0]
        w2_at = arena.used
        w2 = arena.take(n_exp, FC, D)
        w2_end = arena.used
        now_at = arena.used
        w1_now = arena.take(2, K, F)
        if shared:
            arena.used = now_at
            w1s, w2s = arena.take(K, F), arena.take(FC, D)
            b1s = arena.take(FC)
        b1 = arena.take(n_exp, FC)
        b2 = arena.take(D)
        wr = arena.take(K, n_exp)
        mask = arena.take(NT, n_exp + 1)
        mask_T = arena.take(2, P)
        pair_w = arena.take(2, NT)
        pair_at = arena.take(2 * NT, dtype=U32)
        tile_row = arena.take(max(max_tiles), dtype=I32)[0:1, :]
        slot_token = arena.take(max(max_tiles), dtype=U32)
        work_at = arena.used
        rows = arena.take(4, D)
        rows_T = arena.take(2, K, 2 * P)
        hid_s = arena.take(FC, 2 * P) if shared else None
        arena.used = w2_at
        logits = arena.take(NT, n_exp)
        hit = arena.take(2, NT, n_exp)
        probs = arena.take(NT, n_exp)
        tmp = arena.take(NT, n_exp)
        one = arena.take(4, NT)
        member = arena.take(2 * NT, n_exp, dtype=BF16)
        prefix = arena.take(2 * NT * n_exp + 1)
        work = arena.take(2, 512)
        small = arena.take(4, n_exp)
        compare = arena.take(1, n_exp)
        tiles_f, tiles_i = arena.take(1), arena.take(1, dtype=I32)
        pos = arena.take(2 * NT)
        bias_r = arena.take(n_exp)
        pos_i = arena.take(2 * NT, dtype=I32)
        at_tile, at_row = arena.take(2 * NT), arena.take(2 * NT)
        token = arena.take(2, NT)
        to_row = arena.take(2 * NT, P)
        to_tile = arena.take(2 * NT, ntiles)
        assert arena.used <= w2_end

        Q.need(m_space)
        m_router = router_dma.sent(Q.raw.dma_start(wr, router.rearrange("(k p) e -> p k e", p=P)))
        probs_dma.sent(Q.raw.dma_start(b2[0:n_exp, :], b2_dram))
        if shared:
            probs_dma.sent(Q.raw.dma_start(b2[n_exp:n_exp + 1, :], shared[3].unsqueeze(0)))
        if router_bias is not None:
            m_router = router_dma.sent(Q.raw.dma_start(bias_r, router_bias.partition_broadcast(P)))
        with nc.allow_non_contiguous_dma(reason="the first biases, one column per 128 units"):
            if shared:
                probs_dma.sent(Q.raw.dma_start(b1s, shared[1].rearrange("(c p) -> p c", p=P)))
            for e in range(n_exp):
                m_wr = probs_dma.sent(Q.raw.dma_start(b1[:, e, :], b1_dram[e].rearrange("(c p) -> p c", p=P)))
        if shared:
            shared_dma.sent(Q.raw.dma_start(w1s, shared[0].rearrange("(k p) f -> p k f", p=P)))
            m_ws = shared_dma.sent(Q.raw.dma_start(w2s, shared[2].rearrange("(c p) d -> p c d", p=P)))
        if w1_ready is None:
            for e in range(n_exp):
                m_w1 = wide_dma.sent(Q.raw.dma_start(w1[:, e, :, :], w1_dram[e].rearrange("(k p) f -> p k f", p=P)))
        else:
            m_w1 = w1_ready[1]

        m_ln = ln_stats(m_x)
        lb = 2
        turned = {}
        m_normed = {}
        for j in range(NT + 1):
            for i in ((0, 1) if j == 0 else (j + 1,)):
                if i < NT:
                    m_normed[i] = ln_rows(rows[:, i % 4, :], i, [m_ln, m_space], free.get(("rows", i % 4)))
            if j < NT:
                m = m_normed[j]
                for k in range(K):
                    m2 = T.done(T.need(m, bank_free[j % 2]).transpose(bank[j % 2][:, k * P:(k + 1) * P],
                                                                      rows[:, j % 4, k * P:(k + 1) * P], ident))
                n = P if j < NT - 1 else LAST
                free[("rows", j % 4)] = [m2, token_dma.sent(Q.need(m).dma_start(
                    token_rows[layer][j * P:j * P + n, :], rows[0:n, j % 4, :]), j % 4)]
                turned[j] = bank_free[j % 2] = S.done(S.need(m2, free.get(("rows_T", j % 2))).activation(
                    rows_T[:, j % 2, :, 0:P], bank[j % 2][:, 0:K * P].rearrange("p (k n) -> p k n", k=K), ACT.Copy))
            if j:
                i = j - 1
                for k in range(K):
                    m = T.done(T.need(turned[i], m_router, bank_free[lb]).matmul(
                        bank[lb][:, i * n_exp:(i + 1) * n_exp], rows_T[:, i % 2, k, 0:P], wr[:, k, :],
                        start=(k == 0), stop=(k == K - 1)))
                free[("rows_T", i % 2)] = m
        m = V.done(V.need(m, m_space).tensor_copy(logits, bank[lb][:, 0:NT * n_exp].rearrange("p (j e) -> p j e", e=n_exp)))
        bank_free[lb] = m
        if router_bias is not None:
            m = V.done(V.need(m, m_router).tensor_tensor(logits, logits, spread(bias_r, 1, NT), ALU.add))
        top1, top2, den, s4 = (one[:, i, :] for i in range(4))

        def over(v):
            return spread(v, 2, n_exp)

        if shared:
            m = V.done(V.need(m).tensor_reduce(top1, logits, AX.X, ALU.max))
            m = V.done(V.need(m).tensor_tensor(probs, logits, over(top1), ALU.subtract))
            m = S.done(S.need(m).activation(probs, probs, ACT.Exp))
            m = V.done(V.need(m).tensor_reduce(den, probs, AX.X, ALU.add))
            m = V.done(V.need(m).reciprocal(den, den))
            m = V.done(V.need(m).tensor_tensor(probs, probs, over(den), ALU.mult))
            score = probs
        else:
            score = logits
        m_score = m
        experts_iota = iota[:, 0:n_exp]
        for k, best in ((0, top1), (1, top2)):
            src_ = score if k == 0 else tmp
            m = V.done(V.need(m).tensor_reduce(best, src_, AX.X, ALU.max))
            h_ = hit[:, k, :, :]
            m = V.done(V.need(m).tensor_tensor(h_, src_, over(best), ALU.is_lt))
            m = V.done(V.need(m).scalar_tensor_tensor(h_, h_, float(P), spread(experts_iota, 1, NT), ALU.mult, ALU.add))
            m = V.done(V.need(m).tensor_reduce(s4, h_, AX.X, ALU.min))
            m = V.done(V.need(m).tensor_tensor(h_, spread(experts_iota, 1, NT), over(s4), ALU.is_equal))
            if k == 0:
                m = V.done(V.need(m).scalar_tensor_tensor(tmp, h_, -BIG, score, ALU.mult, ALU.add))
        m_hit = m
        if shared:
            m = V.done(V.need(m).tensor_tensor(den, top1, top2, ALU.add))
            m = V.done(V.need(m).reciprocal(den, den))
            V.done(V.need(m).tensor_tensor(pair_w[:, 0, :], top1, den, ALU.mult))
            m = V.done(V.raw.tensor_tensor(pair_w[:, 1, :], top2, den, ALU.mult))
        else:
            m = V.done(V.need(m).tensor_tensor(top2, top2, top1, ALU.subtract))
            m = S.done(S.need(m).activation(top2, top2, ACT.Exp))
            m = V.done(V.need(m).tensor_scalar(den, top2, 1.0, None, ALU.add))
            m = V.done(V.need(m).reciprocal(pair_w[:, 0, :], den))
            m = V.done(V.need(m).tensor_tensor(pair_w[:, 1, :], top2, pair_w[:, 0, :], ALU.mult))
        for k in range(2):
            m = V.done(V.need(m, m_valid).tensor_scalar(hit[:, k, NT - 1, :], hit[:, k, NT - 1, :],
                                                        valid_row, None, ALU.mult))
        V.need(m)
        m = V.done(V.raw.tensor_copy(member, hit.rearrange("p k j e -> p (k j) e")))
        m_mask = V.done(V.raw.memset(mask, 1.0))
        V.done(V.need(m).tensor_tensor(hit[:, 0, :, :], hit[:, 0, :, :], over(pair_w[:, 0, :]), ALU.mult))
        m2 = V.done(V.raw.tensor_tensor(hit[:, 1, :, :], hit[:, 1, :, :], over(pair_w[:, 1, :]), ALU.mult))
        m_mask = V.done(V.need(m2, m_mask).tensor_tensor(mask[:, :, 0:n_exp], hit[:, 0, :, :], hit[:, 1, :, :], ALU.add))
        bk = Buckets(member, 2 * NT, n_exp, prefix, work, small, (2, 3))
        ranks = {"member": m}

        def to_slots():
            m = bk.m_pos
            m_pos = V.done(V.need(m).tensor_copy(pair_at, pos))
            m2 = V.done(V.need(m_valid, m).tensor_scalar(s4[:, 0:1], valid_row, -1.0, None, ALU.add))
            m = m_pos
            for k in range(2):
                at = k * NT + NT - 1
                m = V.done(V.need(m, m2).tensor_tensor(pos[:, at:at + 1], pos[:, at:at + 1], s4[:, 0:1], ALU.add))
            ranks["split"] = split(pos, pos_i, at_tile, at_row, m)

        def to_pairs():
            V.done(V.need(ranks["split"]).tensor_tensor(to_row, spread(iota, 1, 2 * NT), spread(at_row, 2, P),
                                                        ALU.is_equal))
            m1 = V.done(V.raw.tensor_tensor(to_tile, spread(iota[:, 0:ntiles], 1, 2 * NT), spread(at_tile, 2, ntiles),
                                            ALU.is_equal))
            for k in range(2):
                m2 = V.done(V.raw.tensor_scalar(token[:, k, :], iota[:, 0:NT], float(P), iota_item[:, 0:1],
                                                ALU.mult, ALU.add))
            ranks["pairs"] = V.done(V.need(m1, m2).tensor_tensor(
                to_tile, to_tile, spread(token.rearrange("p k j -> p (k j)"), 2, ntiles), ALU.mult))

        def to_tokens():
            for q in range(2 * NT):
                mt = T.need(ranks["pairs"], bank_free[4]).matmul(
                    bank[4][:, 0:ntiles], to_row[:, q, :], to_tile[:, q, :], start=(q == 0), stop=(q == 2 * NT - 1))
            mt = T.done(mt)
            ranks["slots"] = bank_free[4] = V.done(V.need(mt).tensor_copy(slot_token[:, 0:ntiles], bank[4][:, 0:ntiles]))

        def to_experts():
            ranks["row"] = bk.tile_row(ntiles, compare, tiles_f, tiles_i, misc_row[layer], tile_row[:, 0:ntiles],
                                       misc_dma)
            for e in range(n_exp):
                ranks["w2"] = wide2_dma.sent(Q.need(ranks["row"], ranks["slots"], m_mask).dma_start(
                    w2[:, e, :, :], w2_dram[e].rearrange("(c p) d -> p c d", p=P)))

        ranking = [lambda q=q: bk.totals(q, ranks["member"]) for q in range(len(bk.chunks))]
        ranking.append(bk.scan)
        ranking += [lambda q=q: bk.positions(q, pos) for q in range(len(bk.chunks))]
        ranking += [to_slots, to_pairs, to_tokens, to_experts]
        if not shared:
            for f in ranking:
                f()

        m_tokens = token_dma.all()
        pairs = [list(range(a, min(NT, a + 2))) for a in range(0, NT, 2)] if shared else []
        turned, masks = {}, {}

        def shared_turn(c):
            half = c % 2
            for i, j in enumerate(pairs[c]):
                s = half * 2 + i
                m = ln_rows(rows[:, s, :], j, m_ln, free.get(("rows", s)))
                for k in range(K):
                    m2 = T.done(T.need(m, bank_free[i]).transpose(bank[i][:, k * P:(k + 1) * P],
                                                                  rows[:, s, k * P:(k + 1) * P], ident))
                free[("rows", s)] = m2
                turned[c] = bank_free[i] = S.done(S.need(m2, free.get(("rows_T", half))).activation(
                    rows_T[:, half, :, i * P:(i + 1) * P],
                    bank[i][:, 0:K * P].rearrange("p (k n) -> p k n", k=K), ACT.Copy))

        def shared_first(c):
            half, n = c % 2, len(pairs[c]) * P
            for f in range(FC):
                hb = 2 + f % 4
                for k in range(K):
                    m = T.done(T.need(turned[c], m_ws, bank_free[hb]).matmul(
                        bank[hb][:, 0:n], w1s[:, k, f * P:(f + 1) * P], rows_T[:, half, k, 0:n],
                        start=(k == 0), stop=(k == K - 1)))
                masks[f] = bank_free[hb] = S.done(S.need(m, free.get("hid_s"), m_wr).activation(
                    hid_s[:, f, 0:n], bank[hb][:, 0:n], act, bias=b1s[:, f:f + 1]))
            free[("rows_T", half)] = m

        def shared_mask(c):
            for i, j in enumerate(pairs[c]):
                m = T.done(T.need(m_mask, bank_free[i]).transpose(bank[i][0:n_exp + 1, 0:P], mask[:, j, :], ident))
                masks[("T", i)] = bank_free[i] = S.done(S.need(m, free.get(("mask_T", i))).activation(
                    mask_T[0:n_exp + 1, i, :], bank[i][0:n_exp + 1, 0:P], ACT.Copy))

        def shared_second(c):
            for i, j in enumerate(pairs[c]):
                yb = 6 + i
                T.need(masks[("T", i)], m_wr, bank_free[yb]).matmul(
                    bank[yb][:, 0:D], mask_T[0:n_exp + 1, i, :], b2[0:n_exp + 1, :], start=True, stop=False)
                for f in range(FC):
                    m = T.done(T.need(masks[f]).matmul(bank[yb][:, 0:D], hid_s[:, f, i * P:(i + 1) * P], w2s[:, f, :],
                                                       start=False, stop=(f == FC - 1)))
                free[("mask_T", i)] = m
                m_x[j] = bank_free[yb] = V.done(V.need(m).tensor_tensor(x[:, j, :], x[:, j, :], bank[yb][:, 0:D], ALU.add))
            free["hid_s"] = m

        for c in range(len(pairs)):
            if c == 0:
                shared_turn(0)
            shared_first(c)
            shared_mask(c)
            if c + 1 < len(pairs):
                shared_turn(c + 1)
            if ranking:
                ranking.pop(0)()
            shared_second(c)
        assert not (shared and ranking)
        m_slots, m_row, m_w2 = ranks["slots"], ranks["row"], ranks["w2"]
        m_shared = [free.get("hid_s"), m_tokens, bank_free[0], bank_free[1], m_slots, m_x[NT - 1] if shared else None]

        arena.used = work_at
        tin = arena.take(4, D)
        tin_T = arena.take(2, K, P)
        hid = arena.take(2, FC, P)
        tout = arena.take(2, D)
        bcol = arena.take(2, FC)
        assert arena.used <= arena.words
        w1_flat = w1.rearrange("p e k f -> p (e k f)")
        w2_flat = w2.rearrange("p e c d -> p (e c d)")
        b1_flat = b1.rearrange("p e c -> p (e c)")
        m_hid, m_b = {}, {}

        def second(q):
            s = q % 2
            T.need(m_hid[q], m_w2, bank_free[6 + s])
            T.raw.reg_load(exp_t2, tile_row[:, q:q + 1])
            r = T.raw.snap(exp_t2, min_val=0, max_val=n_exp - 1)
            for f in range(FC):
                m = T.raw.matmul(bank[6 + s][:, 0:D], hid[:, s, f, :], w2_flat[:, bass.ds(r * (FC * D) + f * D, D)],
                                 start=(f == 0), stop=(f == FC - 1))
            m = T.done(m)
            free[("hid", s)] = m
            m = V.done(V.need(m, free.get(("tout", s))).tensor_copy(tout[:, s, :], bank[6 + s][:, 0:D]))
            bank_free[6 + s] = m
            free[("tout", s)] = tile_out_dma.sent(Q.need(m).dma_start(expert_out[q * P:(q + 1) * P, :], tout[:, s, :]), s)

        def load(q):
            m_in[q] = tile_in_dma.sent(L.need(m_tokens, m_shared, m_slots, free.get(("tin", q % 4))).indirect_dma_start(
                out=tin[:, q % 4, :], out_offset=None, in_=token_rows[layer],
                in_offset=bass.IndirectOffsetOnAxis(ap=slot_token[:, q:q + 1], axis=0)), q % 4)

        m_in = {}
        for q in range(3):
            load(q)
        S.need(m_shared)
        V.need(m_shared)
        prepared = {}

        def prepare(q):
            s = q % 2
            if q + 3 < ntiles:
                load(q + 3)
            for k in range(K):
                m = T.done(T.need(m_in[q], bank_free[s]).transpose(bank[s][:, k * P:(k + 1) * P],
                                                                   tin[:, q % 4, k * P:(k + 1) * P], ident))
            free[("tin", q % 4)] = m
            V.need(m_w1, m_row, free.get(("w1_now", s)))
            V.raw.reg_load(exp_v, tile_row[:, q:q + 1])
            r = V.raw.snap(exp_v, min_val=0, max_val=n_exp - 1)
            m_now = V.done(V.raw.tensor_copy(w1_now[:, s, :, :].rearrange("p k f -> p (k f)"),
                                             w1_flat[:, bass.ds(r * (K * F), K * F)]))
            bank_free[s] = V.done(V.need(m, free.get(("tin_T", s))).tensor_copy(
                tin_T[:, s, :, :], bank[s][:, 0:K * P].rearrange("p (k n) -> p k n", k=K)))
            S.need(m_row, m_wr, free.get(("bcol", s)))
            S.raw.reg_load(exp_s, tile_row[:, q:q + 1])
            r = S.raw.snap(exp_s, min_val=0, max_val=n_exp - 1)
            m_b = S.done(S.raw.activation(bcol[:, s, :], b1_flat[:, bass.ds(r * FC, FC)], ACT.Copy))
            prepared[q] = ([bank_free[s], m_now], m_b)

        def first(q):
            s, per = q % 2, 4
            m_ready, m_b = prepared[q]
            for f0 in range(0, FC, per):
                hb = 2 + s * 2 + f0 // per
                T.need(m_ready, bank_free[hb])
                for f in range(f0, min(FC, f0 + per)):
                    for k in range(K):
                        m = T.raw.matmul(bank[hb][:, (f - f0) * P:(f - f0 + 1) * P],
                                         w1_now[:, s, k, f * P:(f + 1) * P], tin_T[:, s, k, :],
                                         start=(k == 0), stop=(k == K - 1))
                m = T.done(m)
                for f in range(f0, min(FC, f0 + per)):
                    m2 = S.done(S.need(m, m_b, free.get(("hid", s))).activation(
                        hid[:, s, f, :], bank[hb][:, (f - f0) * P:(f - f0 + 1) * P], act, bias=bcol[:, s, f:f + 1]))
                bank_free[hb] = m2
            free[("tin_T", s)] = free[("w1_now", s)] = m
            m_hid[q] = free[("bcol", s)] = m2

        prepare(0)
        for q in range(ntiles):
            if q + 1 < ntiles:
                prepare(q + 1)
            beside(q)
            first(q)
            if q:
                second(q - 1)
        second(ntiles - 1)
        m_tiles = tile_out_dma.all()

        arena.used = base[0]
        picked = arena.take(4, 2, D)
        finish_space = arena.used
        L.need(m_tiles)
        m_picked = {}
        for i in range(NT + 2):
            if i < NT:
                s = i % 4
                for k in range(2):
                    at = k * NT + i
                    m_picked[i] = pick_dma.sent(L.need(free.get(("picked", s)), free[("hid", 0)], free[("hid", 1)]).indirect_dma_start(
                        out=picked[:, s, k, :], out_offset=None, in_=expert_out,
                        in_offset=bass.IndirectOffsetOnAxis(ap=pair_at[:, at:at + 1], axis=0)), s)
            if i >= 2:
                j = i - 2
                free[("picked", j % 4)] = finish(j, m_picked[j], picked[:, j % 4, :, :], pair_w, mask, mask_T, b2, m_ln,
                                                 finish_space, m_x)
        return free

    exp_v, exp_t2, exp_s = (e.raw.alloc_register(n) for e, n in ((V, "expert_first"), (T, "expert_second"), (S, "expert_bias")))
    token_rows = [dram(f"token_rows{n}", (N, D)) for n in range(2)]
    expert_rows = [dram(f"expert_rows{n}", (max_tiles[n] * P, D)) for n in range(2)]
    misc_row = [dram(f"expert_of_tile{n}", (P,), I32) for n in range(2)]

    def finish_shared(j, m, rows, pair_w, mask, mask_T, b2, m_ln, space, m_x):
        for k in range(2):
            m = V.done(V.need(m, m_x[j]).scalar_tensor_tensor(
                x[:, j, :], rows[:, k, :], pair_w[:, k, j:j + 1], x[:, j, :], ALU.mult, ALU.add))
        m_x[j] = m
        return m

    m_space0 = [list(h2.values()), list(m_x.values())]
    experts(0, m_x, E0, F0, t["L0_ffn_W1p"], t["L0_ffn_b1p"], t["L0_ffn_W2p"], t["L0_ffn_b2p"], t["L0_ffn_Wr"], None,
            (t["L0_ffn_W1s"], t["L0_ffn_b1s"], t["L0_ffn_W2s"], t["L0_ffn_b2s"]), [0], None, ACT.Gelu,
            m_space0, finish_shared)

    arena.used = 0
    w1_next = arena.take(E1, K, F1)
    next_base = 0
    space = list(m_x.values())
    sums = arena.take(NT, D + 2)
    g_ring = arena.take(16, D + 2)
    g_hot = arena.take(2 * G, P)
    s_dst_i = arena.take(NI, dtype=I32)
    s_dst_f = arena.take(NI)
    s_dst = arena.take(NI, dtype=U32)
    s_loc = arena.take(NI)
    wa = arena.take(2, K, D)
    wT = arena.take(2, K, D)
    b12 = arena.take(2, D)
    n_rows = arena.take(4, D)
    n_T = arena.take(2, K * P)
    means = arena.take(4, D)
    r_cnt = arena.take(NT)
    norm_table = dram("norm_table", (N, D))
    l1_dma = Landing(nc, "second_graph_landed")
    norm_dma = Landing(nc, "norm_rows_written", 4)
    g_dma = Landing(nc, "neighbours_gathered", 4)
    next_dma = Landing(nc, "next_weights_landed")
    Q.need(space)
    for n, name in ((0, "L1_gnn_W1"), (1, "L1_gnn_W2")):
        l1_dma.sent(Q.raw.dma_start(wa[:, n, :, :], t[name].rearrange("(o p) i -> p o i", p=P)))
    for n, name in ((0, "L1_gnn_b1"), (1, "L1_gnn_b2")):
        m_in = l1_dma.sent(Q.raw.dma_start(b12[:, n, :], t[name].partition_broadcast(P)))
    V.need(space)
    m_ln = ln_stats(m_x)
    m = V.done(V.need(m_in).tensor_tensor(b12[:, 0, :], b12[:, 0, :], b12[:, 1, :], ALU.add))
    m_b12 = m
    for n in range(2):
        for o in range(K):
            for i in range(K):
                mt = T.done(T.need(m_in, bank_free[4 + n]).transpose(
                    bank[4 + n][:, (i * K + o) * P:(i * K + o + 1) * P], wa[:, n, o, i * P:(i + 1) * P], ident))
        m_wT = V.done(V.need(mt).tensor_copy(wT[:, n, :, :].rearrange("p i o -> p (i o)"), bank[4 + n][:, 0:K * D]))
        bank_free[4 + n] = m_wT
    m = V.done(V.need(sort["sorted"]).tensor_scalar(s_loc, sorted_value, -1.0, None, ALU.add))
    m = V.done(V.need(m).tensor_copy(s_dst_i, s_loc))
    m = V.done(V.need(m).tensor_scalar(s_dst_i, s_dst_i, 7, None, ALU.arith_shift_right))
    m = V.done(V.need(m).tensor_copy(s_dst_f, s_dst_i))
    m = V.done(V.need(m).tensor_scalar(s_dst_f, s_dst_f, 0.0, None, ALU.max))
    m = V.done(V.need(m).scalar_tensor_tensor(s_loc, s_dst_f, -float(P), s_loc, ALU.mult, ALU.add))
    m_sd = V.done(V.raw.tensor_copy(s_dst, s_dst_f))
    m_own = V.done(V.raw.memset(sums, 0.0))
    m_one = V.done(V.raw.memset(g_ring[:, :, D:D + 2], 1.0))
    lfree, turned = {}, {}
    for j in range(NT):
        s = j % 4
        m = ln_rows(n_rows[:, s, :], j, m_ln, lfree.get(("n_rows", s)))
        n = P if j < NT - 1 else LAST
        lfree[("n_rows", s)] = norm_dma.sent(Q.need(m).dma_start(norm_table[j * P:j * P + n, :], n_rows[0:n, s, :]), s)

    def turn_rows(j, rows, m, name):
        b_ = j % 2
        for k in range(K):
            m = T.done(T.need(m, bank_free[b_]).transpose(bank[b_][:, k * P:(k + 1) * P], rows[:, k * P:(k + 1) * P], ident))
        lfree[name] = m
        turned[j] = bank_free[b_] = S.done(S.need(m, lfree.get(("n_T", b_))).activation(
            n_T[:, b_, :], bank[b_][:, 0:K * P], ACT.Copy))

    def add_product(j, which):
        b_ = j % 2
        for k in range(K):
            m = T.done(T.need(turned[j], m_wT, bank_free[2 + b_]).matmul(
                bank[2 + b_][:, 0:D], n_T[:, b_, k * P:(k + 1) * P], wT[:, which, k, :], start=(k == 0), stop=(k == K - 1)))
        lfree[("n_T", b_)] = m
        m_x[j] = bank_free[2 + b_] = V.done(V.need(m, m_x[j]).tensor_tensor(x[:, j, :], x[:, j, :], bank[2 + b_][:, 0:D], ALU.add))

    def own_product(step):
        j = step // 2
        if step % 2 == 0:
            m = ln_rows(n_rows[:, j % 4, :], j, m_ln, lfree.get(("n_rows", j % 4)))
            turn_rows(j, n_rows[:, j % 4, :], m, ("n_rows", j % 4))
        else:
            add_product(j, 0)
            m_x[j] = V.done(V.need(m_x[j], m_b12).tensor_tensor(x[:, j, :], x[:, j, :], b12[:, 0, :], ALU.add))

    for e in range(E1):
        m_w1n = next_dma.sent(Q.raw.dma_start(w1_next[:, e, :, :], t["L1_ffn_w1"][e].rearrange("(k p) f -> p k f", p=P)))
    L.need(norm_dma.all())
    sums_flat = sums.rearrange("p a b -> p (a b)")
    m_acc = m_own
    for g in range(NG):
        n = min(G, NI - g * G)
        s0, half = (g % 4) * G, (g % 2) * G
        for k in range(n):
            c = g * G + k
            m_g = g_dma.sent(L.need(m_sd, lfree.get(("ring", g % 4)), m_one).indirect_dma_start(
                out=g_ring[:, s0 + k, 0:D], out_offset=None, in_=norm_table,
                in_offset=bass.IndirectOffsetOnAxis(ap=s_dst[:, c:c + 1], axis=0)), g % 4)
        m_oh = V.done(V.need(lfree.get(("hot", g % 2))).tensor_tensor(
            g_hot[:, half:half + n, :], spread(iota, 1, n),
            spread(s_loc[:, g * G:g * G + n], 2, P), ALU.is_equal))
        if g < 2 * NT:
            own_product(g)
        for k in range(n):
            ob = 4 + (g * G + k) % 4
            m = T.done(T.need(m_g, m_oh, m_one, bank_free[ob]).matmul(
                bank[ob][:, 0:D + 2], g_hot[:, half + k, :], g_ring[:, s0 + k, :], start=True, stop=True))
            bank_free[ob] = m
        lfree[("hot", g % 2)] = lfree[("ring", g % 4)] = m
        V.need(sort["row"])
        V.raw.reg_load(tile_regs_v[0:n], sorted_tile_row[:, g * G:g * G + n])
        for k in range(n):
            ob = 4 + (g * G + k) % 4
            r = V.raw.snap(tile_regs_v[k], min_val=0, max_val=NT - 1)
            V.need(bank_free[ob])
            at = bass.ds(r * (D + 2), D + 2)
            m_acc = V.done(V.after(m_acc, V.raw.tensor_tensor(sums_flat[:, at], sums_flat[:, at],
                                                              bank[ob][:, 0:D + 2], ALU.add)))
            bank_free[ob] = m_acc
    m = V.done(V.need(m_acc).tensor_scalar(r_cnt, sums[:, :, D], 1.0, None, ALU.max))
    m_rc = V.done(V.need(m).reciprocal(r_cnt, r_cnt))
    m_mean = {}
    for i in range(NT + 2):
        if i < NT:
            m_mean[i] = V.done(V.need(m_rc, lfree.get(("means", i % 4))).tensor_scalar(
                means[:, i % 4, :], sums[:, i, 0:D], r_cnt[:, i:i + 1], None, ALU.mult))
        if 1 <= i <= NT:
            turn_rows(i - 1, means[:, (i - 1) % 4, :], m_mean[i - 1], ("means", (i - 1) % 4))
        if i >= 2:
            add_product(i - 2, 1)

    out_dma = Landing(nc, "out_written")
    efree = {}

    gamma_beta = sbuf("gamma_beta", [P, 2, D])
    for n, name in ((0, "L1_ffn_gamma"), (1, "L1_ffn_beta")):
        m_gb = l1_dma.sent(Q.raw.dma_start(gamma_beta[:, n, :], t[name].partition_broadcast(P)))
    y_dma = Landing(nc, "norm_rows_back", 4)

    def add_beta(q):
        if q < NT:
            m_x[q] = L.done(L.need(m_gb, m_x[q]).tensor_tensor(x[:, q, :], x[:, q, :], gamma_beta[:, 1, :], ALU.add))

    def load_norm(i, m):
        n = P if i < NT - 1 else LAST
        efree[("y_in", i)] = y_dma.sent(Q.need(m, efree.get(("y", i % 4))).dma_start(
            efree["y"][0:n, i % 4, :], token_rows[1][i * P:i * P + n, :]), i % 4)

    def bias_product(j, mask, mask_T, b2):
        b_ = j % 2
        mt = T.done(T.need(bank_free[b_]).transpose(bank[b_][0:E1, 0:P], mask[:, j, 0:E1], ident))
        mt = S.done(S.need(mt, efree.get(("mask_T", b_))).activation(mask_T[0:E1, b_, :], bank[b_][0:E1, 0:P], ACT.Copy))
        bank_free[b_] = mt
        mt = T.done(T.need(mt, bank_free[2 + b_]).matmul(bank[2 + b_][:, 0:D], mask_T[0:E1, b_, :], b2[0:E1, :],
                                                         start=True, stop=True))
        efree[("mask_T", b_)] = efree[("bias", j)] = mt

    def scale_last(j):
        y, st = efree["y"][:, j % 4, :], efree["st"][:, j % 4, :]
        my = V.done(V.need(efree[("root", j)]).reciprocal(st[:, 8:9], st[:, 8:9]))
        my = V.done(V.need(my).tensor_scalar(y, y, st[:, 6:7], st[:, 8:9], ALU.subtract, ALU.mult))
        efree[("scaled", j)] = L.done(L.need(my, m_gb).tensor_tensor(y, y, gamma_beta[:, 0, :], ALU.mult))

    def add_last(j):
        y = efree["y"][:, j % 4, :]
        efree[("y", j % 4)] = m_x[j] = V.done(V.need(efree[("scaled", j)], m_x[j]).tensor_tensor(
            x[:, j, :], x[:, j, :], y, ALU.add))
        n = P if j < NT - 1 else LAST
        out_dma.sent(Q.need(m_x[j]).dma_start(out[j * P:j * P + n, :], x[0:n, j, :]))

    def finish_last(j, m, rows, pair_w, mask, mask_T, b2, m_ln, space, m_x):
        if j == 0:
            arena.used = space
            efree["y"] = arena.take(4, D)
            efree["st"] = arena.take(4, 10)
            for i in range(3):
                load_norm(i, m)
        if j >= 2:
            add_last(j - 2)
        if j >= 1:
            scale_last(j - 1)
        if j and j + 2 < NT:
            load_norm(j + 2, m)
        y, st = efree["y"][:, j % 4, :], efree["st"][:, j % 4, :]
        if j == 0:
            bias_product(0, mask, mask_T, b2)
        if j + 1 < NT:
            bias_product(j + 1, mask, mask_T, b2)
        b_ = j % 2
        mt = efree[("bias", j)]
        my = V.done(V.need(efree[("y_in", j)], mt).tensor_tensor(y, y, bank[2 + b_][:, 0:D], ALU.add))
        bank_free[2 + b_] = my
        for k in range(2):
            my = V.done(V.need(my, m).scalar_tensor_tensor(y, rows[:, k, :], pair_w[:, k, j:j + 1], y, ALU.mult, ALU.add))
        m_free = my
        my = V.done(V.need(my).bn_stats(st[:, 0:6], y))
        my = V.done(V.need(my).bn_aggr(st[:, 6:8], st[:, 0:6]))
        my = V.done(V.need(my).tensor_scalar(st[:, 8:9], st[:, 7:8], EPS, None, ALU.add))
        efree[("root", j)] = S.done(S.need(my).activation(st[:, 8:9], st[:, 8:9], ACT.Sqrt))
        return m_free

    arena.used = 0
    w1_ready = (arena.take(E1, K, F1), m_w1n)
    experts(1, m_x, E1, F1, None, t["L1_ffn_b1"], t["L1_ffn_w2"], t["L1_ffn_b2"], t["L1_ffn_gate_w"],
            t["L1_ffn_gate_b"], None, [arena.used], w1_ready, ACT.Relu,
            list(m_x.values()), finish_last, add_beta)
    add_last(NT - 2)
    scale_last(NT - 1)
    add_last(NT - 1)
    Q.need(out_dma.all())
    return

    out_dma = Landing(nc, "out_written")
    for j in range(NT):
        n = P if j < NT - 1 else LAST
        out_dma.sent(Q.need(m_x[j]).dma_start(out[j * P:j * P + n, :], x[0:n, j, :]))
    Q.need(out_dma.all())


_INS = ['x', 'src', 'dst', 'L0_gnn_W1', 'L0_gnn_al1', 'L0_gnn_ar1', 'L0_gnn_b1', 'L0_gnn_W2', 'L0_gnn_al2',
        'L0_gnn_ar2', 'L0_gnn_b2', 'L0_ffn_Wr', 'L0_ffn_W1s', 'L0_ffn_b1s', 'L0_ffn_W2s', 'L0_ffn_b2s',
        'L0_ffn_W1p', 'L0_ffn_b1p', 'L0_ffn_W2p', 'L0_ffn_b2p', 'L1_gnn_W1', 'L1_gnn_b1', 'L1_gnn_W2',
        'L1_gnn_b2', 'L1_ffn_gate_w', 'L1_ffn_gate_b', 'L1_ffn_w1', 'L1_ffn_b1', 'L1_ffn_w2', 'L1_ffn_b2',
        'L1_ffn_gamma', 'L1_ffn_beta']


def kernel(**inputs):
    import numpy as _np
    import concourse.bacc as _bacc
    from concourse.bass_utils import run_bass_kernel_spmd as _run

    nc = _bacc.Bacc("TRN2", target_bir_lowering=False, num_devices=1)
    arrays, tensors = {}, {}
    for name in _INS:
        a = _np.ascontiguousarray(inputs[name])
        arrays[f"in_{name}"] = a
        tensors[name] = nc.dram_tensor(f"in_{name}", a.shape, mybir.dt.from_np(a.dtype), kind="ExternalInput").ap()
    out = nc.dram_tensor("out_0", tuple(inputs["x"].shape), F32, kind="ExternalOutput").ap()
    build(nc, tensors, out)
    r = _run(nc, [arrays], core_ids=[0])
    return r.results[0]["out_0"]
```
